# Optimizing a Trainium2 kernel written in Bass

```python
import numpy as np
import jax
import jax.numpy as jnp

def _softmax(x, axis=-1):
    return jax.nn.softmax(x, axis=axis)

def _gelu(x):
    return jax.nn.gelu(x, approximate=True)

def _silu(x):
    return jax.nn.silu(x)

def _sigmoid(x):
    return jax.nn.sigmoid(x)

def _layernorm(x, axis=-1, eps=1e-05):
    m = jnp.mean(x, axis=axis, keepdims=True)
    v = jnp.var(x, axis=axis, keepdims=True)
    return (x - m) / jnp.sqrt(v + eps)

def _scatter_add(tgt, idx, src, axis=0):
    return tgt.at[idx].add(src)

def _segment_sum(src, seg, n):
    return jax.ops.segment_sum(src, seg, n)
kernel_name = 'mk_xattn_ffn_d2_seqx_r4_1098a2'

def setup_inputs(seed: int=0):
    np.random.seed(seed)
    _w = jnp.asarray

    def _rec_inputs():
        import jax
        import jax.numpy as jnp
        _rk = jax.random.key(seed)
        x = -0.0002928 + 1 * jax.random.normal(jax.random.fold_in(_rk, 1), (2, 1024, 256), jnp.float32)
        _lenS = 1024 - jax.random.randint(jax.random.fold_in(_rk, 7), (2,), 0, max(1, 1024 // 4) + 1, jnp.int32)
        _lenS2 = 77 - jax.random.randint(jax.random.fold_in(_rk, 8), (2,), 0, max(1, 77 // 4) + 1, jnp.int32)
        _ctx_1024P = jax.random.normal(jax.random.fold_in(_rk, 11), (2, 16, 256), jnp.float32)
        _ctx_1024c = jax.random.dirichlet(jax.random.fold_in(_rk, 511), 0.3 * jnp.ones((16,), jnp.float32), (2, 77))
        _ctx_1024t = jnp.einsum('bsk,bkd->bsd', _ctx_1024c, _ctx_1024P)
        _ctx_1024t = _ctx_1024t * jax.lax.rsqrt(jnp.mean(jnp.square(_ctx_1024t)) + 1e-12) * 0.953939
        ctx_1024 = 4.13588e-05 + 0.999923 * (_ctx_1024t + 0.3 * jax.random.normal(jax.random.fold_in(_rk, 611), (2, 77, 256), jnp.float32))
        _validS = jnp.arange(1024)[None, :] < _lenS[:, None]
        _validS2 = jnp.arange(77)[None, :] < _lenS2[:, None]
        _causal = jnp.tril(jnp.ones((1024, 1024), dtype=bool))
        mask_Bx1x1xS2_ff0 = jnp.where(jnp.ones((2, 1, 1, 77), dtype=bool), 0.0, -1000000000.0).astype(jnp.float32)
        mask_1x1xSxS2_ik0 = jnp.where(jnp.broadcast_to(_validS2[0:1, None, None, :], (1, 1, 1024, 77)), 0, 1).astype(jnp.int32)
        return (x, ctx_1024, mask_Bx1x1xS2_ff0, mask_1x1xSxS2_ik0)
    x, ctx_1024, mask_Bx1x1xS2_ff0, mask_1x1xSxS2_ik0 = _rec_inputs()

    def _L0_xattn_setup():
        import jax, jax.numpy as jnp
        import numpy as np
        H = 16
        D = 256
        F = 1024
        LN_EPS = 1e-05

        def _glorot(key, shape):
            fan_in, fan_out = (shape[0], shape[1])
            lim = np.sqrt(6.0 / (fan_in + fan_out))
            return jax.random.uniform(key, shape, jnp.float32, -lim, lim)

        def _split_heads(x):
            b, l, _ = x.shape
            return x.reshape(b, l, H, D // H)

        def _mha(x, ctx, mask, qw, qb, kw, kb, vw, vb):
            q = _split_heads(x @ qw + qb)
            k = _split_heads(ctx @ kw + kb)
            v = _split_heads(ctx @ vw + vb)
            scores = jnp.einsum('bqhd,bkhd->bhqk', q, k) / np.sqrt(D // H).astype(np.float32)
            if mask is not None:
                scores = scores + mask
            probs = jax.nn.softmax(scores, axis=-1)
            out = jnp.einsum('bhqk,bkhd->bqhd', probs, v)
            return out.reshape(x.shape[0], x.shape[1], D)

        def _self_output(h, residual, w, b, g, be):
            h = h @ w + b
            h = h + residual
            mu = jnp.mean(h, axis=-1, keepdims=True)
            var = jnp.mean(jnp.square(h - mu), axis=-1, keepdims=True)
            return (h - mu) * jax.lax.rsqrt(var + LN_EPS) * g + be
        key = jax.random.key(seed)
        ks = jax.random.split(key, 16)
        inp = {'input_tensor': jax.random.normal(ks[0], (4, 256, D), jnp.float32), 'ctx_tensor': jax.random.normal(ks[1], (4, 512, D), jnp.float32), 'ctx_attn_mask': jnp.zeros((4, 1, 1, 512), jnp.float32), 'cq_w': _glorot(ks[2], (D, D)), 'cq_b': jnp.zeros((D,)), 'ck_w': _glorot(ks[3], (D, D)), 'ck_b': jnp.zeros((D,)), 'cv_w': _glorot(ks[4], (D, D)), 'cv_b': jnp.zeros((D,)), 'co_w': _glorot(ks[5], (D, D)), 'co_b': jnp.zeros((D,)), 'co_g': jnp.ones((D,)), 'co_be': jnp.zeros((D,)), 'sq_w': _glorot(ks[6], (D, D)), 'sq_b': jnp.zeros((D,)), 'sk_w': _glorot(ks[7], (D, D)), 'sk_b': jnp.zeros((D,)), 'sv_w': _glorot(ks[8], (D, D)), 'sv_b': jnp.zeros((D,)), 'so_w': _glorot(ks[9], (D, D)), 'so_b': jnp.zeros((D,)), 'so_g': jnp.ones((D,)), 'so_be': jnp.zeros((D,)), 'fi_w': _glorot(ks[10], (D, F)), 'fi_b': jnp.zeros((F,)), 'fo_w': _glorot(ks[11], (F, D)), 'fo_b': jnp.zeros((D,)), 'fo_g': jnp.ones((D,)), 'fo_be': jnp.zeros((D,))}
        return inp
    _L0_xattn_all = _L0_xattn_setup()
    _L0_xattn_in = {k: v for k, v in _L0_xattn_all.items() if k in ('cq_w', 'cq_b', 'ck_w', 'ck_b', 'cv_w', 'cv_b', 'co_w', 'co_b', 'co_g', 'co_be', 'sq_w', 'sq_b', 'sk_w', 'sk_b', 'sv_w', 'sv_b', 'so_w', 'so_b', 'so_g', 'so_be', 'fi_w', 'fi_b', 'fo_w', 'fo_b', 'fo_g', 'fo_be')}
    del _L0_xattn_all

    def _L0_ffn_setup():
        import jax, jax.numpy as jnp
        import numpy as np
        TOP_K = 2
        key = jax.random.key(seed)
        k1, k2, k3, k4 = jax.random.split(key, 4)
        B, S, D = (2, 512, 256)
        E, W = (8, 256)
        x = jax.random.normal(k1, (B, S, D), dtype=jnp.float32)
        router_w = jax.random.normal(k2, (E, D), dtype=jnp.float32) * 0.02
        w1 = jax.random.normal(k3, (D, E * W), dtype=jnp.float32) * 0.02
        w2 = jax.random.normal(k4, (E * W, D), dtype=jnp.float32) * 0.02
        return {'x': x, 'router_w': router_w, 'w1': w1, 'w2': w2}
    _L0_ffn_all = _L0_ffn_setup()
    _L0_ffn_in = {k: v for k, v in _L0_ffn_all.items() if k in ('router_w', 'w1', 'w2')}
    del _L0_ffn_all

    def _L1_xattn_setup():
        import jax, jax.numpy as jnp
        import numpy as np
        B, S, D, H, P = (4, 512, 256, 16, 10)
        DK = D // H
        key = jax.random.key(seed)
        ks = jax.random.split(key, 12)
        inp = {'q': jax.random.normal(ks[0], (B, S, D), jnp.float32), 'k': jax.random.normal(ks[1], (B, S, D), jnp.float32), 'v': jax.random.normal(ks[2], (B, S, D), jnp.float32), 'mask': jnp.tril(jnp.ones((S, S), jnp.int32))[None, None, :, :], 'Wq': jax.random.normal(ks[3], (D, D), jnp.float32) * (1.0 / np.sqrt(D)), 'bq': jnp.zeros((D,), jnp.float32), 'Wk': jax.random.normal(ks[4], (D, D), jnp.float32) * (1.0 / np.sqrt(D)), 'bk': jnp.zeros((D,), jnp.float32), 'Wv': jax.random.normal(ks[5], (D, D), jnp.float32) * (1.0 / np.sqrt(D)), 'bv': jnp.zeros((D,), jnp.float32), 'Wo': jax.random.normal(ks[6], (D, D), jnp.float32) * (1.0 / np.sqrt(D)), 'bo': jnp.zeros((D,), jnp.float32), 'prefix_k': jax.random.normal(ks[7], (H, P, DK), jnp.float32) * 0.02, 'prefix_v': jax.random.normal(ks[8], (H, P, DK), jnp.float32) * 0.02}
        return inp
    _L1_xattn_all = _L1_xattn_setup()
    _L1_xattn_in = {k: v for k, v in _L1_xattn_all.items() if k in ('Wq', 'bq', 'Wk', 'bk', 'Wv', 'bv', 'Wo', 'bo', 'prefix_k', 'prefix_v')}
    del _L1_xattn_all

    def _L1_ffn_setup():
        import jax, jax.numpy as jnp
        import numpy as np

        def _bitlinear(x, w_latent):
            scale = jax.lax.stop_gradient(jnp.clip(jnp.mean(jnp.abs(w_latent), axis=1, keepdims=True), 1e-05, None))
            tern = jnp.clip(jnp.round(w_latent / scale), -1.0, 1.0)
            w = w_latent + jax.lax.stop_gradient(tern - w_latent)
            return x @ (w * scale).T
        key = jax.random.key(seed)
        ks = jax.random.split(key, 6)
        dim, hidden, rank = (256, 1024, 16)
        B, S = (4, 1024)
        x = jax.random.normal(ks[0], (B, S, dim), dtype=jnp.float32)
        w_fc = 0.02 * jax.random.normal(ks[1], (hidden, dim), dtype=jnp.float32)
        w_proj = 0.02 * jax.random.normal(ks[2], (dim, hidden), dtype=jnp.float32)
        u = 0.02 * jax.random.normal(ks[3], (hidden, rank), dtype=jnp.float32)
        v = 0.02 * jax.random.normal(ks[4], (rank, dim), dtype=jnp.float32)
        fast_b = jax.random.normal(ks[5], (rank, rank), dtype=jnp.float32)
        gate = jnp.float32(0.05)
        return {'x': x, 'fast_b': fast_b, 'w_fc': w_fc, 'w_proj': w_proj, 'u': u, 'v': v, 'gate': gate}
    _L1_ffn_all = _L1_ffn_setup()
    _L1_ffn_in = {k: v for k, v in _L1_ffn_all.items() if k in ('fast_b', 'w_fc', 'w_proj', 'u', 'v', 'gate')}
    del _L1_ffn_all
    return {'x': x, 'ctx_1024': ctx_1024, 'mask_Bx1x1xS2_ff0': mask_Bx1x1xS2_ff0, 'mask_1x1xSxS2_ik0': mask_1x1xSxS2_ik0, 'L0_xattn_cq_w': _L0_xattn_in['cq_w'], 'L0_xattn_cq_b': _L0_xattn_in['cq_b'], 'L0_xattn_ck_w': _L0_xattn_in['ck_w'], 'L0_xattn_ck_b': _L0_xattn_in['ck_b'], 'L0_xattn_cv_w': _L0_xattn_in['cv_w'], 'L0_xattn_cv_b': _L0_xattn_in['cv_b'], 'L0_xattn_co_w': _L0_xattn_in['co_w'], 'L0_xattn_co_b': _L0_xattn_in['co_b'], 'L0_xattn_co_g': _L0_xattn_in['co_g'], 'L0_xattn_co_be': _L0_xattn_in['co_be'], 'L0_xattn_sq_w': _L0_xattn_in['sq_w'], 'L0_xattn_sq_b': _L0_xattn_in['sq_b'], 'L0_xattn_sk_w': _L0_xattn_in['sk_w'], 'L0_xattn_sk_b': _L0_xattn_in['sk_b'], 'L0_xattn_sv_w': _L0_xattn_in['sv_w'], 'L0_xattn_sv_b': _L0_xattn_in['sv_b'], 'L0_xattn_so_w': _L0_xattn_in['so_w'], 'L0_xattn_so_b': _L0_xattn_in['so_b'], 'L0_xattn_so_g': _L0_xattn_in['so_g'], 'L0_xattn_so_be': _L0_xattn_in['so_be'], 'L0_xattn_fi_w': _L0_xattn_in['fi_w'], 'L0_xattn_fi_b': _L0_xattn_in['fi_b'], 'L0_xattn_fo_w': _L0_xattn_in['fo_w'], 'L0_xattn_fo_b': _L0_xattn_in['fo_b'], 'L0_xattn_fo_g': _L0_xattn_in['fo_g'], 'L0_xattn_fo_be': _L0_xattn_in['fo_be'], 'L0_ffn_router_w': _L0_ffn_in['router_w'], 'L0_ffn_w1': _L0_ffn_in['w1'], 'L0_ffn_w2': _L0_ffn_in['w2'], 'L1_xattn_Wq': _L1_xattn_in['Wq'], 'L1_xattn_bq': _L1_xattn_in['bq'], 'L1_xattn_Wk': _L1_xattn_in['Wk'], 'L1_xattn_bk': _L1_xattn_in['bk'], 'L1_xattn_Wv': _L1_xattn_in['Wv'], 'L1_xattn_bv': _L1_xattn_in['bv'], 'L1_xattn_Wo': _L1_xattn_in['Wo'], 'L1_xattn_bo': _L1_xattn_in['bo'], 'L1_xattn_prefix_k': _L1_xattn_in['prefix_k'], 'L1_xattn_prefix_v': _L1_xattn_in['prefix_v'], 'L1_ffn_fast_b': _L1_ffn_in['fast_b'], 'L1_ffn_w_fc': _L1_ffn_in['w_fc'], 'L1_ffn_w_proj': _L1_ffn_in['w_proj'], 'L1_ffn_u': _L1_ffn_in['u'], 'L1_ffn_v': _L1_ffn_in['v'], 'L1_ffn_gate': _L1_ffn_in['gate']}

def reference(x, ctx_1024, mask_Bx1x1xS2_ff0, mask_1x1xSxS2_ik0, L0_xattn_cq_w, L0_xattn_cq_b, L0_xattn_ck_w, L0_xattn_ck_b, L0_xattn_cv_w, L0_xattn_cv_b, L0_xattn_co_w, L0_xattn_co_b, L0_xattn_co_g, L0_xattn_co_be, L0_xattn_sq_w, L0_xattn_sq_b, L0_xattn_sk_w, L0_xattn_sk_b, L0_xattn_sv_w, L0_xattn_sv_b, L0_xattn_so_w, L0_xattn_so_b, L0_xattn_so_g, L0_xattn_so_be, L0_xattn_fi_w, L0_xattn_fi_b, L0_xattn_fo_w, L0_xattn_fo_b, L0_xattn_fo_g, L0_xattn_fo_be, L0_ffn_router_w, L0_ffn_w1, L0_ffn_w2, L1_xattn_Wq, L1_xattn_bq, L1_xattn_Wk, L1_xattn_bk, L1_xattn_Wv, L1_xattn_bv, L1_xattn_Wo, L1_xattn_bo, L1_xattn_prefix_k, L1_xattn_prefix_v, L1_ffn_fast_b, L1_ffn_w_fc, L1_ffn_w_proj, L1_ffn_u, L1_ffn_v, L1_ffn_gate):
    import jax
    import jax.numpy as jnp

    def _L0_xattn_ref(input_tensor, ctx_tensor, ctx_attn_mask, cq_w, cq_b, ck_w, ck_b, cv_w, cv_b, co_w, co_b, co_g, co_be, sq_w, sq_b, sk_w, sk_b, sv_w, sv_b, so_w, so_b, so_g, so_be, fi_w, fi_b, fo_w, fo_b, fo_g, fo_be):
        import jax, jax.numpy as jnp
        import numpy as np
        H = 16
        D = 256
        F = 1024
        LN_EPS = 1e-05

        def _glorot(key, shape):
            fan_in, fan_out = (shape[0], shape[1])
            lim = np.sqrt(6.0 / (fan_in + fan_out))
            return jax.random.uniform(key, shape, jnp.float32, -lim, lim)

        def _split_heads(x):
            b, l, _ = x.shape
            return x.reshape(b, l, H, D // H)

        def _mha(x, ctx, mask, qw, qb, kw, kb, vw, vb):
            q = _split_heads(x @ qw + qb)
            k = _split_heads(ctx @ kw + kb)
            v = _split_heads(ctx @ vw + vb)
            scores = jnp.einsum('bqhd,bkhd->bhqk', q, k) / np.sqrt(D // H).astype(np.float32)
            if mask is not None:
                scores = scores + mask
            probs = jax.nn.softmax(scores, axis=-1)
            out = jnp.einsum('bhqk,bkhd->bqhd', probs, v)
            return out.reshape(x.shape[0], x.shape[1], D)

        def _self_output(h, residual, w, b, g, be):
            h = h @ w + b
            h = h + residual
            mu = jnp.mean(h, axis=-1, keepdims=True)
            var = jnp.mean(jnp.square(h - mu), axis=-1, keepdims=True)
            return (h - mu) * jax.lax.rsqrt(var + LN_EPS) * g + be
        ca = _mha(input_tensor, ctx_tensor, ctx_attn_mask, cq_w, cq_b, ck_w, ck_b, cv_w, cv_b)
        x = _self_output(ca, input_tensor, co_w, co_b, co_g, co_be)
        sa = _mha(x, x, None, sq_w, sq_b, sk_w, sk_b, sv_w, sv_b)
        x = _self_output(sa, x, so_w, so_b, so_g, so_be)
        inter = jax.nn.gelu(x @ fi_w + fi_b, approximate=False)
        x = _self_output(inter, x, fo_w, fo_b, fo_g, fo_be)
        return x

    def _L0_ffn_ref(x, router_w, w1, w2):
        import jax, jax.numpy as jnp
        import numpy as np
        TOP_K = 2
        B, S, D = x.shape
        E = router_w.shape[0]
        W = w1.shape[1] // E
        T = B * S
        xf = x.reshape(T, D)
        router_logits = jnp.einsum('td,ed->te', xf, router_w)
        router_probs = jax.nn.sigmoid(router_logits.astype(jnp.float32))
        top_w, sel = jax.lax.top_k(router_probs, TOP_K)
        top_w = top_w / (top_w.sum(axis=-1, keepdims=True) + 1e-20)
        top_w = top_w.astype(x.dtype)
        W1e = w1.reshape(D, E, W).transpose(1, 0, 2)
        W2e = w2.reshape(E, W, D)
        h = jnp.einsum('td,edw->etw', xf, W1e)
        a = jnp.square(jax.nn.relu(h))
        y = jnp.einsum('etw,ewd->etd', a, W2e)
        cw = jnp.zeros((T, E), dtype=x.dtype).at[jnp.arange(T)[:, None], sel].set(top_w)
        out = jnp.einsum('etd,te->td', y, cw)
        return out.reshape(B, S, D)

    def _L1_xattn_ref(q, k, v, mask, Wq, bq, Wk, bk, Wv, bv, Wo, bo, prefix_k, prefix_v):
        import jax, jax.numpy as jnp
        import numpy as np
        B, S, D, H, P = (4, 512, 256, 16, 10)
        DK = D // H
        bs, sq, d = q.shape
        h, p, dk = prefix_k.shape
        Q = (q @ Wq + bq).reshape(bs, sq, h, dk).transpose(0, 2, 1, 3)
        K = (k @ Wk + bk).reshape(bs, -1, h, dk).transpose(0, 2, 1, 3)
        V = (v @ Wv + bv).reshape(bs, -1, h, dk).transpose(0, 2, 1, 3)
        pK = jnp.broadcast_to(prefix_k[None], (bs, h, p, dk))
        pV = jnp.broadcast_to(prefix_v[None], (bs, h, p, dk))
        K = jnp.concatenate([pK, K], axis=2)
        V = jnp.concatenate([pV, V], axis=2)
        pref_mask = jnp.ones(mask.shape[:3] + (p,), mask.dtype)
        full_mask = jnp.concatenate([pref_mask, mask], axis=-1)
        scores = jnp.einsum('bhqd,bhkd->bhqk', Q, K) / np.sqrt(dk).astype(jnp.float32)
        scores = jnp.where(full_mask == 0, jnp.asarray(-1000000000.0, scores.dtype), scores)
        attn = jax.nn.softmax(scores, axis=-1)
        out = jnp.einsum('bhqk,bhkd->bhqd', attn, V)
        out = out.transpose(0, 2, 1, 3).reshape(bs, sq, d)
        return out @ Wo + bo

    def _L1_ffn_ref(x, fast_b, w_fc, w_proj, u, v, gate):
        import jax, jax.numpy as jnp
        import numpy as np

        def _bitlinear(x, w_latent):
            scale = jax.lax.stop_gradient(jnp.clip(jnp.mean(jnp.abs(w_latent), axis=1, keepdims=True), 1e-05, None))
            tern = jnp.clip(jnp.round(w_latent / scale), -1.0, 1.0)
            w = w_latent + jax.lax.stop_gradient(tern - w_latent)
            return x @ (w * scale).T
        h = _bitlinear(x, w_fc) + gate * (x @ v.T @ fast_b.T @ u.T)
        r = jnp.maximum(h, 0.0)
        return _bitlinear(r * r, w_proj)
    x = x + _L0_xattn_ref(_layernorm(x, axis=-1), ctx_1024, mask_Bx1x1xS2_ff0, L0_xattn_cq_w, L0_xattn_cq_b, L0_xattn_ck_w, L0_xattn_ck_b, L0_xattn_cv_w, L0_xattn_cv_b, L0_xattn_co_w, L0_xattn_co_b, L0_xattn_co_g, L0_xattn_co_be, L0_xattn_sq_w, L0_xattn_sq_b, L0_xattn_sk_w, L0_xattn_sk_b, L0_xattn_sv_w, L0_xattn_sv_b, L0_xattn_so_w, L0_xattn_so_b, L0_xattn_so_g, L0_xattn_so_be, L0_xattn_fi_w, L0_xattn_fi_b, L0_xattn_fo_w, L0_xattn_fo_b, L0_xattn_fo_g, L0_xattn_fo_be)
    x = x + _L0_ffn_ref(_layernorm(x, axis=-1), L0_ffn_router_w, L0_ffn_w1, L0_ffn_w2)
    x = x + _L1_xattn_ref(_layernorm(x, axis=-1), ctx_1024, ctx_1024, mask_1x1xSxS2_ik0, L1_xattn_Wq, L1_xattn_bq, L1_xattn_Wk, L1_xattn_bk, L1_xattn_Wv, L1_xattn_bv, L1_xattn_Wo, L1_xattn_bo, L1_xattn_prefix_k, L1_xattn_prefix_v)
    x = x + _L1_ffn_ref(_layernorm(x, axis=-1), L1_ffn_fast_b, L1_ffn_w_fc, L1_ffn_w_proj, L1_ffn_u, L1_ffn_v, L1_ffn_gate)
    return x

_drawn_inputs = setup_inputs


def setup_inputs(seed=0):
    import zlib

    import numpy as np

    out = dict(_drawn_inputs(seed))
    spreads = {'L0_xattn_cq_b': (0.0, 0.587),
     'L0_xattn_ck_b': (0.0, 2.0),
     'L0_xattn_cv_b': (0.0, 0.1),
     'L0_xattn_co_b': (0.0, 0.1),
     'L0_xattn_co_g': (1.0, 0.2),
     'L0_xattn_co_be': (0.0, 0.1),
     'L0_xattn_sq_b': (0.0, 0.8),
     'L0_xattn_sk_b': (0.0, 2.0),
     'L0_xattn_sv_b': (0.0, 0.1),
     'L0_xattn_so_b': (0.0, 0.1),
     'L0_xattn_so_g': (1.0, 0.2),
     'L0_xattn_so_be': (0.0, 0.1),
     'L0_xattn_fi_b': (0.0, 0.1),
     'L0_xattn_fo_b': (0.0, 0.1),
     'L0_xattn_fo_g': (1.0, 0.2),
     'L0_xattn_fo_be': (0.0, 0.1),
     'L1_xattn_bq': (0.0, 0.8),
     'L1_xattn_bk': (0.0, 0.8),
     'L1_xattn_bv': (0.0, 0.462),
     'L1_xattn_bo': (0.0, 0.1)}
    factors = {'L0_ffn_router_w': 4.257,
     'L0_ffn_w1': 4.053,
     'L0_ffn_w2': 3.673,
     'L1_xattn_prefix_k': 64.0,
     'L1_xattn_prefix_v': 29.932,
     'L1_ffn_fast_b': 8.0,
     'L1_ffn_u': 8.0,
     'L1_ffn_v': 8.0}
    for name, (base, spread) in spreads.items():
        noise = np.random.default_rng([zlib.crc32(name.encode()), seed]).standard_normal(out[name].shape)
        drawn = base * np.exp(spread * noise) if base else spread * noise
        out[name] = jnp.asarray(drawn.astype(out[name].dtype))
    for name, factor in factors.items():
        out[name] = (out[name] * factor).astype(out[name].dtype)
    return out
```

```python
from contextlib import ExitStack

import numpy as np
import concourse.bass as bass
from concourse import mybir

F32 = mybir.dt.float32
BF16 = mybir.dt.bfloat16
I32 = mybir.dt.int32
ALU = mybir.AluOpType
ACT = mybir.ActivationFunctionType
AX = mybir.AxisListType.X

B, S, D, H = 2, 1024, 256, 16
DH = D // H
KD = D // 128
SC = 77
NP = 10
SC1 = SC + NP
F = 1024
MF = F // 128
E, W = 8, 256
R = 16
T = B * S // 128
BT = 4
HALVES = S // (BT * 128)
N = BT * 128
QT_PER_HEAD = S // 128
KP = 96
NH = B * H
VW = DH + 1
EPS = 1e-5
DC = 16
CHUNK_HEADS = 4
NCH = H // CHUNK_HEADS
QROWS = 6 * DH
UNROLL = 4
LAG = 6


class Signal:

    def __init__(self, sem, credit=0, setup=0, a=0, b0=0, b=0, blast=0, c=0):
        self.sem = sem
        self.per = {"setup": setup, "a": a, "b0": b0, "b": b, "blast": blast, "c": c}
        trips = {"setup": 1, "a": B * HALVES, "b0": 1, "b": NH // UNROLL - 1, "blast": 1, "c": B * HALVES}
        self.credit = credit
        self.base, total = {}, credit
        for part, n in self.per.items():
            self.base[part] = total
            total += n * trips[part]
        self.total = total


class Tally:

    def __init__(self, part, i=0):
        self.part, self.i, self.n = part, i, {}

    def value(self, s):
        return self.i * s.per[self.part] + (s.base[self.part] + self.n.get(s, 0))

    def next(self, s, m=1):
        self.n[s] = self.n.get(s, 0) + m
        return self.value(s)

    def back(self, s, lag):
        return self.i * s.per[self.part] + max(s.base[self.part] + self.n.get(s, 0) - lag, s.credit)

    def slot(self, s, ring):
        before = s.base[self.part] - s.credit
        assert before % ring == 0 and (isinstance(self.i, int) or s.per[self.part] % ring == 0)
        return self.n.get(s, 0) % ring

    def close(self, *signals):
        for s in signals:
            assert self.n.get(s, 0) == s.per[self.part], (self.part, s.sem, self.n.get(s, 0), s.per[self.part])


def build(nc, A, out):
    ctx = ExitStack()
    with ctx:
        def sb(name, shape, dt=F32):
            return ctx.enter_context(nc.sbuf_tensor(name, shape, dt))

        def ps(name, shape, dt=F32):
            return ctx.enter_context(nc.psum_tensor(name, shape, dt))

        def sem(name):
            return ctx.enter_context(nc.semaphore(name))

        X = sb("X", [128, T, D])
        OA = sb("OA", [128, NH, QT_PER_HEAD, DH])
        wfc_raw = OA[:, 0:16].rearrange("p n q d -> p (n q d)").rearrange("p (m d) -> p m d", m=MF)
        wproj_raw = OA[:, 16:32].rearrange("p n q d -> p (n q d)").rearrange("p (m d) -> p m d", m=KD)

        shared = sb("shared", [128, 3 * 4096])
        VX = shared[:, 0:NH * 8 * VW].rearrange("p (n k d) -> p n k d", n=NH, k=8)
        o = NH * 8 * VW
        PC = shared[:, o:o + 3072].bitcast(BF16).rearrange("p (e c n) -> p e c n", e=4, c=3)
        PTB = shared[:, o:o + 2048].rearrange("p (r n) -> p r n", r=2)
        o += 3072
        KB0 = shared[:, o:o + B * H * SC].rearrange("p (b n) -> p b n", b=B)
        QX = [shared[:, o + 512 * j:o + 512 * (j + 1)].bitcast(BF16) for j in range(UNROLL)]
        KX = [shared[:, o + 2048 + 512 * j:o + 2048 + 512 * (j + 1)].bitcast(BF16) for j in range(UNROLL)]
        assert o + 4096 <= 3 * 4096
        w1 = shared[:, 0:4096].rearrange("p (k n) -> p k n", k=KD)
        w2 = shared[:, 4096:8192].rearrange("p (m n) -> p m n", m=2 * E)
        hid = shared[:, 8192:12288].rearrange("p (m n) -> p m n", m=MF)
        fifo = sb("fifo", [128, 2 * 2048])
        cq, co, sq, sk, sv = (fifo[:, 512 * j:512 * (j + 1)].rearrange("p (k n) -> p k n", k=KD) for j in range(5))
        fi = fifo[:, 0:2048].rearrange("p (k n) -> p k n", k=KD)
        fo = fifo[:, 2048:4096].rearrange("p (m n) -> p m n", m=MF)

        fcT = sb("fcT", [128, KD, F])
        projT = sb("projT", [128, MF, D])
        so, wq, wo = (sb(n, [128, KD, D]) for n in ("so", "wq", "wo"))
        routerT = sb("routerT", [128, KD, E])
        KB1 = sb("KB1", [128, B, H * SC1])
        VS0 = sb("VS0", [128, B, H, VW])
        VS1 = sb("VS1", [128, B, H, VW])
        VSW = sb("VSW", [128, H, 32])
        mask0 = sb("mask0", [128, B, SC], BF16)
        mask1 = sb("mask1", [128, QT_PER_HEAD, SC1], BF16)
        rows = {n: sb(n, [128, D]) for n in ("co_b", "co_g", "co_be", "sv_b", "so_b", "so_g", "so_be",
                                             "fo_b", "fo_g", "fo_be", "bo")}
        cols = {n: sb(n, [128, m]) for n, m in (("cq_b", KD), ("sq_b", KD), ("sk_b", KD), ("bq", KD),
                                                ("ck_b", KD), ("bk", KD), ("fi_b", MF))}
        identf = sb("identf", [128, 128])
        identb = sb("identb", [128, 128], BF16)
        onesb = sb("onesb", [128, 128], BF16)
        blockmask = sb("blockmask", [128, 128 // DH])

        XN = sb("XN", [128, BT, D])
        RB = sb("RB", [128, BT, D])
        TOK = sb("TOK", [128, 2, D])
        HB = sb("HB", [128, 2, D])
        xTa = sb("xTa", [128, KD, N])
        xTb = sb("xTb", [128, KD, N])
        QT = sb("QT", [128, KD, N])
        P = sb("P", [128, 2, H, KP])
        ck, cv, wk, wv = (P[:, j // 2].rearrange("p h k -> p (h k)")[:, 512 * (j % 2):512 * (j % 2) + 512]
                          .rearrange("p (k n) -> p k n", k=KD) for j in range(4))
        PTS = sb("PTS", [128, H, 128])
        OSB = sb("OSB", [128, 512])
        CA = sb("CA", [128, D])
        CAT = sb("CAT", [128, KD, 128])
        RR = PTS[:, 0:8, :].rearrange("p h n -> p (h n)").rearrange("p (r n) -> p r n", r=2)
        VH = sb("VH", [128, 2, QT_PER_HEAD, 32])
        small = sb("small", [128, 512])
        mv = small[:, 0:8].rearrange("p (r s) -> p r s", r=4)
        rstd = small[:, 8:12]
        ve = small[:, 12:16]
        minus_half = small[:, 16:17]
        stats = small[:, 20:26]
        rsum = small[:, 32:48]
        mx = small[:, 48:64]
        lg = small[:, 64:96]
        pr = small[:, 96:128].rearrange("p (t e) -> p t e", e=E)
        pw = small[:, 128:160].rearrange("p (t e) -> p t e", e=E)
        eq = small[:, 160:192].rearrange("p (t e) -> p t e", e=E)
        hot = small[:, 192:224].rearrange("p (t e) -> p t e", e=E)
        cw = small[:, 224:256].rearrange("p (t e) -> p t e", e=E)
        rank = small[:, 256:264]
        top = small[:, 264:288].rearrange("p (j t) -> p j t", t=BT)
        nm2 = small[:, 288:304]
        nm = small[:, 304:320].rearrange("p (r q) -> p r q", r=2)
        nres = small[:, 320:328]
        wscale = small[:, 328:352].rearrange("p (j m) -> p j m", j=3)
        gate = small[0:R, 352:353]
        ms = small[:, 360:384].bitcast(BF16).rearrange("p (r n) -> p r n", r=2)
        MT = sb("MT", [24, 128], BF16)
        ctxs = XN[0:SC, 0:B, :]
        ctxT = xTa[:, :, 0:B * SC]
        kT = xTb[:, :, 0:B * SC]
        kT1 = xTb[:, :, B * SC:2 * B * SC]
        pkT = QT[:, :, 0:NP]
        masks = QT[0:3, 0, 256:256 + 2 * SC]
        mtmp = QT[0:3, 1, 256:256 + 2 * SC]
        mpiece = OSB[0:3, 0:B * SC].bitcast(BF16)[:, 0:2 * SC]
        maski = X[:, 0:4, :].rearrange("p a n -> p (a n)")[:, 0:QT_PER_HEAD * SC].bitcast(I32)\
            .rearrange("p (q k) -> p q k", k=SC)
        vb0, vb1 = TOK[:, 0, :], TOK[:, 1, :]
        u_sb = HB[:, 0, 0:MF * R].rearrange("p (m r) -> p m r", r=R)
        fbT = HB[0:R, 1, 0:R]
        v_sb = CA[0:R, :]
        G_sb = CAT[0:R, :, :].rearrange("p k n -> p (k n)")
        uT = RB[0:R, :, :].rearrange("p t n -> p (t n)")
        tA = PTS[:, 0:2, :].rearrange("p h n -> p (h n)")
        wt = PTS[:, 2:10, :].rearrange("p h n -> p (h n)")

        SCR = ps("SCR", [128, 4, 512])
        TR = ps("TR", [128, 2, 512])
        OUT = ps("OUT", [128, 2, 512])
        SQ = [TR[:, 0, :], TR[:, 1, :], OUT[:, 0, :]]
        PV = OUT[:, 1, :]

        scratch = nc.dram_tensor("pieces", [2, 3, NH * DH, S], BF16)
        x1_dram = nc.dram_tensor("x1", [128, T, D], F32)
        mscratch = nc.dram_tensor("maxima", [2, 24, 128], BF16)

        d_ctx, d_kv, d_low, d_tern, d_const, d_x, d_aw, d_cw, d_mask, d_prefix, d_fifo, d_moe, d_m1, d_m2, \
            d_pieces, d_out = (sem(n) for n in (
                "ctx_loaded", "small_kv_weights_loaded", "low_rank_loaded", "ternary_sources_loaded",
                "biases_loaded", "x_loaded", "part_a_weights_loaded", "part_c_weights_loaded", "masks_loaded",
                "prefix_loaded", "gelu_weights_loaded", "expert_weights_loaded",
                "maxima_to_dram", "maxima_to_rows", "pieces_stored", "out_stored"))
        tr_full = Signal(sem("tr_full"), setup=1 + 4 + 2 + 1 + MF + 4, a=4 + 2 + (4 + 3) * BT + 4, c=4 + 4 + MF + 4 + 2 * E + 4 + 2 + 7 * BT + MF)
        tr_done = Signal(sem("tr_done"), **{k: v for k, v in tr_full.per.items()})
        out_full = Signal(sem("out_full"), setup=4 + MF, a=2 * BT + BT, c=BT + BT + 2 + E * BT + 2 * BT + BT)
        out_done = Signal(sem("out_done"), **out_full.per)
        sc_full = Signal(sem("scores_full"), 1, a=BT, c=BT)
        sc_done = Signal(sem("scores_done"), 1, **sc_full.per)
        p_ready = Signal(sem("probs_ready"), **sc_full.per)
        ln_stats = Signal(sem("ln_stats"), a=2 * BT, c=5 * BT)
        ln_rstd = Signal(sem("ln_rstd"), **ln_stats.per)
        tok_ready = Signal(sem("token_tile_ready"), **ln_stats.per)
        resid_ready = Signal(sem("residual_ready"), a=BT, c=2 * BT)
        d_x1 = [sem(f"x1_stored_{r}") for r in range(2)]
        d_x1_back = sem("x1_loaded")
        stage_ready = Signal(sem("stage_ready"), c=BT)
        vsw_ready = Signal(sem("small_values_ready"), a=1, c=1)
        pc_ready = Signal(sem("pieces_ready"), a=4)
        gate_exp = Signal(sem("gate_exp"), c=1)
        a_ready = Signal(sem("activated_ready"), c=2 * E + MF)
        sq_per = 2 * QT_PER_HEAD + 2
        sq_full = Signal(sem("max_scores_full"), b0=2 * 2 * QT_PER_HEAD + 1,
                         b=UNROLL * sq_per, blast=UNROLL * sq_per - 2 * 2 * QT_PER_HEAD - 1)
        sq_done = Signal(sem("max_scores_done"), **sq_full.per)
        st_full = Signal(sem("t_scores_full"), 1, b=UNROLL * 16, blast=UNROLL * 16)
        st_done = Signal(sem("t_probs_ready"), 1, **st_full.per)
        pv_full = Signal(sem("head_out_full"), 1, b=UNROLL, blast=UNROLL)
        pv_done = Signal(sem("head_out_done"), 1, **pv_full.per)
        vh_ready = Signal(sem("head_values_ready"), b0=2, b=UNROLL, blast=UNROLL - 2)
        max_ready = Signal(sem("maxima_ready"), b0=2, b=UNROLL, blast=UNROLL - 2)
        m_split = Signal(sem("maxima_split"), **max_ready.per)
        c_ready = Signal(sem("constants_ready"), setup=6)
        carrier = sem("wait_carrier")
        s_dve, s_pool = sem("vector_step"), sem("gpsimd_step")
        wproj_scaled = Signal(sem("wproj_scaled"), setup=KD)
        mask1_ready = Signal(sem("mask1_ready"), setup=1)
        setup_done = Signal(sem("setup_done"), setup=1)
        d_head = [sem(f"head_loaded_{j}") for j in range(UNROLL)]

        def r4(ap):
            return ap.rearrange("(k p) n -> p k n", p=128)

        def col(ap):
            return ap.rearrange("(k p) -> p k", p=128)

        def row(ap, parts=128):
            return ap.rearrange("(o n) -> o n", o=1).to_broadcast([parts, ap.shape[0]])

        def skewed(stages):
            for step in range(BT + LAG):
                for lag, stage in stages:
                    if 0 <= step - lag < BT:
                        stage(step - lag)

        def carry_wait(eng):
            eng.sem_inc(carrier, 1)

        def lagged(first, then):
            for t in range(BT + 1):
                if t < BT:
                    first(t)
                if t > 0:
                    then(t - 1)

        def sq_events(j, kt, last):
            n = 0
            for jj in range(UNROLL):
                for s in range(QT_PER_HEAD):
                    if (jj, s) == (j, kt):
                        return n
                    n += 0 if last and jj >= 2 else 2
                    n += 1 if s == 1 and jj >= 1 else 0
                    n += 1 if s == 2 and not (last and jj == UNROLL - 1) else 0
            return n

        def maxima_event(tl, j, last):
            tl2 = Tally(tl.part, tl.i)
            return tl2.next(sq_done, sq_events(j, 3, last))

        block = ctx.enter_context(nc.Block())

        @block.sync
        def _(sp):
            with nc.allow_non_contiguous_dma(reason="biases and small transposed loads"):
                sp.dma_start(ctxs, A["ctx_1024"].rearrange("b s d -> s b d")).then_inc(d_ctx, 16)
                for dst, n in ((ck, "L0_xattn_ck_w"), (cv, "L0_xattn_cv_w"), (wk, "L1_xattn_Wk"), (wv, "L1_xattn_Wv")):
                    sp.dma_start(dst, r4(A[n])).then_inc(d_kv, 16)
                for dst, n in ((cols["ck_b"], "L0_xattn_ck_b"), (cols["bk"], "L1_xattn_bk")):
                    sp.dma_start(dst[:, :], col(A[n])).then_inc(d_kv, 16)
                for dst, n in ((vb0, "L0_xattn_cv_b"), (vb1, "L1_xattn_bv")):
                    sp.dma_start(dst, row(A[n])).then_inc(d_kv, 16)
                for h in range(H):
                    sp.dma_start(pkT[h % 8 * DH:(h % 8 + 1) * DH, h // 8, :],
                                 A["L1_xattn_prefix_k"][h].rearrange("p d -> d p")).then_inc(d_prefix, 16)
                sp.dma_start(u_sb, A["L1_ffn_u"].rearrange("(m p) r -> p m r", p=128)).then_inc(d_low, 16)
                sp.dma_start(fbT, A["L1_ffn_fast_b"].rearrange("a b -> b a")).then_inc(d_low, 16)
                sp.dma_start(v_sb, A["L1_ffn_v"]).then_inc(d_low, 16)
                sp.dma_start(gate, row(A["L1_ffn_gate"], R)).then_inc(d_low, 16)
                sp.dma_start(wfc_raw, A["L1_ffn_w_fc"].rearrange("(m p) d -> p m d", p=128)).then_inc(d_tern, 16)
                sp.dma_start(wproj_raw, A["L1_ffn_w_proj"].rearrange("(m p) d -> p m d", p=128)).then_inc(d_tern, 16)
                m0 = A["mask_Bx1x1xS2_ff0"].rearrange("b x y k -> (x y) (b k)")
                sp.dma_start(masks, m0.to_broadcast([3, B * SC])).then_inc(d_mask, 16)
                sp.dma_start(maski, A["mask_1x1xSxS2_ik0"].rearrange("x y (q p) k -> p (x y q) k", p=128))\
                    .then_inc(d_mask, 16)
                for dst, n in ((cq, "cq_w"), (co, "co_w"), (sq, "sq_w"), (sk, "sk_w"), (sv, "sv_w")):
                    sp.dma_start(dst, r4(A["L0_xattn_" + n])).then_inc(d_aw, 16)
                for n, dst in rows.items():
                    sp.dma_start(dst[:, :], row(A["L1_xattn_bo" if n == "bo" else "L0_xattn_" + n])).then_inc(d_const, 16)
                for n in ("cq_b", "sq_b", "sk_b", "bq", "fi_b"):
                    sp.dma_start(cols[n][:, :], col(A["L1_xattn_bq" if n == "bq" else "L0_xattn_" + n])).then_inc(d_const, 16)
                sp.wait_ge(mask1_ready.sem, 1)
                sp.dma_start(X[:, :, :], A["x"].rearrange("b (t p) d -> p (b t) d", p=128)).then_inc(d_x, 16)
                for dst, n in ((so, "L0_xattn_so_w"), (wq, "L1_xattn_Wq"), (wo, "L1_xattn_Wo")):
                    sp.dma_start(dst[:, :, :], r4(A[n])).then_inc(d_cw, 16)
                for k in range(KD):
                    sp.dma_start(routerT[:, k, :], A["L0_ffn_router_w"][:, k * 128:(k + 1) * 128]
                                 .rearrange("e p -> p e")).then_inc(d_cw, 16)
                sp.wait_ge(c_ready.sem, c_ready.total)
                for b in range(B):
                    sp.dma_start(VS1[SC:SC1, b, :, 0:DH], A["L1_xattn_prefix_v"].rearrange("h p d -> p h d"))\
                        .then_inc(d_prefix, 16)

                with sp.Fori(0, B) as b:
                    with sp.Fori(0, HALVES) as half:
                        i = b * HALVES + half
                        tl = Tally("a", i)
                        tl.next(tok_ready, BT)
                        for t in range(BT):
                            sp.wait_ge(tok_ready.sem, tl.next(tok_ready))
                            sp.dma_start(x1_dram[:, i * BT + t, :], TOK[:, t % 2, :]).then_inc(d_x1[t % 2], 16)
                        for e in range(4):
                            sp.wait_ge(pc_ready.sem, tl.next(pc_ready))
                            dst = scratch[e // 2, :, :, :].rearrange("c r s -> r c s")[
                                bass.ds(b * D + (e % 2) * 128, 128), :, bass.ds(half * N, N)]
                            sp.dma_start(dst, PC[:, e]).then_inc(d_pieces, 16)
                sp.wait_ge(d_pieces, DC + 16 * 4 * B * HALVES)
                for r in range(2):
                    sp.wait_ge(d_x1[r], DC + 16 * T // 2)
                sp.wait_ge(out_done.sem, out_done.base["b0"])
                sp.dma_start(fi, r4(A["L0_xattn_fi_w"])).then_inc(d_fifo, 16)
                sp.dma_start(fo, A["L0_xattn_fo_w"].rearrange("(m p) n -> p m n", p=128)).then_inc(d_fifo, 16)

                def load_head(n, j):
                    src = scratch[:, :, bass.ds(n * DH, DH), :]
                    for c, r, m in ((0, 0, 3), (1, 3, 2), (2, 5, 1)):
                        for k in range(m):
                            sp.dma_start(QX[j][(r + k) * DH:(r + k + 1) * DH, :], src[0, c]).then_inc(d_head[j], 16)
                            sp.dma_start(KX[j][(r + k) * DH:(r + k + 1) * DH, :], src[1, k]).then_inc(d_head[j], 16)

                def store_maxima(tl, events, j):
                    sp.wait_ge(sq_done.sem, events)
                    sp.dma_start(mscratch[j % 2], MT[:, :]).then_inc(d_m1, 16)
                    return mscratch[j % 2].rearrange("(c q) t -> c (q t)", c=3)

                for j in range(3):
                    load_head(j, j)
                src = store_maxima(None, sq_done.base["b0"] + 4 * QT_PER_HEAD + 1, 0)
                sp.wait_ge(d_m1, 16)
                sp.dma_start(QX[0][QROWS:QROWS + 3, :], src).then_inc(d_m2, 16)

                def head(tl, i, j, last):
                    n = i * UNROLL + j
                    if not (last and j >= 1):
                        sp.wait_ge(pv_full.sem, tl.value(pv_full))
                        load_head(n + 3, (j + 3) % UNROLL)
                    tl.next(pv_full)
                    if not (last and j == UNROLL - 1):
                        src = store_maxima(tl, maxima_event(tl, j, last), (j + 1) % UNROLL)
                        sp.wait_ge(d_m1, 16 + 16 * (n + 1))
                        sp.dma_start(QX[(j + 1) % UNROLL][QROWS:QROWS + 3, :], src).then_inc(d_m2, 16)

                with sp.Fori(0, NH // UNROLL - 1) as i:
                    tl = Tally("b", i)
                    for j in range(UNROLL):
                        head(tl, i, j, False)
                tl = Tally("blast")
                for j in range(UNROLL):
                    head(tl, NH // UNROLL - 1, j, True)

                sp.wait_ge(pv_full.sem, pv_full.total)
                for k in range(KD):
                    sp.dma_start(w1[:, k, :], A["L0_ffn_w1"][k * 128:(k + 1) * 128, :]).then_inc(d_moe, 16)
                for m in range(2):
                    sp.dma_start(w2[:, m * E:(m + 1) * E, :],
                                 A["L0_ffn_w2"][m * 1024:(m + 1) * 1024, :].rearrange("(m p) n -> p m n", p=128))\
                        .then_inc(d_moe, 16)
                with sp.Fori(0, B) as b:
                    with sp.Fori(0, HALVES) as half:
                        i = b * HALVES + half
                        tl = Tally("c", i)
                        sp.wait_ge(tok_ready.sem, tl.value(tok_ready))
                        sp.dma_start(RB[:, :, :], x1_dram[:, bass.ds(i * BT, BT), :]).then_inc(d_x1_back, 16)
                        tl.next(out_done, out_done.per["c"] - BT)
                        for t in range(BT):
                            sp.wait_ge(out_done.sem, tl.next(out_done))
                            sp.dma_start(out[b, bass.ds(half * N + t * 128, 128), :], XN[:, t, :]).then_inc(d_out, 16)
                sp.wait_ge(d_out, DC + 16 * T)

        @block.tensor
        def _(pe):
            def tr_bank(tl):
                bank = tl.slot(tr_full, 2)
                tl.next(tr_full)
                v = tl.back(tr_full, 2)
                pe.wait_ge(tr_done.sem, v)
                return TR[:, bank, :]

            def out_bank(tl):
                bank = tl.slot(out_full, 2)
                tl.next(out_full)
                v = tl.back(out_full, 2)
                pe.wait_ge(out_done.sem, v)
                return OUT[:, bank, :]

            def evacuated(tl):
                pe.wait_ge(tr_done.sem, tl.value(tr_full))

            def product(dst, pairs):
                for n, (l, r) in enumerate(pairs):
                    ins = nc.tensor.matmul(dst, l, r, start=(n == 0), stop=(n == len(pairs) - 1))
                return ins

            def transposes(dst, srcs, ident=identf, width=128):
                for n, s in enumerate(srcs):
                    m, p = s.shape[1], s.shape[0]
                    ins = nc.tensor.transpose(dst[0:m, n * width:n * width + p], s, ident[0:p, 0:p])
                return ins

            tl = Tally("setup")
            pe.wait_ge(c_ready.sem, c_ready.total)
            pe.wait_ge(d_ctx, 16)
            bank = tr_bank(tl)
            transposes(bank, [ctxs[:, b, k * 128:(k + 1) * 128] for b in range(B) for k in range(KD)], width=SC)\
                .then_inc(tr_full.sem, 1)
            evacuated(tl)
            pe.wait_ge(d_kv, 16 * 8)
            for w in (ck, wk):
                for m in range(KD):
                    bank = tr_bank(tl)
                    product(bank[:, 0:B * SC], [(w[:, k, m * 128:(m + 1) * 128], ctxT[:, k, :]) for k in range(KD)])\
                        .then_inc(tr_full.sem, 1)
            for w in (cv, wv):
                for b in range(B):
                    bank = out_bank(tl)
                    product(bank[0:SC, 0:D], [(ctxT[:, k, b * SC:(b + 1) * SC], w[:, k, :]) for k in range(KD)])\
                        .then_inc(out_full.sem, 1)
            pe.wait_ge(d_low, 16 * 4)
            for hf in range(2):
                bank = tr_bank(tl)
                transposes(bank, [u_sb[:, 4 * hf + m, :] for m in range(4)]).then_inc(tr_full.sem, 1)
            bank = tr_bank(tl)
            product(bank[0:R, 0:D], [(fbT, v_sb)]).then_inc(tr_full.sem, 1)
            evacuated(tl)
            for m in range(MF):
                bank = out_bank(tl)
                product(bank[:, 0:D], [(uT[:, m * 128:(m + 1) * 128], G_sb)]).then_inc(out_full.sem, 1)
                pe.wait_ge(out_done.sem, tl.value(out_full))
                bank = tr_bank(tl)
                transposes(bank, [tA[:, k * 128:(k + 1) * 128] for k in range(KD)]).then_inc(tr_full.sem, 1)
            for m in range(KD):
                pe.wait_ge(wproj_scaled.sem, m + 1)
                for hf in range(2):
                    bank = tr_bank(tl)
                    transposes(bank, [wt[:, (4 * hf + c) * 128:(4 * hf + c + 1) * 128] for c in range(4)])\
                        .then_inc(tr_full.sem, 1)
            tl.close(tr_full, out_full)

            def token_transposes(tl, srcs_of, t):
                pe.wait_ge(tok_ready.sem, tl.next(tok_ready))
                bank = tr_bank(tl)
                src = srcs_of(t)
                transposes(bank, [src[:, k * 128:(k + 1) * 128] for k in range(KD)]).then_inc(tr_full.sem, 1)

            def feature_major(tl, w, src, m):
                bank = tr_bank(tl)
                product(bank, [(w[:, k, m * 128:(m + 1) * 128], src[:, k, :]) for k in range(KD)])\
                    .then_inc(tr_full.sem, 1)

            def small_attention(tl, b, half, keys, nk, project):
                def scores(t):
                    tl.next(sc_full)
                    pe.wait_ge(sc_done.sem, tl.back(sc_full, 1))
                    w = CHUNK_HEADS * nk
                    for c in range(NCH):
                        k = c * CHUNK_HEADS // 8
                        nc.tensor.matmul(SCR[:, c, 0:w], QT[:, k, t * 128:(t + 1) * 128],
                                         keys[:, b, c * w:(c + 1) * w], start=True, stop=False)
                        if nk == SC:
                            l, m = onesb[:, :], mask0[:, b, :]
                        else:
                            l, m = identb[:, :], mask1[:, half * BT + t, :]
                        ins = nc.tensor.matmul(SCR[:, c, 0:w].rearrange("p (h k) -> p h k", k=nk), l,
                                               m.unsqueeze(1).to_broadcast([128, CHUNK_HEADS, nk]),
                                               start=False, stop=True)
                    ins.then_inc(sc_full.sem, 1)

                def prob_transposes(t):
                    pe.wait_ge(p_ready.sem, tl.next(p_ready))
                    for g in range(4):
                        bank = tr_bank(tl)
                        transposes(bank, [P[:, t % 2, 4 * g + hh, :] for hh in range(4)]).then_inc(tr_full.sem, 1)

                def values(t):
                    evacuated(tl)
                    if t == 0:
                        pe.wait_ge(vsw_ready.sem, tl.next(vsw_ready))
                    bank = tr_bank(tl)
                    for h in range(H):
                        g, c = h % 4, h // 4
                        ins = nc.tensor.matmul(bank[32 * g:32 * g + 32, c * 128:(c + 1) * 128], VSW[0:KP, h, :],
                                               PTS[0:KP, h, :], start=True, stop=True)
                    ins.then_inc(tr_full.sem, 1)

                def out_transposes(t):
                    evacuated(tl)
                    bank = out_bank(tl)
                    transposes(bank, [OSB[:, c * 128:(c + 1) * 128] for c in range(4)]).then_inc(out_full.sem, 1)

                def ca_transposes(t):
                    pe.wait_ge(out_done.sem, tl.value(out_full))
                    bank = tr_bank(tl)
                    transposes(bank, [CA[:, k * 128:(k + 1) * 128] for k in range(KD)]).then_inc(tr_full.sem, 1)

                def projected(t):
                    evacuated(tl)
                    bank = out_bank(tl)
                    product(bank[:, 0:D], [(CAT[:, k, :], project[:, k, :]) for k in range(KD)])\
                        .then_inc(out_full.sem, 1)

                skewed([(6, lambda t: token_transposes(tl, lambda t: TOK[:, t % 2, :], t)), (5, projected),
                        (4, ca_transposes), (3, out_transposes), (2, values), (1, prob_transposes), (0, scores)])

            pe.wait_ge(setup_done.sem, 1)
            pe.wait_ge(d_aw, 16 * 5)
            with pe.Fori(0, B) as b:
                with pe.Fori(0, HALVES) as half:
                    tl = Tally("a", b * HALVES + half)
                    for t in range(BT):
                        token_transposes(tl, lambda t: XN[:, t, :], t)
                    evacuated(tl)
                    for m in range(KD):
                        feature_major(tl, cq, xTa, m)
                    evacuated(tl)
                    small_attention(tl, b, half, KB0, SC, co)
                    evacuated(tl)
                    for w in (sq, sk):
                        for m in range(KD):
                            feature_major(tl, w, xTb, m)
                    for t in range(BT):
                        bank = out_bank(tl)
                        product(bank[:, 0:D], [(xTb[:, k, t * 128:(t + 1) * 128], sv[:, k, :]) for k in range(KD)])\
                            .then_inc(out_full.sem, 1)
                    tl.close(tr_full, out_full, sc_full, tok_ready)

            def sq_bank(tl):
                bank = tl.slot(sq_full, 3)
                tl.next(sq_full)
                v = tl.back(sq_full, 3)
                pe.wait_ge(sq_done.sem, v)
                return SQ[bank]

            def max_scores(tl, j, kt):
                for hf in range(2):
                    bank = sq_bank(tl)
                    nc.tensor.matmul(bank, QX[j][0:QROWS, kt * 128:(kt + 1) * 128],
                                     KX[j][0:QROWS, hf * 512:(hf + 1) * 512], start=True, stop=True)\
                        .then_inc(sq_full.sem, 1)

            def maxima_transpose(tl, r, heads):
                pe.wait_ge(m_split.sem, heads)
                bank = sq_bank(tl)
                nc.tensor.transpose(bank.bitcast(BF16)[0:24, 0:128], ms[:, r, :], identb[:, :])\
                    .then_inc(sq_full.sem, 1)

            def head_out_transposes(tl):
                pe.wait_ge(pv_done.sem, tl.value(pv_full))
                bank = sq_bank(tl)
                transposes(bank, [OSB[:, s * 128:(s + 1) * 128] for s in range(2)]).then_inc(sq_full.sem, 1)

            tl = Tally("b0")
            pe.wait_ge(tr_done.sem, tr_done.base["b0"])
            pe.wait_ge(out_done.sem, out_done.base["b0"])
            pe.wait_ge(sc_done.sem, sc_done.base["b0"])
            for j in range(2):
                pe.wait_ge(d_head[j], 16 * 12)
                for kt in range(QT_PER_HEAD):
                    max_scores(tl, j, kt)
            maxima_transpose(tl, 0, 1)
            tl.close(sq_full)

            def head(tl, i, j, last):
                n = i * UNROLL + j

                def t_scores(kt):
                    for hf in range(2):
                        bank = tl.slot(st_full, 4)
                        tl.next(st_full)
                        pe.wait_ge(st_done.sem, tl.back(st_full, 4))
                        nc.tensor.matmul(SCR[:, bank, :], KX[j][0:QROWS + 3, kt * 128:(kt + 1) * 128],
                                         QX[j][0:QROWS + 3, hf * 512:(hf + 1) * 512], start=True, stop=True)\
                            .then_inc(st_full.sem, 1)

                def values(kt, ahead):
                    pe.wait_ge(st_done.sem, tl.back(st_full, ahead))
                    if kt == 0:
                        pe.wait_ge(pv_done.sem, tl.value(pv_full))
                        pe.wait_ge(vh_ready.sem, (n + 1))
                    for g in range(4):
                        ins = nc.tensor.matmul(PV[32 * g:32 * g + 32, 0:256], VH[:, j % 2, kt, :],
                                               PTB[:, kt % 2, g * 256:(g + 1) * 256], start=(kt == 0),
                                               stop=(kt == QT_PER_HEAD - 1))
                    if kt == QT_PER_HEAD - 1:
                        ins.then_inc(pv_full.sem, 1)
                        tl.next(pv_full)

                for kt in range(QT_PER_HEAD):
                    if not (last and j >= 2):
                        if kt == 0:
                            pe.wait_ge(d_head[(j + 2) % UNROLL], (i + (1 + (j + 2) // UNROLL)) * (16 * 12))
                        max_scores(tl, (j + 2) % UNROLL, kt)
                    if kt == 0:
                        pe.wait_ge(d_m2, (n + 1) * 16)
                    t_scores(kt)
                    if kt > 0:
                        values(kt - 1, 2)
                    if kt == 1 and j >= 1:
                        head_out_transposes(tl)
                    if kt == 2 and not (last and j == UNROLL - 1):
                        maxima_transpose(tl, (j + 1) % 2, n + 2)
                values(QT_PER_HEAD - 1, 0)
                if j == UNROLL - 1:
                    head_out_transposes(tl)

            with pe.Fori(0, NH // UNROLL - 1) as i:
                tl = Tally("b", i)
                for j in range(UNROLL):
                    head(tl, i, j, False)
                tl.close(sq_full, st_full, pv_full)
            tl = Tally("blast")
            for j in range(UNROLL):
                head(tl, NH // UNROLL - 1, j, True)
            tl.close(sq_full, st_full, pv_full)

            pe.wait_ge(sq_done.sem, sq_done.total)
            pe.wait_ge(st_done.sem, st_done.total)
            pe.wait_ge(pv_done.sem, pv_done.total)
            pe.wait_ge(d_cw, 16 * 5)
            pe.wait_ge(d_fifo, 16 * 2)
            pe.wait_ge(d_moe, 16 * 4)
            with pe.Fori(0, B) as b:
                with pe.Fori(0, HALVES) as half:
                    tl = Tally("c", b * HALVES + half)
                    for t in range(BT):
                        pe.wait_ge(stage_ready.sem, tl.next(stage_ready))
                        bank = tr_bank(tl)
                        transposes(bank, [TOK[:, t % 2, k * 128:(k + 1) * 128] for k in range(KD)])\
                            .then_inc(tr_full.sem, 1)
                    evacuated(tl)

                    def token_major(src, w, t, ks):
                        bank = out_bank(tl)
                        product(bank[:, 0:D], [(src[:, k, t * 128:(t + 1) * 128], w[:, k, :]) for k in ks])\
                            .then_inc(out_full.sem, 1)

                    lagged(lambda t: token_major(xTa, so, t, range(KD)),
                           lambda t: token_transposes(tl, lambda t: XN[:, t, :], t))
                    evacuated(tl)
                    for m in range(MF):
                        feature_major(tl, fi, xTb, m)
                    evacuated(tl)

                    lagged(lambda t: token_major(hid, fo, t, range(MF)),
                           lambda t: (tl.next(tok_ready), token_transposes(tl, lambda t: TOK[:, t % 2, :], t)))
                    evacuated(tl)
                    for hf in range(2):
                        bank = out_bank(tl)
                        for c in range(2):
                            t = 2 * hf + c
                            ins = product(bank[:, c * E:(c + 1) * E],
                                          [(xTa[:, k, t * 128:(t + 1) * 128], routerT[:, k, :]) for k in range(KD)])
                        ins.then_inc(out_full.sem, 1)

                    def expert_up(e):
                        for m in range(2):
                            feature_major(tl, w1, xTa, 2 * e + m)

                    expert_up(0)
                    for e in range(E):
                        if e + 1 < E:
                            expert_up(e + 1)
                        pe.wait_ge(a_ready.sem, tl.next(a_ready, 2))

                        def expert_down(t, e=e):
                            bank = out_bank(tl)
                            product(bank[:, 0:D], [(hid[:, (e % 2) * 2 + m, t * 128:(t + 1) * 128],
                                                    w2[:, 2 * e + m, :]) for m in range(2)]).then_inc(out_full.sem, 1)

                        if e < E - 1:
                            for t in range(BT):
                                expert_down(t)
                        else:
                            lagged(expert_down, lambda t: token_transposes(tl, lambda t: TOK[:, t % 2, :], t))
                    evacuated(tl)
                    for m in range(KD):
                        feature_major(tl, wq, xTb, m)
                    evacuated(tl)
                    small_attention(tl, b, half, KB1, SC1, wo)
                    evacuated(tl)
                    for m in range(MF):
                        feature_major(tl, fcT, xTb, m)
                    pe.wait_ge(a_ready.sem, tl.next(a_ready, MF))
                    for t in range(BT):
                        token_major(hid, projT, t, range(MF))
                    tl.close(tr_full, out_full, sc_full, tok_ready, a_ready)

        @block.scalar
        def _(act):
            def emptied(tl):
                bank = tl.slot(tr_full, 2)
                act.wait_ge(tr_full.sem, tl.next(tr_full))
                return TR[:, bank, :]

            tl = Tally("setup")
            bank = emptied(tl)
            nc.scalar.activation(ctxT.rearrange("p k (b n) -> p b k n", b=B),
                                 bank[:, 0:B * KD * SC].rearrange("p (b k n) -> p b k n", b=B, k=KD), ACT.Copy)\
                .then_inc(tr_done.sem, 1)
            for dst, bias in ((kT, cols["ck_b"]), (kT1, cols["bk"])):
                for m in range(KD):
                    bank = emptied(tl)
                    if m == 0:
                        act.wait_ge(d_kv, 16 * 8)
                    nc.scalar.activation(dst[:, m, :], bank[:, 0:B * SC], ACT.Identity, bias=bias[:, m:m + 1])\
                        .then_inc(tr_done.sem, 1)
            for hf in range(2):
                bank = emptied(tl)
                nc.scalar.activation(uT[:, hf * 512:(hf + 1) * 512], bank[0:R, :], ACT.Copy).then_inc(tr_done.sem, 1)
            bank = emptied(tl)
            act.wait_ge(d_low, 16 * 4)
            nc.scalar.activation(G_sb, bank[0:R, 0:D], ACT.Identity, scale=gate).then_inc(tr_done.sem, 1)
            for m in range(MF):
                bank = emptied(tl)
                nc.scalar.activation(fcT[:, :, m * 128:(m + 1) * 128],
                                     bank[:, 0:256].rearrange("p (k n) -> p k n", k=KD), ACT.Copy)\
                    .then_inc(tr_done.sem, 1)
            for m in range(KD):
                for hf in range(2):
                    bank = emptied(tl)
                    nc.scalar.activation(projT[:, 4 * hf:4 * hf + 4, m * 128:(m + 1) * 128],
                                         bank.rearrange("p (c n) -> p c n", c=4), ACT.Copy).then_inc(tr_done.sem, 1)

            def copy_transposed(tl, dst, t):
                bank = emptied(tl)
                nc.scalar.activation(dst[:, :, t * 128:(t + 1) * 128],
                                     bank[:, 0:256].rearrange("p (k n) -> p k n", k=KD), ACT.Copy)\
                    .then_inc(tr_done.sem, 1)

            def small_attention(tl, nk, dst):
                def exps(t):
                    act.wait_ge(sc_done.sem, tl.next(sc_done))
                    v = P[:, t % 2, :, 0:nk]
                    nc.scalar.activation(v, v, ACT.Exp, scale=DH ** -0.5).then_inc(p_ready.sem, 1)

                def prob_transposes(t):
                    for g in range(4):
                        bank = emptied(tl)
                        nc.scalar.activation(PTS[0:KP, 4 * g:4 * g + 4, :],
                                             bank[0:KP].rearrange("p (h n) -> p h n", h=4), ACT.Copy)\
                            .then_inc(tr_done.sem, 1)

                def values(t):
                    bank = emptied(tl)
                    nc.scalar.activation(OSB[:, :], bank, ACT.Copy).then_inc(tr_done.sem, 1)

                def ca(t):
                    copy_transposed(tl, CAT, 0)

                skewed([(6, lambda t: copy_transposed(tl, dst, t)), (4, ca), (2, values), (1, prob_transposes),
                        (0, exps)])

            act.wait_ge(d_const, 16 * 16)
            with act.Fori(0, B) as b:
                with act.Fori(0, HALVES) as half:
                    tl = Tally("a", b * HALVES + half)
                    for t in range(BT):
                        copy_transposed(tl, xTa, t)
                    for m in range(KD):
                        bank = emptied(tl)
                        nc.scalar.activation(QT[:, m, :], bank, ACT.Identity, bias=cols["cq_b"][:, m:m + 1])\
                            .then_inc(tr_done.sem, 1)
                    small_attention(tl, SC, xTb)
                    for e in range(4):
                        bank = emptied(tl)
                        bias = cols["sq_b" if e < 2 else "sk_b"][:, e % 2:e % 2 + 1]
                        if e >= 2:
                            act.wait_ge(pc_ready.sem, tl.next(pc_ready))
                        nc.scalar.activation(QT[:, e % 2, :], bank, ACT.Identity, bias=bias).then_inc(tr_done.sem, 1)
                    tl.close(tr_full, sc_done)

            def head(tl, j):
                for kt in range(QT_PER_HEAD):
                    for hf in range(2):
                        bank = tl.slot(st_full, 4)
                        act.wait_ge(st_full.sem, tl.next(st_full))
                        nc.scalar.activation(PTB[:, kt % 2, hf * 512:(hf + 1) * 512], SCR[:, bank, :], ACT.Exp,
                                             scale=DH ** -0.5).then_inc(st_done.sem, 1)
                act.wait_ge(pv_full.sem, tl.next(pv_full))
                nc.scalar.activation(OSB[:, 0:256], PV[:, 0:256], ACT.Copy).then_inc(pv_done.sem, 1)

            act.wait_ge(d_pieces, DC + 16 * 4 * B * HALVES)
            with act.Fori(0, NH // UNROLL - 1) as i:
                tl = Tally("b", i)
                for j in range(UNROLL):
                    head(tl, j)
            tl = Tally("blast")
            for j in range(UNROLL):
                head(tl, j)

            with act.Fori(0, B) as b:
                with act.Fori(0, HALVES) as half:
                    tl = Tally("c", b * HALVES + half)
                    for t in range(BT):
                        copy_transposed(tl, xTa, t)
                    for t in range(BT):
                        copy_transposed(tl, xTb, t)
                    for m in range(MF):
                        bank = emptied(tl)
                        nc.scalar.activation(hid[:, m, :], bank, ACT.Gelu, bias=cols["fi_b"][:, m:m + 1])\
                            .then_inc(tr_done.sem, 1)
                    for t in range(BT):
                        copy_transposed(tl, xTa, t)
                    act.wait_ge(out_done.sem, tl.next(out_done, 2 * BT + 2))
                    nc.scalar.activation(pr.rearrange("p t e -> p (t e)"), lg, ACT.Exp, scale=-1.0)\
                        .then_inc(gate_exp.sem, 1)

                    def relu(n):
                        bank = emptied(tl)
                        if n >= 2:
                            act.wait_ge(a_ready.sem, tl.next(a_ready))
                        nc.scalar.activation(RR[:, n % 2, :], bank, ACT.Relu).then_inc(tr_done.sem, 1)

                    for n in range(2 * E):
                        relu(n)
                    for t in range(BT):
                        copy_transposed(tl, xTb, t)
                    for m in range(KD):
                        bank = emptied(tl)
                        nc.scalar.activation(QT[:, m, :], bank, ACT.Identity, bias=cols["bq"][:, m:m + 1])\
                            .then_inc(tr_done.sem, 1)
                    small_attention(tl, SC1, xTb)
                    tl.next(a_ready, 2)
                    for n in range(MF):
                        relu(n)
                    tl.next(a_ready, 2)
                    tl.close(tr_full, a_ready)

        @block.vector
        def _(dve):
            steps = [0]

            def link(ins):
                steps[0] += 1
                ins.then_inc(s_dve, 1)
                dve.wait_ge(s_dve, steps[0])

            class Chain:
                def __init__(self, i, per):
                    self.i, self.per, self.n, self.at = i, per, 0, steps[0]

                def __call__(self, ins):
                    self.n += 1
                    ins.then_inc(s_dve, 1)
                    dve.wait_ge(s_dve, self.i * self.per + (self.at + self.n))
                    carry_wait(dve)

                def close(self, trips):
                    assert self.n == self.per, self.n
                    steps[0] += self.per * trips

            tl = Tally("setup")
            dve.wait_ge(c_ready.sem, c_ready.total)
            dve.wait_ge(d_mask, 32)
            m0 = mask0[0:3].rearrange("p b k -> p (b k)")
            link(nc.vector.tensor_scalar(masks, masks, 4.0, -3.0e38, ALU.mult, ALU.max))
            for c in range(3):
                link(nc.vector.tensor_copy(mpiece, masks))
                if c == 0:
                    link(nc.vector.tensor_scalar(m0, mpiece, identf[0:3, 0:1], None, ALU.mult))
                else:
                    link(nc.vector.scalar_tensor_tensor(m0, mpiece, identf[0:3, c:c + 1], m0, ALU.mult, ALU.add))
                link(nc.vector.tensor_tensor(masks, masks, mpiece, ALU.subtract))
            nc.vector.tensor_scalar(mask1[:, :, 0:SC], maski, 0, 4.0 * -1.0e9, ALU.is_equal, ALU.mult)\
                .then_inc(mask1_ready.sem, 1)
            dve.wait_ge(tr_done.sem, tl.next(tr_done, 5))
            dve.wait_ge(d_prefix, 16 * KD * 8 + 32)
            kb1 = KB1[:, :, :].rearrange("p b (k h n) -> p b k h n", k=KD, n=SC1)
            kb0 = KB0.rearrange("p b (k h n) -> p b k h n", k=KD, n=SC)
            for hh in range(8):
                bm = blockmask[:, hh:hh + 1]
                for b in range(B):
                    nc.vector.tensor_scalar(kb0[:, b, :, hh, :], kT[:, :, b * SC:(b + 1) * SC], bm, None, ALU.mult)
                    nc.vector.tensor_scalar(kb1[:, b, :, hh, 0:SC], kT1[:, :, b * SC:(b + 1) * SC], bm, None, ALU.mult)
                    ins = nc.vector.tensor_scalar(kb1[:, b, :, hh, SC:SC1], pkT, bm, None, ALU.mult)
            link(ins)
            for vs, bias in ((VS0, vb0), (VS1, vb1)):
                for b in range(B):
                    bank = tl.slot(out_full, 2)
                    dve.wait_ge(out_full.sem, tl.next(out_full))
                    if b == 0:
                        dve.wait_ge(d_kv, 16 * 8)
                    nc.vector.tensor_tensor(vs[0:SC, b, :, 0:DH],
                                            OUT[0:SC, bank, 0:D].rearrange("p (h d) -> p h d", d=DH),
                                            bias[0:SC].rearrange("p (h d) -> p h d", d=DH), ALU.add)\
                        .then_inc(out_done.sem, 1)
            dve.wait_ge(d_tern, 32)

            def scales(raw, m, width):
                sc, hi, lo = wscale[:, 0, 0:m], wscale[:, 1, 0:m], wscale[:, 2, 0:m]
                link(nc.vector.tensor_reduce(sc, raw, AX, ALU.add, apply_absolute_value=True))
                link(nc.vector.tensor_scalar(sc, sc, 1.0 / width, 1e-5, ALU.mult, ALU.max))
                nc.vector.tensor_scalar(hi, sc, 0.5, None, ALU.mult)
                link(nc.vector.tensor_scalar(lo, sc, -0.5, None, ALU.mult))

            def ternary(dst, raw, m):
                link(nc.vector.tensor_scalar(dst, raw[:, m, :], wscale[:, 2, m:m + 1], None, ALU.is_lt))
                link(nc.vector.scalar_tensor_tensor(dst, raw[:, m, :], wscale[:, 1, m:m + 1], dst,
                                                    ALU.is_gt, ALU.subtract))

            scales(wfc_raw, MF, D)
            for m in range(MF):
                if m > 0:
                    dve.wait_ge(tr_full.sem, 8 + m)
                ternary(tA, wfc_raw, m)
                bank = tl.slot(out_full, 2)
                dve.wait_ge(out_full.sem, tl.next(out_full))
                nc.vector.scalar_tensor_tensor(tA, tA, wscale[:, 0, m:m + 1], OUT[:, bank, 0:D], ALU.mult, ALU.add)\
                    .then_inc(out_done.sem, 1)
            scales(wproj_raw, KD, F)
            for m in range(KD):
                if m > 0:
                    dve.wait_ge(tr_full.sem, 8 + MF + 2 * m)
                ternary(wt, wproj_raw, m)
                nc.vector.tensor_scalar(wt, wt, wscale[:, 0, m:m + 1], None, ALU.mult).then_inc(wproj_scaled.sem, 1)
            tl.close(out_full)
            dve.wait_ge(tr_done.sem, tr_done.base["a"])
            nc.vector.memset(P[:, :, :, SC:KP], 0.0)
            nc.vector.memset(VX[:, :, :, DH:VW], 1.0)
            nc.vector.memset(VSW[:, :, VW:32], 0.0)
            dve.wait_ge(d_x, 16)
            dve.wait_ge(d_const, 16 * 16)
            nc.vector.memset(VH[:, :, :, VW:32], 0.0).then_inc(setup_done.sem, 1)
            dve.wait_ge(setup_done.sem, 1)

            def norm(tl, chain, src, dst, affine=None, after=None, signal=True):
                r = tl.slot(ln_stats, 4)
                carry_wait(dve)
                chain(nc.vector.bn_stats(stats, src))
                nc.vector.bn_aggr(mv[:, r, :], stats).then_inc(ln_stats.sem, 1)
                dve.wait_ge(ln_stats.sem, tl.next(ln_stats))
                dve.wait_ge(ln_rstd.sem, tl.next(ln_rstd))
                ins = nc.vector.tensor_scalar(dst, src, mv[:, r, 0:1], rstd[:, r:r + 1], ALU.subtract, ALU.mult)
                if affine:
                    chain(ins)
                    chain(nc.vector.tensor_tensor(dst, dst, rows[affine + "_g"][:, :], ALU.mult))
                    ins = nc.vector.tensor_tensor(dst, dst, rows[affine + "_be"][:, :], ALU.add)
                ins.then_inc(tok_ready.sem, 1)
                tl.next(tok_ready)

            def filled(tl):
                bank = tl.slot(out_full, 2)
                dve.wait_ge(out_full.sem, tl.next(out_full))
                return OUT[:, bank, :]

            def signal_out(tl, ins):
                ins.then_inc(out_done.sem, 1)
                dve.wait_ge(out_done.sem, tl.next(out_done))

            def small_attention(tl, chain, nk, projected):
                def scores(t):
                    dve.wait_ge(sc_full.sem, tl.next(sc_full))
                    v = SCR[:, :, 0:CHUNK_HEADS * nk].rearrange("p c (h k) -> p c h k", k=nk)
                    chain(nc.vector.tensor_reduce(mx, v, AX, ALU.max))
                    nc.vector.tensor_tensor(P[:, t % 2, :, 0:nk].rearrange("p (c h) k -> p c h k", c=NCH), v,
                                            mx.rearrange("p (c h) -> p c h", c=NCH).unsqueeze(3)
                                            .to_broadcast([128, NCH, CHUNK_HEADS, nk]), ALU.subtract)\
                        .then_inc(sc_done.sem, 1)

                def normalise(t):
                    bank = filled(tl).rearrange("p (h d) -> p h d", d=32)
                    chain(nc.vector.reciprocal(rsum, bank[:, :, DH]))
                    signal_out(tl, nc.vector.tensor_tensor(CA[:, :].rearrange("p (h d) -> p h d", d=DH),
                                                           bank[:, :, 0:DH],
                                                           rsum.unsqueeze(2).to_broadcast([128, H, DH]), ALU.mult))

                skewed([(5, projected), (3, normalise), (0, scores)])

            with dve.Fori(0, B) as b:
                with dve.Fori(0, HALVES) as half:
                    i = b * HALVES + half
                    tl = Tally("a", i)
                    chain = Chain(i, BT + 5 * BT + 12)
                    nc.vector.tensor_copy(VSW[0:KP, :, 0:VW], VS0[0:KP, b, :, :]).then_inc(vsw_ready.sem, 1)
                    for t in range(BT):
                        norm(tl, chain, X[:, i * BT + t, :], XN[:, t, :])

                    def projected(t):
                        bank = filled(tl)
                        dve.wait_ge(resid_ready.sem, tl.next(resid_ready))
                        signal_out(tl, nc.vector.tensor_tensor(HB[:, t % 2, :], bank[:, 0:D], RB[:, t, :], ALU.add))
                        dve.wait_ge(d_x1[t % 2], i * (BT // 2 * 16) + (t // 2 * 16 + DC))
                        norm(tl, chain, HB[:, t % 2, :], TOK[:, t % 2, :], affine="co")

                    small_attention(tl, chain, SC, projected)
                    tl.next(tr_done, 4 + 2 + 7 * BT)
                    dve.wait_ge(d_pieces, i * (16 * 4) + DC)
                    for e in range(4):
                        dve.wait_ge(tr_done.sem, tl.next(tr_done))
                        f = QT[:, e % 2, :]
                        chain(nc.vector.tensor_copy(PC[:, e, 0, :], f))
                        chain(nc.vector.tensor_tensor(RR[:, 0, :], f, PC[:, e, 0, :], ALU.subtract))
                        chain(nc.vector.tensor_copy(PC[:, e, 1, :], RR[:, 0, :]))
                        nc.vector.tensor_tensor(PC[:, e, 2, :], RR[:, 0, :], PC[:, e, 1, :], ALU.subtract)\
                            .then_inc(pc_ready.sem, 1)
                        dve.wait_ge(pc_ready.sem, tl.next(pc_ready))
                    for t in range(BT):
                        bank = filled(tl)
                        signal_out(tl, nc.vector.tensor_tensor(
                            VX[:, bass.ds(b * H, H), half * BT + t, 0:DH],
                            bank[:, 0:D].rearrange("p (h d) -> p h d", d=DH),
                            rows["sv_b"][:, :].rearrange("p (h d) -> p h d", d=DH), ALU.add))
                    tl.close(tr_done, out_full, out_done, sc_full, ln_stats, tok_ready)
            chain.close(B * HALVES)

            dve.wait_ge(sc_full.sem, sc_full.base["b0"])
            for j in range(UNROLL):
                ins = nc.vector.memset(KX[j][QROWS:QROWS + 3, :], 1.0)
            link(ins)

            def sq_filled(tl):
                bank = tl.slot(sq_full, 3)
                dve.wait_ge(sq_full.sem, tl.next(sq_full))
                return SQ[bank]

            def max_scores(tl, kt):
                for hf in range(2):
                    bank = sq_filled(tl)
                    nc.vector.tensor_reduce(nm2[:, 2 * kt + hf:2 * kt + hf + 1], bank, AX, ALU.max)\
                        .then_inc(sq_done.sem, 1)
                    tl.next(sq_done)

            def maxima(tl, r):
                dve.wait_ge(sq_done.sem, tl.value(sq_done))
                nc.vector.tensor_reduce(nm[:, r, :], nm2.rearrange("p (q h) -> p q h", h=2), AX, ALU.max,
                                        negate=True).then_inc(max_ready.sem, 1)
                dve.wait_ge(max_ready.sem, tl.next(max_ready))

            def maxima_rows(tl, stored):
                bank = sq_filled(tl)
                dve.wait_ge(d_m1, stored)
                nc.vector.tensor_copy(MT[:, :], bank.bitcast(BF16)[0:24, 0:128]).then_inc(sq_done.sem, 1)
                tl.next(sq_done)

            def head_out(tl, chain, n):
                bank = sq_filled(tl)[:, 0:256].rearrange("p (s g d) -> p g s d", s=2, g=4)
                rs = rsum[:, 0:8].rearrange("p (g s) -> p g s", s=2)
                chain(nc.vector.reciprocal(rs, bank[:, :, :, DH]))
                nc.vector.tensor_tensor(OA[:, n, :, :].rearrange("p (g s) d -> p g s d", s=2),
                                        bank[:, :, :, 0:DH],
                                        rs.unsqueeze(3).to_broadcast([128, 4, 2, DH]), ALU.mult)\
                    .then_inc(sq_done.sem, 1)
                dve.wait_ge(sq_done.sem, tl.next(sq_done))

            tl = Tally("b0")
            for j in range(2):
                for kt in range(QT_PER_HEAD):
                    max_scores(tl, kt)
                maxima(tl, j)
            maxima_rows(tl, 0)
            tl.close(sq_full)

            def head(tl, chain, i, j, last):
                n = i * UNROLL + j
                for kt in range(QT_PER_HEAD):
                    if not (last and j >= 2):
                        max_scores(tl, kt)
                    if kt == 1 and j >= 1:
                        head_out(tl, chain, n - 1)
                    if kt == 2 and not (last and j == UNROLL - 1):
                        maxima_rows(tl, (n + 1) * 16)
                if not (last and j >= 2):
                    maxima(tl, j % 2)
                if j == UNROLL - 1:
                    head_out(tl, chain, n)

            with dve.Fori(0, NH // UNROLL - 1) as i:
                tl = Tally("b", i)
                chain = Chain(i, UNROLL)
                for j in range(UNROLL):
                    head(tl, chain, i, j, False)
                tl.close(sq_full, sq_done, max_ready)
            chain.close(NH // UNROLL - 1)
            tl = Tally("blast")
            chain = Chain(0, UNROLL)
            for j in range(UNROLL):
                head(tl, chain, NH // UNROLL - 1, j, True)
            tl.close(sq_full, sq_done, max_ready)
            chain.close(1)

            with dve.Fori(0, B) as b:
                with dve.Fori(0, HALVES) as half:
                    i = b * HALVES + half
                    tl = Tally("c", i)
                    chain = Chain(i, 3 * BT + 5 * BT + 20 + BT + 4 * BT)
                    nc.vector.tensor_copy(VSW[0:KP, :, 0:VW], VS1[0:KP, b, :, :]).then_inc(vsw_ready.sem, 1)

                    def with_residual(t):
                        bank = filled(tl)
                        dve.wait_ge(resid_ready.sem, tl.next(resid_ready))
                        signal_out(tl, nc.vector.tensor_tensor(HB[:, t % 2, :], bank[:, 0:D], RB[:, t, :], ALU.add))

                    dve.wait_ge(d_out, i * (16 * BT) + DC)
                    for t in range(BT):
                        with_residual(t)
                        norm(tl, chain, HB[:, t % 2, :], XN[:, t, :], affine="so")
                    for t in range(BT):
                        with_residual(t)
                        xt = X[:, i * BT + t, :]
                        norm(tl, chain, HB[:, t % 2, :], HB[:, t % 2, :], affine="fo")
                        dve.wait_ge(tok_ready.sem, tl.value(tok_ready))
                        chain(nc.vector.tensor_tensor(xt, xt, HB[:, t % 2, :], ALU.add))
                        norm(tl, chain, xt, TOK[:, t % 2, :])
                    for hf in range(2):
                        bank = filled(tl)
                        signal_out(tl, nc.vector.tensor_copy(lg[:, hf * 2 * E:(hf + 1) * 2 * E], bank[:, 0:2 * E]))
                    dve.wait_ge(gate_exp.sem, tl.next(gate_exp))
                    chain(nc.vector.tensor_scalar(pr, pr, 1.0, None, ALU.add))
                    chain(nc.vector.reciprocal(pr, pr))
                    rk = rank.unsqueeze(1).to_broadcast([128, BT, E])
                    chain(nc.vector.tensor_copy(pw, pr))
                    for c in range(2):
                        v, key = top[:, 3 * c, :], top[:, 3 * c + 1, :]
                        vb = v.unsqueeze(2).to_broadcast([128, BT, E])
                        chain(nc.vector.tensor_reduce(v, pw, AX, ALU.max))
                        chain(nc.vector.tensor_tensor(eq, pw, vb, ALU.is_equal))
                        chain(nc.vector.tensor_tensor(eq, eq, rk, ALU.mult))
                        chain(nc.vector.tensor_reduce(key, eq, AX, ALU.max))
                        h = hot if c == 0 else eq
                        chain(nc.vector.tensor_tensor(h, eq, key.unsqueeze(2).to_broadcast([128, BT, E]), ALU.is_equal))
                        if c == 0:
                            chain(nc.vector.scalar_tensor_tensor(pw, h, -4.0, pw, ALU.mult, ALU.add))
                        else:
                            chain(nc.vector.tensor_tensor(hot, hot, h, ALU.add))
                    chain(nc.vector.tensor_tensor(top[:, 2, :], top[:, 0, :], top[:, 3, :], ALU.add))
                    chain(nc.vector.tensor_scalar(top[:, 2, :], top[:, 2, :], 1e-20, None, ALU.add))
                    chain(nc.vector.reciprocal(top[:, 5, :], top[:, 2, :]))
                    nc.vector.tensor_tensor(hot, hot, pr, ALU.mult).then_inc(s_dve, 1)
                    chain.n += 1
                    dve.wait_ge(s_dve, chain.i * chain.per + (chain.at + chain.n))
                    nc.vector.tensor_tensor(cw, hot, top[:, 5, :].unsqueeze(2).to_broadcast([128, BT, E]), ALU.mult)\
                        .then_inc(s_dve, 1)
                    chain.n += 1
                    dve.wait_ge(s_dve, chain.i * chain.per + (chain.at + chain.n))

                    def square(slot):
                        dve.wait_ge(tr_done.sem, tl.next(tr_done))
                        r = RR[:, square.n % 2, :]
                        square.n += 1
                        nc.vector.tensor_tensor(hid[:, slot, :], r, r, ALU.mult).then_inc(a_ready.sem, 1)

                    square.n = 0
                    tl.next(tr_done, 4 + 4 + MF + 4)

                    def up(e):
                        for m in range(2):
                            square((e % 2) * 2 + m)

                    up(0)
                    for e in range(E):
                        if e + 1 < E:
                            up(e + 1)
                        for t in range(BT):
                            bank = filled(tl)
                            xt = X[:, i * BT + t, :]
                            signal_out(tl, nc.vector.scalar_tensor_tensor(xt, bank[:, 0:D], cw[:, t, e:e + 1], xt,
                                                                          ALU.mult, ALU.add))
                            if e == E - 1:
                                norm(tl, chain, xt, TOK[:, t % 2, :])

                    def projected(t):
                        bank = filled(tl)
                        xt = X[:, i * BT + t, :]
                        signal_out(tl, nc.vector.tensor_tensor(xt, bank[:, 0:D], xt, ALU.add))
                        chain(nc.vector.tensor_tensor(xt, xt, rows["bo"][:, :], ALU.add))
                        norm(tl, chain, xt, TOK[:, t % 2, :])

                    small_attention(tl, chain, SC1, projected)
                    tl.next(tr_done, 4 + 2 + 7 * BT)
                    for m in range(MF):
                        square(m)
                    for t in range(BT):
                        bank = filled(tl)
                        nc.vector.tensor_tensor(XN[:, t, :], bank[:, 0:D], X[:, i * BT + t, :], ALU.add)\
                            .then_inc(out_done.sem, 1)
                        tl.next(out_done)
                    tl.close(tr_done, out_full, out_done, sc_full, ln_stats, tok_ready, resid_ready)
            chain.close(B * HALVES)

        @block.gpsimd
        def _(pool):
            steps = [0]

            def link(ins):
                steps[0] += 1
                ins.then_inc(s_pool, 1)
                pool.wait_ge(s_pool, steps[0])

            for s in (sc_full, sc_done, st_full, st_done, pv_full, pv_done):
                pool.sem_inc(s.sem, s.credit)
            for s in (d_pieces, d_x1[0], d_x1[1], d_out):
                pool.sem_inc(s, DC)
            nc.gpsimd.memset(identf[:, :], 0.0)
            nc.gpsimd.memset(identb[:, :], 0.0)
            nc.gpsimd.memset(blockmask[:, :], 1.0)
            nc.gpsimd.memset(minus_half, -0.5)
            nc.gpsimd.memset(onesb[:, :], 1.0)
            nc.gpsimd.memset(mask0[:, :, :], 0.0)
            nc.gpsimd.memset(mask1[:, :, :], 0.0)
            nc.gpsimd.memset(VS0[:, :, :, :], 0.0)
            link(nc.gpsimd.memset(VS1[:, :, :, :], 0.0))
            for m in (identf, identb):
                nc.gpsimd.affine_select(out=m[:, :], in_=m[:, :], compare_op=ALU.not_equal, fill=1.0, base=0,
                                        pattern=[[-1, 128]], channel_multiplier=1).then_inc(c_ready.sem, 1)
            for vs in (VS0, VS1):
                nc.gpsimd.memset(vs[:, :, :, DH:VW], 1.0).then_inc(c_ready.sem, 1)
            link(nc.gpsimd.affine_select(out=blockmask[:, :], in_=blockmask[:, :], compare_op=ALU.is_ge, fill=0.0,
                                         base=0, pattern=[[-DH, 128 // DH]], channel_multiplier=1))
            nc.gpsimd.affine_select(out=blockmask[:, :], in_=blockmask[:, :], compare_op=ALU.is_ge, fill=0.0,
                                    base=DH - 1, pattern=[[DH, 128 // DH]], channel_multiplier=-1)\
                .then_inc(c_ready.sem, 1)
            for e in range(E):
                ins = nc.gpsimd.memset(rank[:, e:e + 1], float(E - e))
            ins.then_inc(c_ready.sem, 1)

            class Chain:
                def __init__(self, i, per):
                    self.i, self.per, self.n, self.at = i, per, 0, steps[0]

                def __call__(self, ins):
                    self.n += 1
                    ins.then_inc(s_pool, 1)
                    pool.wait_ge(s_pool, self.i * self.per + (self.at + self.n))
                    carry_wait(pool)

                def close(self, trips):
                    assert self.n == self.per, self.n
                    steps[0] += self.per * trips

            def root(tl, chain):
                r = tl.slot(ln_stats, 4)
                pool.wait_ge(ln_stats.sem, tl.next(ln_stats))
                carry_wait(pool)
                chain(nc.gpsimd.tensor_scalar(ve[:, r:r + 1], mv[:, r, 1:2], EPS, None, ALU.add))
                nc.gpsimd.tensor_tensor(rstd[:, r:r + 1], ve[:, r:r + 1], minus_half, ALU.pow)\
                    .then_inc(ln_rstd.sem, 1)

            pool.wait_ge(setup_done.sem, 1)
            with pool.Fori(0, B) as b:
                with pool.Fori(0, HALVES) as half:
                    i = b * HALVES + half
                    tl = Tally("a", i)
                    chain = Chain(i, 2 * BT)
                    for t in range(BT):
                        root(tl, chain)
                    for t in range(BT):
                        pool.wait_ge(tok_ready.sem, tl.next(tok_ready))
                        nc.gpsimd.tensor_tensor(RB[:, t, :], XN[:, t, :], rows["co_b"][:, :], ALU.add)\
                            .then_inc(resid_ready.sem, 1)
                    for t in range(BT):
                        root(tl, chain)
            chain.close(B * HALVES)

            def head_values(n, j):
                carry_wait(pool)
                nc.gpsimd.tensor_copy(VH[:, j % 2, :, 0:VW], VX[:, n, :, :]).then_inc(vh_ready.sem, 1)

            def split(tl, chain, r):
                pool.wait_ge(max_ready.sem, tl.next(max_ready))
                carry_wait(pool)
                v = nm[:, r, :]
                chain(nc.gpsimd.tensor_copy(ms[:, r, 0:8], v))
                chain(nc.gpsimd.tensor_tensor(nres, v, ms[:, r, 0:8], ALU.subtract))
                chain(nc.gpsimd.tensor_copy(ms[:, r, 8:16], nres))
                nc.gpsimd.tensor_tensor(ms[:, r, 16:24], nres, ms[:, r, 8:16], ALU.subtract).then_inc(m_split.sem, 1)
                pool.wait_ge(m_split.sem, tl.next(m_split))

            pool.wait_ge(out_done.sem, out_done.base["b0"])
            tl = Tally("b0")
            chain = Chain(0, 6)
            for j in range(2):
                head_values(j, j)
            for j in range(2):
                split(tl, chain, j)
            chain.close(1)

            def head(tl, chain, i, j, last):
                n = i * UNROLL + j
                if not (last and j >= 2):
                    split(tl, chain, j % 2)
                    pool.wait_ge(pv_full.sem, tl.next(pv_full))
                    head_values(n + 2, j)

            with pool.Fori(0, NH // UNROLL - 1) as i:
                tl = Tally("b", i)
                chain = Chain(i, 3 * UNROLL)
                for j in range(UNROLL):
                    head(tl, chain, i, j, False)
            chain.close(NH // UNROLL - 1)
            tl = Tally("blast")
            chain = Chain(0, 3 * (UNROLL - 2))
            for j in range(UNROLL):
                head(tl, chain, NH // UNROLL - 1, j, True)
            chain.close(1)

            pool.wait_ge(sq_done.sem, sq_done.total)
            with pool.Fori(0, B) as b:
                with pool.Fori(0, HALVES) as half:
                    i = b * HALVES + half
                    tl = Tally("c", i)
                    chain = Chain(i, 5 * BT)
                    pool.wait_ge(tok_ready.sem, tl.value(tok_ready))
                    pool.wait_ge(tr_done.sem, tl.value(tr_done))
                    for t in range(BT):
                        if t >= 2:
                            pool.wait_ge(tr_full.sem, tl.next(tr_full))
                        carry_wait(pool)
                        nc.gpsimd.tensor_copy(TOK[:, t % 2, :].rearrange("p (h d) -> p h d", d=DH),
                                              OA[:, bass.ds(b * H, H), half * BT + t, :]).then_inc(stage_ready.sem, 1)
                    for t in range(BT):
                        if t == 0:
                            pool.wait_ge(d_x1_back, i * 16 + 16)
                        nc.gpsimd.tensor_tensor(RB[:, t, :], RB[:, t, :], rows["so_b"][:, :], ALU.add)\
                            .then_inc(resid_ready.sem, 1)
                    for t in range(BT):
                        root(tl, chain)
                        pool.wait_ge(tok_ready.sem, tl.next(tok_ready))
                        nc.gpsimd.tensor_tensor(RB[:, t, :], XN[:, t, :], rows["fo_b"][:, :], ALU.add)\
                            .then_inc(resid_ready.sem, 1)
                    for _ in range(4 * BT):
                        root(tl, chain)
                    tl.close(ln_stats)
            chain.close(B * HALVES)


def kernel(**inputs):
    import concourse.bacc as bacc
    from concourse.bass_utils import run_bass_kernel_spmd

    nc = bacc.Bacc("TRN2", target_bir_lowering=False, num_devices=1)
    arrays, aps = {}, {}
    for name, value in inputs.items():
        a = np.ascontiguousarray(value)
        if a.ndim == 0:
            a = a.reshape(1)
        arrays[f"in_{name}"] = a
        aps[name] = nc.dram_tensor(f"in_{name}", a.shape, mybir.dt.from_np(a.dtype), kind="ExternalInput").ap()
    out = nc.dram_tensor("out", (B, S, D), F32, kind="ExternalOutput").ap()
    build(nc, aps, out)
    result = run_bass_kernel_spmd(nc, [arrays], core_ids=[0])
    return result.results[0]["out"]
```

```python
from contextlib import ExitStack

import numpy as np
import concourse.bass as bass
from concourse import mybir

F32 = mybir.dt.float32
BF16 = mybir.dt.bfloat16
I32 = mybir.dt.int32
ALU = mybir.AluOpType
ACT = mybir.ActivationFunctionType
AX = mybir.AxisListType.X

B, S, D, H = 2, 1024, 256, 16
DH = D // H
KD = D // 128
SC = 77
NP = 10
SC1 = SC + NP
F = 1024
MF = F // 128
E, W = 8, 256
R = 16
T = B * S // 128
BT = 4
N = BT * 128
TB = S // 128
BLOCKS = TB // BT
QT_PER_HEAD = S // 128
KP = 96
NH = B * H
VW = DH + 1
EPS = 1e-5
DC = 16
CHUNK_HEADS = 4
NCH = H // CHUNK_HEADS
QROWS = 6 * DH
UNROLL = 4


STEP = {
    "VW": dict(vsw=1),
    "LS": dict(ln=1),
    "LN0": dict(tr=1, tok=1),
    "QP": dict(tr=KD),
    "S": dict(sc=1),
    "E": dict(exp=1),
    "T": dict(tr=4),
    "PV": dict(tr=1),
    "OT": dict(out=1),
    "CT": dict(tr=1),
    "PJ": dict(out=1, ln=1),
    "PN": dict(tok=1),
    "LT": dict(tr=1),
    "RA": dict(res=1),
    "QK": dict(tr=2 * KD, pc=2 * KD),
    "SV": dict(out=1),
    "LD": dict(),
    "ST": dict(tr=1),
    "RS": dict(res=1),
    "SO": dict(out=1, ln=1),
    "SN": dict(tok=1),
    "LX": dict(tr=1),
    "FI": dict(tr=MF),
    "RF": dict(res=1),
    "FO": dict(out=1, ln=1),
    "FN": dict(ln=1),
    "FM": dict(tok=1),
    "L2": dict(tr=1),
    "RT": dict(out=2, gate=1),
    "UP": dict(tr=2, act=2),
    "DN": dict(out=1),
    "DL": dict(out=1, ln=1),
    "DM": dict(tok=1),
    "L3": dict(tr=1),
    "RX": dict(res=1),
    "FC": dict(tr=MF, act=MF),
    "FP": dict(out=1),
}
ORDER_A = """
LS.0 LS.1 LS.2 LS.3 LS.4 LS.5 LS.6 LS.7 VW LN0.0 LN0.1 RA.0 LN0.2 RA.1 LN0.3 RA.2 LN0.4 RA.3 QP.0 RA.4 LN0.5
LN0.6 RA.5 S.0 RA.6 E.0 S.1 T.0 E.1 PV.0 LN0.7 S.2 T.1 OT.0 RA.7 E.2 PV.1 CT.0 S.3 T.2 OT.1 QP.1 E.3 PV.2 PJ.0
T.3 PN.0 S.4 CT.1 OT.2 LT.0 PV.3 PJ.1 E.4 S.5 CT.2 OT.3 T.4 PN.1 PJ.2 E.5 PV.4 CT.3 S.6 T.5 PN.2 OT.4 LT.1 PJ.3
E.6 PV.5 T.6 PN.3 S.7 CT.4 LT.3 OT.5 LT.2 PJ.4 QK.0 E.7 CT.5 PN.4 SV.0 SV.1 PV.6 T.7 PJ.5 OT.6 PV.7 CT.6 PN.5
SV.3 OT.7 PJ.6 CT.7 SV.2 PJ.7 LT.4 PN.6 LT.5 SV.4 SV.5 PN.7 LT.6 SV.6 LT.7 QK.1 SV.7
"""
ORDER_C = """
LD.0 ST.0 ST.1 ST.2 ST.3 VW RS.0 RS.1 RS.2 RS.3 SO.0 SO.1 ST.4 SO.2 SO.3 LD.1 RS.4 RS.5 RS.6 RS.7 SN.0 SN.1 ST.5
ST.6 ST.7 SN.2 SN.3 LX.0 RF.0 LX.1 RF.1 LX.2 RF.2 LX.3 RF.3 FI.0 FO.0 FO.1 FN.0 FO.2 FN.1 FO.3 FN.2 SO.4 FM.0
FM.1 SO.5 FN.3 SO.6 L2.0 L2.1 SO.7 FM.2 SN.4 SN.5 FM.3 SN.6 L2.2 SN.7 LX.4 RF.4 LX.5 L2.3 RF.5 UP.0.0 LX.7 RT.0
LX.6 RF.7 UP.0.1 RF.6 FI.1 DN.0.0.3 DN.0.0.0 DN.0.0.2 DN.0.0.1 UP.0.2 DN.0.1.0 DN.0.1.2 DN.0.1.1 DN.0.1.3 UP.0.3
FO.4 DN.0.2.3 DN.0.2.0 FN.4 DN.0.2.2 DN.0.2.1 UP.0.4 FO.5 DN.0.3.0 FM.4 DN.0.3.2 FN.5 DN.0.3.1 DN.0.3.3 UP.0.5
FO.6 DN.0.4.3 FM.5 L2.4 DN.0.4.0 FN.6 DN.0.4.2 DN.0.4.1 UP.0.6 FO.7 DN.0.5.0 L2.5 DN.0.5.2 FN.7 DN.0.5.1
DN.0.5.3 UP.0.7 DN.0.6.0 DN.0.6.2 FM.6 FM.7 DN.0.6.1 DN.0.6.3 DL.0.7.3 DL.0.7.0 L2.7 DL.0.7.2 DL.0.7.1 DM.0 L2.6
RT.1 UP.1.0 DM.1 UP.1.1 DN.1.0.4 DN.1.0.6 RX.0 RX.1 L3.0 DM.2 L3.1 DM.3 DN.1.0.5 DN.1.0.7 UP.1.2 DN.1.1.4
DN.1.1.6 RX.2 RX.3 L3.3 DN.1.1.5 DN.1.1.7 UP.1.3 DN.1.2.5 DN.1.2.7 L3.2 DN.1.2.4 DN.1.2.6 UP.1.4 DN.1.3.4
DN.1.3.6 QP.0 DN.1.3.5 DN.1.3.7 UP.1.5 DN.1.4.4 DN.1.4.6 S.0 DN.1.4.5 DN.1.4.7 UP.1.6 DN.1.5.6 DN.1.5.5 E.0 S.1
T.0 DN.1.5.7 PV.0 DN.1.5.4 UP.1.7 OT.0 DN.1.6.4 E.1 S.2 T.1 DL.1.7.4 PV.1 CT.0 DN.1.6.5 DL.1.7.5 DN.1.6.6 DM.4
E.2 T.2 DL.1.7.6 RX.4 DN.1.6.7 DM.5 L3.4 DL.1.7.7 RX.5 OT.1 PV.2 DM.6 L3.5 PJ.0 RX.6 CT.1 DM.7 OT.2 L3.6 S.3
RX.7 L3.7 PJ.1 QP.1 CT.2 E.3 PN.0 PN.1 S.4 T.3 PJ.2 E.4 PV.3 S.5 T.4 OT.3 LT.0 PV.4 E.5 CT.3 S.6 T.5 OT.4 PJ.3
E.6 S.7 CT.4 PV.5 T.6 E.7 OT.5 LT.1 PV.6 PJ.4 PN.2 PN.3 T.7 CT.5 OT.6 PV.7 LT.2 PJ.5 CT.6 LT.3 OT.7 PN.4 FC.0
PJ.6 CT.7 PN.5 LT.4 PJ.7 FP.0 PN.6 LT.5 PN.7 FP.1 LT.7 LT.6 FP.2 FP.3 FC.1 FP.4 FP.5 FP.6 FP.7
"""


def attention_order(before):
    for t in range(TB - 1):
        for a, b in (("PV", "T"), ("OT", "PV"), ("CT", "OT"), ("PJ", "CT")):
            before((a, t), (b, t + 1))
        if t + 2 < TB:
            before(("T", t), ("S", t + 2))
            before(("LT", t), ("PN", t + 2))
    before(("S", BT - 1), ("QP", 1))
    before(("QP", 1), ("S", BT))


def parsed(text):
    order = [(w.split(".")[0], *map(int, w.split(".")[1:])) for w in text.split()]
    assert len(set(order)) == len(order)

    def before(a, b):
        assert order.index(a) < order.index(b), (a, b)

    return order, before


def schedule_a():
    order, before = parsed(ORDER_A)
    attention_order(before)
    for t in range(BT):
        before(("SV", t), ("LT", BT))
    for t in range(TB - 2):
        before(("PN", t), ("PJ", t + 2))
    return order


def schedule_c():
    order, before = parsed(ORDER_C)
    attention_order(before)
    for t in range(BT):
        before(("SO", t), ("ST", t + BT))
        before(("FO", t), ("SO", t + BT))
        before(("SO", t), ("LD", 1))
        before(("DN", 0, E - 2, t), ("UP", 1, 0))
        before(("DL", 0, E - 1, t), ("UP", 1, 1))
        before(("FO", t), ("FI", 1))
        before(("SO", t + BT), ("LT", 0))
        before(("FO", t + BT), ("FC", 0))
        before(("FP", t), ("FC", 1))
        before(("ST", t + BT), ("T", 0))
    for t in range(TB - 2):
        before(("FN", t), ("FO", t + 2))
        before(("L2", t), ("FM", t + 2))
        before(("L3", t), ("DM", t + 2))
    for k in range(BLOCKS):
        for e in range(2, E):
            for t in range(BT):
                before(("DN", k, e - 2, k * BT + t), ("UP", k, e))
    before(("FI", 0), ("LX", BT))
    before(("RT", 0), ("RT", 1))
    before(("FI", 1), ("L3", 0))
    before(("QP", 0), ("L3", BT))
    before(("FC", 0), ("LT", BT))
    return order


class Signal:

    TRIPS = {"setup": 1, "a": B, "b0": 1, "b": NH // UNROLL - 1, "blast": 1, "c": B}

    def __init__(self, sem, credit=0, **per):
        self.sem, self.credit = sem, credit
        self.per = {part: per.get(part, 0) for part in self.TRIPS}
        self.base, total = {}, credit
        for part, n in self.per.items():
            self.base[part] = total
            total += n * self.TRIPS[part]
        self.total = total


class Tally:

    def __init__(self, part, i=0):
        self.part, self.i, self.n = part, i, {}

    def at(self, s, n):
        return self.i * s.per[self.part] + max(s.base[self.part] + n, s.credit)

    def value(self, s):
        return self.at(s, self.n.get(s, 0))

    def next(self, s, m=1):
        self.n[s] = self.n.get(s, 0) + m
        return self.value(s)

    def back(self, s, lag):
        return self.at(s, self.n.get(s, 0) - lag)

    def slot(self, s, ring):
        before = s.base[self.part] - s.credit
        assert before % ring == 0 and (isinstance(self.i, int) or s.per[self.part] % ring == 0)
        return self.n.get(s, 0) % ring

    def slot_of(self, s, ring, *step):
        n = self.counts[step][s]
        assert self.n.get(s, 0) <= n - 1 + ring, step
        return (n - 1) % ring

    def close(self, *signals):
        for s in signals:
            assert self.n.get(s, 0) == s.per[self.part], (self.part, s.sem, self.n.get(s, 0), s.per[self.part])

    def walk(self, order, groups, handlers):
        self.counts, n = {}, {s: 0 for g in groups.values() for s in g}
        for step in order:
            for g, m in STEP[step[0]].items():
                for s in groups[g]:
                    n[s] += m
            self.counts[step] = dict(n)
        n = {s: 0 for s in n}
        for self.now, step in enumerate(order):
            self.n = dict(n)
            if step[0] in handlers:
                handlers[step[0]](*step[1:])
            n = self.counts[step]

    def after(self, s, *step):
        assert list(self.counts).index(step) <= self.now, step
        return self.at(s, self.counts[step][s])

    def after_block(self, s, name, k):
        last = max(range(k * BT, (k + 1) * BT), key=lambda t: self.counts[name, t][s])
        return self.after(s, name, last)


def build(nc, A, out):
    ctx = ExitStack()
    with ctx:
        def sb(name, shape, dt=F32):
            return ctx.enter_context(nc.sbuf_tensor(name, shape, dt))

        def ps(name, shape, dt=F32):
            return ctx.enter_context(nc.psum_tensor(name, shape, dt))

        def sem(name):
            return ctx.enter_context(nc.semaphore(name))

        X = sb("X", [128, T, D])
        wfc_raw = X[:, 0:MF, :]
        wproj_raw = X[:, MF:, :].rearrange("p t d -> p (t d)").rearrange("p (m d) -> p m d", m=KD)

        shared = sb("shared", [128, 3 * 4096])
        VX = shared[:, 0:NH * 8 * VW].rearrange("p (n k d) -> p n k d", n=NH, k=8)
        o = NH * 8 * VW
        PC = shared[:, o:o + 3072].bitcast(BF16).rearrange("p (e c n) -> p e c n", e=4, c=3)
        PTB = shared[:, o:o + 2048].rearrange("p (r n) -> p r n", r=2)
        o += 3072
        KB0 = shared[:, o:o + B * H * SC].rearrange("p (b n) -> p b n", b=B)
        QX = [shared[:, o + 512 * j:o + 512 * (j + 1)].bitcast(BF16) for j in range(UNROLL)]
        KX = [shared[:, o + 2048 + 512 * j:o + 2048 + 512 * (j + 1)].bitcast(BF16) for j in range(UNROLL)]
        assert o + 4096 <= 3 * 4096
        w1 = shared[:, 0:4096].rearrange("p (k n) -> p k n", k=KD)
        w2 = shared[:, 4096:8192].rearrange("p (m n) -> p m n", m=2 * E)
        hid = shared[:, 8192:12288].rearrange("p (m n) -> p m n", m=MF)
        fifo = sb("fifo", [128, 2 * 2048])
        cq, co, sq, sk, sv = (fifo[:, 512 * j:512 * (j + 1)].rearrange("p (k n) -> p k n", k=KD) for j in range(5))
        fi = fifo[:, 0:2048].rearrange("p (k n) -> p k n", k=KD)
        fo = fifo[:, 2048:4096].rearrange("p (m n) -> p m n", m=MF)

        fcT = sb("fcT", [128, KD, F])
        projT = sb("projT", [128, MF, D])
        so, wq, wo = (sb(n, [128, KD, D]) for n in ("so", "wq", "wo"))
        routerT = sb("routerT", [128, KD, E])
        KB1 = sb("KB1", [128, B, H * SC1])
        VS0 = sb("VS0", [128, B, H, VW])
        VS1 = sb("VS1", [128, B, H, VW])
        VSW = sb("VSW", [128, H, 32])
        mask0 = sb("mask0", [128, B, SC], BF16)
        mask1 = sb("mask1", [128, QT_PER_HEAD, SC1], BF16)
        rows_a = sb("rows_a", [128, 4, D])
        rows = {n: rows_a[:, j, :] for j, n in enumerate(("co_b", "co_g", "co_be", "sv_b"))}
        rows |= {n: sb(n, [128, D])[:, :] for n in ("so_b", "so_g", "so_be", "fo_b", "fo_g", "fo_be", "bo")}
        TOKF, OB = rows_a[:, 0:2, :], rows_a[:, 2:4, :]
        cols = {n: sb(n, [128, m]) for n, m in (("cq_b", KD), ("sq_b", KD), ("sk_b", KD), ("bq", KD),
                                                ("ck_b", KD), ("bk", KD), ("fi_b", MF))}
        identf = sb("identf", [128, 128])
        identb = sb("identb", [128, 128], BF16)
        onesb = sb("onesb", [128, 128], BF16)
        blockmask = sb("blockmask", [128, 128 // DH])

        XN = sb("XN", [128, TB, D])
        RB = XN[:, BT:, :]
        TOK = sb("TOK", [128, 2, D])
        TOKM = sb("TOKM", [128, 2, D])
        HB = sb("HB", [128, 2, D])
        xT2 = sb("xT2", [128, 2, KD, N])
        xTb = sb("xTb", [128, KD, N])
        xTs = sb("xTs", [128, KD, N])
        QT = sb("QT", [128, KD, N])
        P = sb("P", [128, 2, H, KP])
        ck, cv, wk, wv = (P[:, j // 2].rearrange("p h k -> p (h k)")[:, 512 * (j % 2):512 * (j % 2) + 512]
                          .rearrange("p (k n) -> p k n", k=KD) for j in range(4))
        PTS = sb("PTS", [128, H, 128])
        OSB = sb("OSB", [128, 512])
        CA = sb("CA", [128, D])
        CAT = sb("CAT", [128, KD, 128])
        TOKS = PTS[:, :, :].rearrange("p h n -> p (h n)").rearrange("p (t d) -> p t d", d=D)
        RR = sb("RR", [128, 2, N])
        HM = sb("HM", [128, 4, N])
        VH = HM[:, 0, :].rearrange("p (r k d) -> p r k d", r=2, d=32)
        OH = HM[:, 1, 0:256].rearrange("p (r q d) -> p r q d", r=2, d=DH)
        small = sb("small", [128, 512])
        LR = 8
        mv = small[:, 448:464].rearrange("p (r s) -> p r s", r=LR)
        rstd = small[:, 464:472]
        ve = small[:, 472:480]
        minus_half = small[:, 16:17]
        stats = small[:, 20:26]
        rsum = small[:, 32:48]
        mx = small[:, 48:64]
        lg = small[:, 64:96]
        pr = small[:, 96:128].rearrange("p (t e) -> p t e", e=E)
        pw = small[:, 128:160].rearrange("p (t e) -> p t e", e=E)
        eq = small[:, 160:192].rearrange("p (t e) -> p t e", e=E)
        hot = small[:, 192:224].rearrange("p (t e) -> p t e", e=E)
        cw = small[:, 384:448].rearrange("p (t e) -> p t e", e=E)
        rank = small[:, 256:264]
        top = small[:, 264:288].rearrange("p (j t) -> p j t", t=BT)
        nm2 = small[:, 288:304]
        nm = small[:, 304:320].rearrange("p (r q) -> p r q", r=2)
        nres = small[:, 320:328]
        wscale = small[:, 328:352].rearrange("p (j m) -> p j m", j=3)
        gate = small[0:R, 352:353]
        ms = small[:, 360:384].bitcast(BF16).rearrange("p (r n) -> p r n", r=2)
        MT = sb("MT", [24, 128], BF16)
        ctxs = XN[0:SC, 0:B, :]
        ctxT = xT2[:, 0, :, 0:B * SC]
        kT = xTb[:, :, 0:B * SC]
        kT1 = xTb[:, :, B * SC:2 * B * SC]
        pkT = QT[:, :, 0:NP]
        masks = QT[0:3, 0, 256:256 + 2 * SC]
        mtmp = QT[0:3, 1, 256:256 + 2 * SC]
        mpiece = OSB[0:3, 0:B * SC].bitcast(BF16)[:, 0:2 * SC]
        maski = HM[:, 2:4, :].rearrange("p a n -> p (a n)")[:, 0:QT_PER_HEAD * SC].bitcast(I32)\
            .rearrange("p (q k) -> p q k", k=SC)
        vb0, vb1 = TOK[:, 0, :], TOK[:, 1, :]
        u_sb = HB[:, 0, 0:MF * R].rearrange("p (m r) -> p m r", r=R)
        fbT = HB[0:R, 1, 0:R]
        v_sb = CA[0:R, :]
        G_sb = CAT[0:R, :, :].rearrange("p k n -> p (k n)")
        uT = RB[0:R, :, :].rearrange("p t n -> p (t n)")
        tA = PTS[:, 0:2, :].rearrange("p h n -> p (h n)")
        wt = PTS[:, 2:10, :].rearrange("p h n -> p (h n)")

        SCR = ps("SCR", [128, 4, 512])
        TR = ps("TR", [128, 2, 512])
        OUT = ps("OUT", [128, 2, 512])
        SQ = [TR[:, 0, :], TR[:, 1, :], OUT[:, 0, :]]
        PV = OUT[:, 1, :]

        scratch = nc.dram_tensor("pieces", [2, 3, NH * DH, S], BF16)
        o_dram = nc.dram_tensor("self_out", [128, TB, NH * DH], F32)
        x1_dram = nc.dram_tensor("x1", [128, T, D], F32)
        mscratch = nc.dram_tensor("maxima", [2, 24, 128], BF16)

        d_ctx, d_kv, d_low, d_tern, d_const, d_x, d_aw, d_cw, d_mask, d_prefix, d_fifo, d_moe, d_m1, d_m2, \
            d_pieces, d_rb, d_o = (sem(n) for n in (
                "ctx_loaded", "small_kv_weights_loaded", "low_rank_loaded", "ternary_sources_loaded",
                "biases_loaded", "x_loaded", "part_a_weights_loaded", "part_c_weights_loaded", "masks_loaded",
                "prefix_loaded", "gelu_weights_loaded", "expert_weights_loaded",
                "maxima_to_dram", "maxima_to_rows", "pieces_stored", "residuals_loaded", "self_out_loaded"))
        order_a, order_c = schedule_a(), schedule_c()

        def count(group):
            return {part: sum(STEP[s[0]].get(group, 0) for s in order) for part, order in (("a", order_a), ("c", order_c))}

        tr_full = Signal(sem("tr_full"), setup=1 + 4 + 2 + 1 + MF + 4, **count("tr"))
        tr_done = Signal(sem("tr_done"), **tr_full.per)
        out_full = Signal(sem("out_full"), setup=4 + MF, **count("out"))
        out_done = Signal(sem("out_done"), **out_full.per)
        sc_full = Signal(sem("scores_full"), 1, **count("sc"))
        sc_done = Signal(sem("scores_done"), 1, **count("sc"))
        p_ready = Signal(sem("probs_ready"), **count("exp"))
        ln_stats = Signal(sem("ln_stats"), 1, **count("ln"))
        ln_rstd = Signal(sem("ln_rstd"), **count("ln"))
        tok_ready = Signal(sem("token_tile_ready"), **count("tok"))
        resid_ready = Signal(sem("residual_ready"), **count("res"))
        vsw_ready = Signal(sem("small_values_ready"), **count("vsw"))
        pc_ready = Signal(sem("pieces_ready"), 1, **count("pc"))
        gate_exp = Signal(sem("gate_exp"), **count("gate"))
        a_ready = Signal(sem("squared_ready"), 1, **count("act"))
        groups = {"tr": (tr_full, tr_done), "out": (out_full, out_done), "sc": (sc_full, sc_done), "exp": (p_ready,),
                  "ln": (ln_stats, ln_rstd), "tok": (tok_ready,), "res": (resid_ready,), "vsw": (vsw_ready,),
                  "pc": (pc_ready,), "gate": (gate_exp,), "act": (a_ready,)}
        d_x1, d_out, d_oh = ([sem(f"{n}_{r}") for r in range(2)] for n in ("x1_stored", "out_stored", "head_out_stored"))
        sq_per = 2 * QT_PER_HEAD + 2
        sq_full = Signal(sem("max_scores_full"), b0=2 * 2 * QT_PER_HEAD + 1,
                         b=UNROLL * sq_per, blast=UNROLL * sq_per - 2 * 2 * QT_PER_HEAD - 1)
        sq_done = Signal(sem("max_scores_done"), **sq_full.per)
        st_full = Signal(sem("t_scores_full"), 1, b=UNROLL * 16, blast=UNROLL * 16)
        st_done = Signal(sem("t_probs_ready"), 1, **st_full.per)
        pv_full = Signal(sem("head_out_full"), 1, b=UNROLL, blast=UNROLL)
        pv_done = Signal(sem("head_out_done"), 1, **pv_full.per)
        vh_ready = Signal(sem("head_values_ready"), b0=2, b=UNROLL, blast=UNROLL - 2)
        max_ready = Signal(sem("maxima_ready"), b0=2, b=UNROLL, blast=UNROLL - 2)
        m_split = Signal(sem("maxima_split"), **max_ready.per)
        c_ready = Signal(sem("constants_ready"), setup=6)
        carrier = sem("wait_carrier")
        s_dve, s_pool = sem("vector_step"), sem("gpsimd_step")
        wproj_scaled = Signal(sem("wproj_scaled"), setup=KD)
        mask1_ready = Signal(sem("mask1_ready"), setup=1)
        setup_done = Signal(sem("setup_done"), setup=1)
        d_head = [sem(f"head_loaded_{j}") for j in range(UNROLL)]

        def r4(ap):
            return ap.rearrange("(k p) n -> p k n", p=128)

        def col(ap):
            return ap.rearrange("(k p) -> p k", p=128)

        def row(ap, parts=128):
            return ap.rearrange("(o n) -> o n", o=1).to_broadcast([parts, ap.shape[0]])

        def carry_wait(eng):
            eng.sem_inc(carrier, 1)

        def sq_events(j, kt, last):
            n = 0
            for jj in range(UNROLL):
                for s in range(QT_PER_HEAD):
                    if (jj, s) == (j, kt):
                        return n
                    n += 0 if last and jj >= 2 else 2
                    n += 1 if s == 1 and jj >= 1 else 0
                    n += 1 if s == 2 and not (last and jj == UNROLL - 1) else 0
            return n

        def sq_value(tl, events):
            return Tally(tl.part, tl.i).next(sq_done, events)

        block = ctx.enter_context(nc.Block())

        @block.sync
        def _(sp):
            with nc.allow_non_contiguous_dma(reason="biases and small transposed loads"):
                sp.dma_start(ctxs, A["ctx_1024"].rearrange("b s d -> s b d")).then_inc(d_ctx, 16)
                for dst, n in ((ck, "L0_xattn_ck_w"), (cv, "L0_xattn_cv_w"), (wk, "L1_xattn_Wk"), (wv, "L1_xattn_Wv")):
                    sp.dma_start(dst, r4(A[n])).then_inc(d_kv, 16)
                for dst, n in ((cols["ck_b"], "L0_xattn_ck_b"), (cols["bk"], "L1_xattn_bk")):
                    sp.dma_start(dst[:, :], col(A[n])).then_inc(d_kv, 16)
                for dst, n in ((vb0, "L0_xattn_cv_b"), (vb1, "L1_xattn_bv")):
                    sp.dma_start(dst, row(A[n])).then_inc(d_kv, 16)
                for h in range(H):
                    sp.dma_start(pkT[h % 8 * DH:(h % 8 + 1) * DH, h // 8, :],
                                 A["L1_xattn_prefix_k"][h].rearrange("p d -> d p")).then_inc(d_prefix, 16)
                sp.dma_start(u_sb, A["L1_ffn_u"].rearrange("(m p) r -> p m r", p=128)).then_inc(d_low, 16)
                sp.dma_start(fbT, A["L1_ffn_fast_b"].rearrange("a b -> b a")).then_inc(d_low, 16)
                sp.dma_start(v_sb, A["L1_ffn_v"]).then_inc(d_low, 16)
                sp.dma_start(gate, row(A["L1_ffn_gate"], R)).then_inc(d_low, 16)
                sp.dma_start(wfc_raw, A["L1_ffn_w_fc"].rearrange("(m p) d -> p m d", p=128)).then_inc(d_tern, 16)
                sp.dma_start(wproj_raw, A["L1_ffn_w_proj"].rearrange("(m p) d -> p m d", p=128)).then_inc(d_tern, 16)
                m0 = A["mask_Bx1x1xS2_ff0"].rearrange("b x y k -> (x y) (b k)")
                sp.dma_start(masks, m0.to_broadcast([3, B * SC])).then_inc(d_mask, 16)
                sp.dma_start(maski, A["mask_1x1xSxS2_ik0"].rearrange("x y (q p) k -> p (x y q) k", p=128))\
                    .then_inc(d_mask, 16)
                for dst, n in ((cq, "cq_w"), (co, "co_w"), (sq, "sq_w"), (sk, "sk_w"), (sv, "sv_w")):
                    sp.dma_start(dst, r4(A["L0_xattn_" + n])).then_inc(d_aw, 16)
                for n, dst in rows.items():
                    sp.dma_start(dst[:, :], row(A["L1_xattn_bo" if n == "bo" else "L0_xattn_" + n])).then_inc(d_const, 16)
                for n in ("cq_b", "sq_b", "sk_b", "bq", "fi_b"):
                    sp.dma_start(cols[n][:, :], col(A["L1_xattn_bq" if n == "bq" else "L0_xattn_" + n])).then_inc(d_const, 16)
                for dst, n in ((so, "L0_xattn_so_w"), (wq, "L1_xattn_Wq"), (wo, "L1_xattn_Wo")):
                    sp.dma_start(dst[:, :, :], r4(A[n])).then_inc(d_cw, 16)
                for k in range(KD):
                    sp.dma_start(routerT[:, k, :], A["L0_ffn_router_w"][:, k * 128:(k + 1) * 128]
                                 .rearrange("e p -> p e")).then_inc(d_cw, 16)
                sp.wait_ge(c_ready.sem, c_ready.total)
                for b in range(B):
                    sp.dma_start(VS1[SC:SC1, b, :, 0:DH], A["L1_xattn_prefix_v"].rearrange("h p d -> p h d"))\
                        .then_inc(d_prefix, 16)

                x_tiles = A["x"].rearrange("b (t p) d -> p (b t) d", p=128)
                sp.wait_ge(out_done.sem, 4 + MF)
                sp.dma_start(X[:, 0:MF, :], x_tiles[:, 0:MF, :]).then_inc(d_x, 16)
                sp.wait_ge(wproj_scaled.sem, KD)
                sp.dma_start(X[:, MF:, :], x_tiles[:, MF:, :]).then_inc(d_x, 16)

                with sp.Fori(0, B) as b:
                    tl = Tally("a", b)

                    def store_x1(t):
                        sp.wait_ge(tok_ready.sem, tl.after(tok_ready, "PN", t))
                        sp.dma_start(x1_dram[:, b * TB + t, :], TOK[:, t % 2, :]).then_inc(d_x1[t % 2], 16)

                    def store_pieces(k):
                        for e in range(2 * KD):
                            sp.wait_ge(pc_ready.sem, tl.next(pc_ready))
                            dst = scratch[e // 2, :, :, :].rearrange("c r s -> r c s")[
                                bass.ds(b * D + (e % 2) * 128, 128), :, k * N:(k + 1) * N]
                            sp.dma_start(dst, PC[:, e]).then_inc(d_pieces, 16)

                    tl.walk(order_a, groups, {"PN": store_x1, "QK": store_pieces})
                sp.wait_ge(d_pieces, DC + 16 * 4 * B * BLOCKS)
                for r in range(2):
                    sp.wait_ge(d_x1[r], DC + 16 * T // 2)
                sp.wait_ge(out_done.sem, out_done.base["b0"])
                sp.dma_start(fi, r4(A["L0_xattn_fi_w"])).then_inc(d_fifo, 16)
                sp.dma_start(fo, A["L0_xattn_fo_w"].rearrange("(m p) n -> p m n", p=128)).then_inc(d_fifo, 16)

                def load_head(n, j):
                    src = scratch[:, :, bass.ds(n * DH, DH), :]
                    for c, r, m in ((0, 0, 3), (1, 3, 2), (2, 5, 1)):
                        for k in range(m):
                            sp.dma_start(QX[j][(r + k) * DH:(r + k + 1) * DH, :], src[0, c]).then_inc(d_head[j], 16)
                            sp.dma_start(KX[j][(r + k) * DH:(r + k + 1) * DH, :], src[1, k]).then_inc(d_head[j], 16)

                def store_output(tl, n, r, events):
                    sp.wait_ge(sq_done.sem, sq_value(tl, events))
                    carry_wait(sp)
                    sp.dma_start(o_dram[:, :, bass.ds(n * DH, DH)], OH[:, r, :, :]).then_inc(d_oh[r], 16)

                def store_maxima(events, j):
                    sp.wait_ge(sq_done.sem, events)
                    sp.dma_start(mscratch[j % 2], MT[:, :]).then_inc(d_m1, 16)
                    return mscratch[j % 2].rearrange("(c q) t -> c (q t)", c=3)

                for j in range(3):
                    load_head(j, j)
                src = store_maxima(sq_done.base["b0"] + 4 * QT_PER_HEAD + 1, 0)
                sp.wait_ge(d_m1, 16)
                sp.dma_start(QX[0][QROWS:QROWS + 3, :], src).then_inc(d_m2, 16)

                def head(tl, i, j, last):
                    n = i * UNROLL + j
                    if not (last and j >= 1):
                        sp.wait_ge(pv_full.sem, tl.value(pv_full))
                        load_head(n + 3, (j + 3) % UNROLL)
                    tl.next(pv_full)
                    if j >= 1:
                        store_output(tl, n - 1, (j - 1) % 2, sq_events(j, 2, last))
                    if not (last and j == UNROLL - 1):
                        src = store_maxima(sq_value(tl, sq_events(j, 3, last)), (j + 1) % UNROLL)
                        sp.wait_ge(d_m1, 16 + 16 * (n + 1))
                        sp.dma_start(QX[(j + 1) % UNROLL][QROWS:QROWS + 3, :], src).then_inc(d_m2, 16)
                    if j == UNROLL - 1:
                        store_output(tl, n, j % 2, sq_done.per[tl.part])

                with sp.Fori(0, NH // UNROLL - 1) as i:
                    tl = Tally("b", i)
                    for j in range(UNROLL):
                        head(tl, i, j, False)
                tl = Tally("blast")
                for j in range(UNROLL):
                    head(tl, NH // UNROLL - 1, j, True)

                sp.wait_ge(pv_full.sem, pv_full.total)
                for k in range(KD):
                    sp.dma_start(w1[:, k, :], A["L0_ffn_w1"][k * 128:(k + 1) * 128, :]).then_inc(d_moe, 16)
                for m in range(2):
                    sp.dma_start(w2[:, m * E:(m + 1) * E, :],
                                 A["L0_ffn_w2"][m * 1024:(m + 1) * 1024, :].rearrange("(m p) n -> p m n", p=128))\
                        .then_inc(d_moe, 16)
                for r in range(2):
                    sp.wait_ge(d_oh[r], DC + 16 * NH // 2)
                with sp.Fori(0, B) as b:
                    tl = Tally("c", b)
                    sp.wait_ge(tr_done.sem, tl.value(tr_done))
                    carry_wait(sp)
                    sp.dma_start(TOKS, o_dram[:, :, bass.ds(b * D, D)]).then_inc(d_o, 16)

                    def load_residuals(k):
                        sp.wait_ge(out_done.sem, tl.value(out_done) if k == 0 else tl.after(out_done, "SO", BT * k - 1))
                        carry_wait(sp)
                        sp.dma_start(RB, x1_dram[:, bass.ds(b * TB + k * BT, BT), :]).then_inc(d_rb, 16)

                    def store_out(t):
                        sp.wait_ge(out_done.sem, tl.after(out_done, "FP", t))
                        sp.dma_start(out[b, t * 128:(t + 1) * 128, :], OB[:, t % 2, :]).then_inc(d_out[t % 2], 16)

                    tl.walk(order_c, groups, {"LD": load_residuals, "FP": store_out})
                for r in range(2):
                    sp.wait_ge(d_out[r], DC + 16 * T // 2)

        @block.tensor
        def _(pe):
            def tr_bank(tl):
                bank = tl.slot(tr_full, 2)
                tl.next(tr_full)
                v = tl.back(tr_full, 2)
                pe.wait_ge(tr_done.sem, v)
                return TR[:, bank, :]

            def out_bank(tl):
                bank = tl.slot(out_full, 2)
                tl.next(out_full)
                v = tl.back(out_full, 2)
                pe.wait_ge(out_done.sem, v)
                return OUT[:, bank, :]

            def evacuated(tl):
                pe.wait_ge(tr_done.sem, tl.value(tr_full))

            def product(dst, pairs):
                for n, (l, r) in enumerate(pairs):
                    ins = nc.tensor.matmul(dst, l, r, start=(n == 0), stop=(n == len(pairs) - 1))
                return ins

            def transposes(dst, srcs, ident=identf, width=128):
                for n, s in enumerate(srcs):
                    m, p = s.shape[1], s.shape[0]
                    ins = nc.tensor.transpose(dst[0:m, n * width:n * width + p], s, ident[0:p, 0:p])
                return ins

            tl = Tally("setup")
            pe.wait_ge(c_ready.sem, c_ready.total)
            pe.wait_ge(d_ctx, 16)
            bank = tr_bank(tl)
            transposes(bank, [ctxs[:, b, k * 128:(k + 1) * 128] for b in range(B) for k in range(KD)], width=SC)\
                .then_inc(tr_full.sem, 1)
            evacuated(tl)
            pe.wait_ge(d_kv, 16 * 8)
            for w in (ck, wk):
                for m in range(KD):
                    bank = tr_bank(tl)
                    product(bank[:, 0:B * SC], [(w[:, k, m * 128:(m + 1) * 128], ctxT[:, k, :]) for k in range(KD)])\
                        .then_inc(tr_full.sem, 1)
            for w in (cv, wv):
                for b in range(B):
                    bank = out_bank(tl)
                    product(bank[0:SC, 0:D], [(ctxT[:, k, b * SC:(b + 1) * SC], w[:, k, :]) for k in range(KD)])\
                        .then_inc(out_full.sem, 1)
            pe.wait_ge(d_low, 16 * 4)
            for hf in range(2):
                bank = tr_bank(tl)
                transposes(bank, [u_sb[:, 4 * hf + m, :] for m in range(4)]).then_inc(tr_full.sem, 1)
            bank = tr_bank(tl)
            product(bank[0:R, 0:D], [(fbT, v_sb)]).then_inc(tr_full.sem, 1)
            evacuated(tl)
            for m in range(MF):
                bank = out_bank(tl)
                product(bank[:, 0:D], [(uT[:, m * 128:(m + 1) * 128], G_sb)]).then_inc(out_full.sem, 1)
                pe.wait_ge(out_done.sem, tl.value(out_full))
                bank = tr_bank(tl)
                transposes(bank, [tA[:, k * 128:(k + 1) * 128] for k in range(KD)]).then_inc(tr_full.sem, 1)
            for m in range(KD):
                pe.wait_ge(wproj_scaled.sem, m + 1)
                for hf in range(2):
                    bank = tr_bank(tl)
                    transposes(bank, [wt[:, (4 * hf + c) * 128:(4 * hf + c + 1) * 128] for c in range(4)])\
                        .then_inc(tr_full.sem, 1)
            tl.close(tr_full, out_full)

            class Steps:

                def __init__(self, tl, b):
                    self.tl, self.b = tl, b

                def copied(self, *step):
                    pe.wait_ge(tr_done.sem, self.tl.after(tr_done, *step))

                def block_copied(self, name, k):
                    pe.wait_ge(tr_done.sem, self.tl.after_block(tr_done, name, k))

                def transposed(self, src, behind):
                    pe.wait_ge(tok_ready.sem, self.tl.after(tok_ready, *behind))
                    bank = tr_bank(self.tl)
                    transposes(bank, [src[:, k * 128:(k + 1) * 128] for k in range(KD)]).then_inc(tr_full.sem, 1)

                def feature_major(self, w, src, m):
                    bank = tr_bank(self.tl)
                    product(bank, [(w[:, k, m * 128:(m + 1) * 128], src[:, k, :]) for k in range(KD)])\
                        .then_inc(tr_full.sem, 1)

                def token_major(self, src, w, t, ks):
                    bank = out_bank(self.tl)
                    c = t % BT * 128
                    product(bank[:, 0:D], [(src[:, k, c:c + 128], w[:, k, :]) for k in ks]).then_inc(out_full.sem, 1)

                def attention(self, keys, nk, project):
                    tl, b = self.tl, self.b

                    def scores(t):
                        if t % BT == 0:
                            self.copied("QP", t // BT)
                        pe.wait_ge(sc_done.sem, tl.value(sc_done))
                        w = CHUNK_HEADS * nk
                        c0 = t % BT * 128
                        for c in range(NCH):
                            k = c * CHUNK_HEADS // 8
                            nc.tensor.matmul(SCR[:, c, 0:w], QT[:, k, c0:c0 + 128],
                                             keys[:, b, c * w:(c + 1) * w], start=True, stop=False)
                            if nk == SC:
                                l, m = onesb[:, :], mask0[:, b, :]
                            else:
                                l, m = identb[:, :], mask1[:, t, :]
                            ins = nc.tensor.matmul(SCR[:, c, 0:w].rearrange("p (h k) -> p h k", k=nk), l,
                                                   m.unsqueeze(1).to_broadcast([128, CHUNK_HEADS, nk]),
                                                   start=False, stop=True)
                        ins.then_inc(sc_full.sem, 1)

                    def prob_transposes(t):
                        pe.wait_ge(p_ready.sem, tl.after(p_ready, "E", t))
                        for g in range(4):
                            bank = tr_bank(tl)
                            transposes(bank, [P[:, t % 2, 4 * g + hh, :] for hh in range(4)]).then_inc(tr_full.sem, 1)

                    def values(t):
                        self.copied("T", t)
                        if t == 0:
                            pe.wait_ge(vsw_ready.sem, tl.after(vsw_ready, "VW"))
                        bank = tr_bank(tl)
                        for h in range(H):
                            g, c = h % 4, h // 4
                            ins = nc.tensor.matmul(bank[32 * g:32 * g + 32, c * 128:(c + 1) * 128], VSW[0:KP, h, :],
                                                   PTS[0:KP, h, :], start=True, stop=True)
                        ins.then_inc(tr_full.sem, 1)

                    def out_transposes(t):
                        self.copied("PV", t)
                        bank = out_bank(tl)
                        transposes(bank, [OSB[:, c * 128:(c + 1) * 128] for c in range(4)]).then_inc(out_full.sem, 1)

                    def ca_transposes(t):
                        pe.wait_ge(out_done.sem, tl.after(out_done, "OT", t))
                        bank = tr_bank(tl)
                        transposes(bank, [CA[:, k * 128:(k + 1) * 128] for k in range(KD)]).then_inc(tr_full.sem, 1)

                    def projected(t):
                        self.copied("CT", t)
                        bank = out_bank(tl)
                        product(bank[:, 0:D], [(CAT[:, k, :], project[:, k, :]) for k in range(KD)])\
                            .then_inc(out_full.sem, 1)

                    return {"S": scores, "T": prob_transposes, "PV": values, "OT": out_transposes,
                            "CT": ca_transposes, "PJ": projected,
                            "LT": lambda t: self.transposed(TOK[:, t % 2, :], ("PN", t))}

            pe.wait_ge(setup_done.sem, 1)
            pe.wait_ge(d_aw, 16 * 5)
            with pe.Fori(0, B) as b:
                tl = Tally("a", b)
                at = Steps(tl, b)

                def queries(k):
                    at.block_copied("LN0", k)
                    for m in range(KD):
                        at.feature_major(cq, xT2[:, k], m)

                def self_qk(k):
                    at.block_copied("LT", k)
                    for w in (sq, sk):
                        for m in range(KD):
                            at.feature_major(w, xTb, m)

                def self_values(t):
                    at.copied("LT", t)
                    at.token_major(xTb, sv, t, range(KD))

                tl.walk(order_a, groups, at.attention(KB0, SC, co) | {
                    "LN0": lambda t: at.transposed(XN[:, t, :], ("LN0", t)),
                    "QP": queries, "QK": self_qk, "SV": self_values})

            def sq_bank(tl):
                bank = tl.slot(sq_full, 3)
                tl.next(sq_full)
                v = tl.back(sq_full, 3)
                pe.wait_ge(sq_done.sem, v)
                return SQ[bank]

            def max_scores(tl, j, kt):
                for hf in range(2):
                    bank = sq_bank(tl)
                    nc.tensor.matmul(bank, QX[j][0:QROWS, kt * 128:(kt + 1) * 128],
                                     KX[j][0:QROWS, hf * 512:(hf + 1) * 512], start=True, stop=True)\
                        .then_inc(sq_full.sem, 1)

            def maxima_transpose(tl, r, heads):
                pe.wait_ge(m_split.sem, heads)
                bank = sq_bank(tl)
                nc.tensor.transpose(bank.bitcast(BF16)[0:24, 0:128], ms[:, r, :], identb[:, :])\
                    .then_inc(sq_full.sem, 1)

            def head_out_transposes(tl):
                pe.wait_ge(pv_done.sem, tl.value(pv_full))
                bank = sq_bank(tl)
                transposes(bank, [OSB[:, s * 128:(s + 1) * 128] for s in range(2)]).then_inc(sq_full.sem, 1)

            tl = Tally("b0")
            pe.wait_ge(tr_done.sem, tr_done.base["b0"])
            pe.wait_ge(out_done.sem, out_done.base["b0"])
            pe.wait_ge(sc_done.sem, sc_done.base["b0"])
            for j in range(2):
                pe.wait_ge(d_head[j], 16 * 12)
                for kt in range(QT_PER_HEAD):
                    max_scores(tl, j, kt)
            maxima_transpose(tl, 0, 1)
            tl.close(sq_full)

            def head(tl, i, j, last):
                n = i * UNROLL + j

                def t_scores(kt):
                    for hf in range(2):
                        bank = tl.slot(st_full, 4)
                        tl.next(st_full)
                        pe.wait_ge(st_done.sem, tl.back(st_full, 4))
                        nc.tensor.matmul(SCR[:, bank, :], KX[j][0:QROWS + 3, kt * 128:(kt + 1) * 128],
                                         QX[j][0:QROWS + 3, hf * 512:(hf + 1) * 512], start=True, stop=True)\
                            .then_inc(st_full.sem, 1)

                def values(kt, ahead):
                    pe.wait_ge(st_done.sem, tl.back(st_full, ahead))
                    if kt == 0:
                        pe.wait_ge(pv_done.sem, tl.value(pv_full))
                        pe.wait_ge(vh_ready.sem, (n + 1))
                    for g in range(4):
                        ins = nc.tensor.matmul(PV[32 * g:32 * g + 32, 0:256], VH[:, j % 2, kt, :],
                                               PTB[:, kt % 2, g * 256:(g + 1) * 256], start=(kt == 0),
                                               stop=(kt == QT_PER_HEAD - 1))
                    if kt == QT_PER_HEAD - 1:
                        ins.then_inc(pv_full.sem, 1)
                        tl.next(pv_full)

                for kt in range(QT_PER_HEAD):
                    if not (last and j >= 2):
                        if kt == 0:
                            pe.wait_ge(d_head[(j + 2) % UNROLL], (i + (1 + (j + 2) // UNROLL)) * (16 * 12))
                        max_scores(tl, (j + 2) % UNROLL, kt)
                    if kt == 0:
                        pe.wait_ge(d_m2, (n + 1) * 16)
                    t_scores(kt)
                    if kt > 0:
                        values(kt - 1, 2)
                    if kt == 1 and j >= 1:
                        head_out_transposes(tl)
                    if kt == 2 and not (last and j == UNROLL - 1):
                        maxima_transpose(tl, (j + 1) % 2, n + 2)
                values(QT_PER_HEAD - 1, 0)
                if j == UNROLL - 1:
                    head_out_transposes(tl)

            with pe.Fori(0, NH // UNROLL - 1) as i:
                tl = Tally("b", i)
                for j in range(UNROLL):
                    head(tl, i, j, False)
                tl.close(sq_full, st_full, pv_full)
            tl = Tally("blast")
            for j in range(UNROLL):
                head(tl, NH // UNROLL - 1, j, True)
            tl.close(sq_full, st_full, pv_full)

            pe.wait_ge(sq_done.sem, sq_done.total)
            pe.wait_ge(st_done.sem, st_done.total)
            pe.wait_ge(pv_done.sem, pv_done.total)
            pe.wait_ge(d_cw, 16 * 5)
            pe.wait_ge(d_fifo, 16 * 2)
            with pe.Fori(0, B) as b:
                tl = Tally("c", b)
                at = Steps(tl, b)

                def self_output_transposes(t):
                    pe.wait_ge(d_o, b * 16 + 16)
                    bank = tr_bank(tl)
                    transposes(bank, [TOKS[:, t, k * 128:(k + 1) * 128] for k in range(KD)]).then_inc(tr_full.sem, 1)

                def self_projection(t):
                    at.copied("ST", t)
                    at.token_major(xTs, so, t, range(KD))

                def gelu_up(k):
                    at.block_copied("LX", k)
                    for m in range(MF):
                        at.feature_major(fi, xTb, m)

                def gelu_down(t):
                    at.copied("FI", t // BT)
                    at.token_major(hid, fo, t, range(MF))

                def router(k):
                    at.block_copied("L2", k)
                    for hf in range(2):
                        bank = out_bank(tl)
                        for c in range(2):
                            t = 2 * hf + c
                            ins = product(bank[:, c * E:(c + 1) * E],
                                          [(xT2[:, k, f, t * 128:(t + 1) * 128], routerT[:, f, :]) for f in range(KD)])
                        ins.then_inc(out_full.sem, 1)

                def expert_up(k, e):
                    if e == 0:
                        pe.wait_ge(d_moe, 16 * 4)
                        at.block_copied("L2", k)
                    for m in range(2):
                        at.feature_major(w1, xT2[:, k], 2 * e + m)

                def expert_down(k, e, t):
                    pe.wait_ge(a_ready.sem, tl.after(a_ready, "UP", k, e))
                    c = t % BT * 128
                    bank = out_bank(tl)
                    product(bank[:, 0:D], [(HM[:, (e % 2) * 2 + m, c:c + 128], w2[:, 2 * e + m, :]) for m in range(2)])\
                        .then_inc(out_full.sem, 1)

                def queries(k):
                    at.block_copied("L3", k)
                    for m in range(KD):
                        at.feature_major(wq, xTb, m)

                def ternary_up(k):
                    at.block_copied("LT", k)
                    for m in range(MF):
                        at.feature_major(fcT, xTs, m)

                def ternary_down(t):
                    pe.wait_ge(a_ready.sem, tl.after(a_ready, "FC", t // BT))
                    at.token_major(hid, projT, t, range(MF))

                tl.walk(order_c, groups, at.attention(KB1, SC1, wo) | {
                    "ST": self_output_transposes, "SO": self_projection,
                    "LX": lambda t: at.transposed(XN[:, t % BT, :], ("SN", t)),
                    "FI": gelu_up, "FO": gelu_down,
                    "L2": lambda t: at.transposed(TOKF[:, t % 2, :], ("FM", t)),
                    "RT": router, "UP": expert_up, "DN": expert_down, "DL": expert_down,
                    "L3": lambda t: at.transposed(TOKM[:, t % 2, :], ("DM", t)),
                    "QP": queries, "FC": ternary_up, "FP": ternary_down})

        @block.scalar
        def _(act):
            def emptied(tl):
                bank = tl.slot(tr_full, 2)
                act.wait_ge(tr_full.sem, tl.next(tr_full))
                return TR[:, bank, :]

            tl = Tally("setup")
            bank = emptied(tl)
            nc.scalar.activation(ctxT.rearrange("p k (b n) -> p b k n", b=B),
                                 bank[:, 0:B * KD * SC].rearrange("p (b k n) -> p b k n", b=B, k=KD), ACT.Copy)\
                .then_inc(tr_done.sem, 1)
            for dst, bias in ((kT, cols["ck_b"]), (kT1, cols["bk"])):
                for m in range(KD):
                    bank = emptied(tl)
                    if m == 0:
                        act.wait_ge(d_kv, 16 * 8)
                    nc.scalar.activation(dst[:, m, :], bank[:, 0:B * SC], ACT.Identity, bias=bias[:, m:m + 1])\
                        .then_inc(tr_done.sem, 1)
            for hf in range(2):
                bank = emptied(tl)
                nc.scalar.activation(uT[:, hf * 512:(hf + 1) * 512], bank[0:R, :], ACT.Copy).then_inc(tr_done.sem, 1)
            bank = emptied(tl)
            act.wait_ge(d_low, 16 * 4)
            nc.scalar.activation(G_sb, bank[0:R, 0:D], ACT.Identity, scale=gate).then_inc(tr_done.sem, 1)
            for m in range(MF):
                bank = emptied(tl)
                nc.scalar.activation(fcT[:, :, m * 128:(m + 1) * 128],
                                     bank[:, 0:256].rearrange("p (k n) -> p k n", k=KD), ACT.Copy)\
                    .then_inc(tr_done.sem, 1)
            for m in range(KD):
                for hf in range(2):
                    bank = emptied(tl)
                    nc.scalar.activation(projT[:, 4 * hf:4 * hf + 4, m * 128:(m + 1) * 128],
                                         bank.rearrange("p (c n) -> p c n", c=4), ACT.Copy).then_inc(tr_done.sem, 1)

            def copy_transposed(tl, dst, t):
                bank = emptied(tl)
                c = t % BT * 128
                nc.scalar.activation(dst[:, :, c:c + 128],
                                     bank[:, 0:256].rearrange("p (k n) -> p k n", k=KD), ACT.Copy)\
                    .then_inc(tr_done.sem, 1)

            def attention(tl, nk, bias, dst):
                def queries(k):
                    for m in range(KD):
                        bank = emptied(tl)
                        nc.scalar.activation(QT[:, m, :], bank, ACT.Identity, bias=bias[:, m:m + 1])\
                            .then_inc(tr_done.sem, 1)

                def exps(t):
                    act.wait_ge(sc_done.sem, tl.after(sc_done, "S", t))
                    v = P[:, t % 2, :, 0:nk]
                    nc.scalar.activation(v, v, ACT.Exp, scale=DH ** -0.5).then_inc(p_ready.sem, 1)

                def prob_transposes(t):
                    for g in range(4):
                        bank = emptied(tl)
                        nc.scalar.activation(PTS[0:KP, 4 * g:4 * g + 4, :],
                                             bank[0:KP].rearrange("p (h n) -> p h n", h=4), ACT.Copy)\
                            .then_inc(tr_done.sem, 1)

                def values(t):
                    bank = emptied(tl)
                    nc.scalar.activation(OSB[:, :], bank, ACT.Copy).then_inc(tr_done.sem, 1)

                return {"QP": queries, "E": exps, "T": prob_transposes, "PV": values,
                        "CT": lambda t: copy_transposed(tl, CAT, 0), "LT": lambda t: copy_transposed(tl, dst, t)}

            act.wait_ge(d_const, 16 * 16)
            with act.Fori(0, B) as b:
                tl = Tally("a", b)

                def self_qk(k):
                    act.wait_ge(d_pieces, b * (BLOCKS * 4 * 16) + (k * 4 * 16 + DC))
                    for e in range(2 * KD):
                        bank = emptied(tl)
                        bias = cols["sq_b" if e < KD else "sk_b"][:, e % KD:e % KD + 1]
                        act.wait_ge(pc_ready.sem, tl.back(pc_ready, 1))
                        tl.next(pc_ready)
                        nc.scalar.activation(PC[:, e, 0, :], bank, ACT.Identity, bias=bias)
                        nc.scalar.activation(RR[:, e % 2, :], bank, ACT.Identity, bias=bias).then_inc(tr_done.sem, 1)

                tl.walk(order_a, groups, attention(tl, SC, cols["cq_b"], xTb) | {
                    "LN0": lambda t: copy_transposed(tl, xT2[:, t // BT], t), "QK": self_qk})

            def head(tl, j):
                for kt in range(QT_PER_HEAD):
                    for hf in range(2):
                        bank = tl.slot(st_full, 4)
                        act.wait_ge(st_full.sem, tl.next(st_full))
                        nc.scalar.activation(PTB[:, kt % 2, hf * 512:(hf + 1) * 512], SCR[:, bank, :], ACT.Exp,
                                             scale=DH ** -0.5).then_inc(st_done.sem, 1)
                act.wait_ge(pv_full.sem, tl.next(pv_full))
                nc.scalar.activation(OSB[:, 0:256], PV[:, 0:256], ACT.Copy).then_inc(pv_done.sem, 1)

            act.wait_ge(d_pieces, DC + 16 * 4 * B * BLOCKS)
            with act.Fori(0, NH // UNROLL - 1) as i:
                tl = Tally("b", i)
                for j in range(UNROLL):
                    head(tl, j)
            tl = Tally("blast")
            for j in range(UNROLL):
                head(tl, j)

            with act.Fori(0, B) as b:
                tl = Tally("c", b)

                def gelu_up(k):
                    for m in range(MF):
                        bank = emptied(tl)
                        nc.scalar.activation(hid[:, m, :], bank, ACT.Gelu, bias=cols["fi_b"][:, m:m + 1])\
                            .then_inc(tr_done.sem, 1)

                def router(k):
                    act.wait_ge(out_done.sem, tl.after(out_done, "RT", k))
                    nc.scalar.activation(pr.rearrange("p t e -> p (t e)"), lg, ACT.Exp, scale=-1.0)\
                        .then_inc(gate_exp.sem, 1)

                def relus(count):
                    for _ in range(count):
                        bank = emptied(tl)
                        act.wait_ge(a_ready.sem, tl.back(a_ready, 1))
                        nc.scalar.activation(RR[:, tl.slot(a_ready, 2), :], bank, ACT.Relu).then_inc(tr_done.sem, 1)
                        tl.next(a_ready)

                tl.walk(order_c, groups, attention(tl, SC1, cols["bq"], xTs) | {
                    "ST": lambda t: copy_transposed(tl, xTs, t), "LX": lambda t: copy_transposed(tl, xTb, t),
                    "FI": gelu_up, "L2": lambda t: copy_transposed(tl, xT2[:, t // BT], t), "RT": router,
                    "UP": lambda k, e: relus(2), "L3": lambda t: copy_transposed(tl, xTb, t),
                    "FC": lambda k: relus(MF)})

        @block.vector
        def _(dve):
            steps = [0]

            def link(ins):
                steps[0] += 1
                ins.then_inc(s_dve, 1)
                dve.wait_ge(s_dve, steps[0])

            class Chain:
                def __init__(self, i, per):
                    self.i, self.per, self.n, self.at = i, per, 0, steps[0]

                def __call__(self, ins):
                    self.n += 1
                    ins.then_inc(s_dve, 1)
                    dve.wait_ge(s_dve, self.i * self.per + (self.at + self.n))
                    carry_wait(dve)

                def close(self, trips):
                    assert self.n == self.per, self.n
                    steps[0] += self.per * trips

            tl = Tally("setup")
            dve.wait_ge(c_ready.sem, c_ready.total)
            dve.wait_ge(d_mask, 32)
            m0 = mask0[0:3].rearrange("p b k -> p (b k)")
            link(nc.vector.tensor_scalar(masks, masks, 4.0, -3.0e38, ALU.mult, ALU.max))
            for c in range(3):
                link(nc.vector.tensor_copy(mpiece, masks))
                if c == 0:
                    link(nc.vector.tensor_scalar(m0, mpiece, identf[0:3, 0:1], None, ALU.mult))
                else:
                    link(nc.vector.scalar_tensor_tensor(m0, mpiece, identf[0:3, c:c + 1], m0, ALU.mult, ALU.add))
                link(nc.vector.tensor_tensor(masks, masks, mpiece, ALU.subtract))
            nc.vector.tensor_scalar(mask1[:, :, 0:SC], maski, 0, 4.0 * -1.0e9, ALU.is_equal, ALU.mult)\
                .then_inc(mask1_ready.sem, 1)
            dve.wait_ge(tr_done.sem, tl.next(tr_done, 5))
            dve.wait_ge(d_prefix, 16 * KD * 8 + 32)
            kb1 = KB1[:, :, :].rearrange("p b (k h n) -> p b k h n", k=KD, n=SC1)
            kb0 = KB0.rearrange("p b (k h n) -> p b k h n", k=KD, n=SC)
            for hh in range(8):
                bm = blockmask[:, hh:hh + 1]
                for b in range(B):
                    nc.vector.tensor_scalar(kb0[:, b, :, hh, :], kT[:, :, b * SC:(b + 1) * SC], bm, None, ALU.mult)
                    nc.vector.tensor_scalar(kb1[:, b, :, hh, 0:SC], kT1[:, :, b * SC:(b + 1) * SC], bm, None, ALU.mult)
                    ins = nc.vector.tensor_scalar(kb1[:, b, :, hh, SC:SC1], pkT, bm, None, ALU.mult)
            link(ins)
            for vs, bias in ((VS0, vb0), (VS1, vb1)):
                for b in range(B):
                    bank = tl.slot(out_full, 2)
                    dve.wait_ge(out_full.sem, tl.next(out_full))
                    if b == 0:
                        dve.wait_ge(d_kv, 16 * 8)
                    nc.vector.tensor_tensor(vs[0:SC, b, :, 0:DH],
                                            OUT[0:SC, bank, 0:D].rearrange("p (h d) -> p h d", d=DH),
                                            bias[0:SC].rearrange("p (h d) -> p h d", d=DH), ALU.add)\
                        .then_inc(out_done.sem, 1)
            dve.wait_ge(d_tern, 32)

            def scales(raw, m, width):
                sc, hi, lo = wscale[:, 0, 0:m], wscale[:, 1, 0:m], wscale[:, 2, 0:m]
                link(nc.vector.tensor_reduce(sc, raw, AX, ALU.add, apply_absolute_value=True))
                link(nc.vector.tensor_scalar(sc, sc, 1.0 / width, 1e-5, ALU.mult, ALU.max))
                nc.vector.tensor_scalar(hi, sc, 0.5, None, ALU.mult)
                link(nc.vector.tensor_scalar(lo, sc, -0.5, None, ALU.mult))

            def ternary(dst, raw, m):
                link(nc.vector.tensor_scalar(dst, raw[:, m, :], wscale[:, 2, m:m + 1], None, ALU.is_lt))
                link(nc.vector.scalar_tensor_tensor(dst, raw[:, m, :], wscale[:, 1, m:m + 1], dst,
                                                    ALU.is_gt, ALU.subtract))

            scales(wfc_raw, MF, D)
            for m in range(MF):
                if m > 0:
                    dve.wait_ge(tr_full.sem, 8 + m)
                ternary(tA, wfc_raw, m)
                bank = tl.slot(out_full, 2)
                dve.wait_ge(out_full.sem, tl.next(out_full))
                nc.vector.scalar_tensor_tensor(tA, tA, wscale[:, 0, m:m + 1], OUT[:, bank, 0:D], ALU.mult, ALU.add)\
                    .then_inc(out_done.sem, 1)
            scales(wproj_raw, KD, F)
            for m in range(KD):
                if m > 0:
                    dve.wait_ge(tr_full.sem, 8 + MF + 2 * m)
                ternary(wt, wproj_raw, m)
                nc.vector.tensor_scalar(wt, wt, wscale[:, 0, m:m + 1], None, ALU.mult).then_inc(wproj_scaled.sem, 1)
            tl.close(out_full)
            dve.wait_ge(tr_done.sem, tr_done.base["a"])
            nc.vector.memset(P[:, :, :, SC:KP], 0.0)
            nc.vector.memset(VX[:, :, :, DH:VW], 1.0)
            nc.vector.memset(VSW[:, :, VW:32], 0.0)
            dve.wait_ge(d_x, 32)
            dve.wait_ge(d_const, 16 * 16)
            nc.vector.memset(VH[:, :, :, VW:32], 0.0).then_inc(setup_done.sem, 1)
            dve.wait_ge(setup_done.sem, 1)

            def moments(tl, chain, src):
                r = tl.slot(ln_stats, LR)
                dve.wait_ge(ln_stats.sem, tl.value(ln_stats))
                tl.next(ln_stats)
                carry_wait(dve)
                chain(nc.vector.bn_stats(stats, src))
                nc.vector.bn_aggr(mv[:, r, :], stats).then_inc(ln_stats.sem, 1)

            def normalised(tl, chain, behind, src, dst, affine=None):
                r = tl.slot_of(ln_stats, LR, *behind)
                dve.wait_ge(ln_rstd.sem, tl.after(ln_rstd, *behind))
                ins = nc.vector.tensor_scalar(dst, src, mv[:, r, 0:1], rstd[:, r:r + 1], ALU.subtract, ALU.mult)
                if affine:
                    chain(ins)
                    chain(nc.vector.tensor_tensor(dst, dst, rows[affine + "_g"], ALU.mult))
                    ins = nc.vector.tensor_tensor(dst, dst, rows[affine + "_be"], ALU.add)
                return ins

            def filled(tl):
                bank = tl.slot(out_full, 2)
                dve.wait_ge(out_full.sem, tl.next(out_full))
                return OUT[:, bank, :]

            def signal_out(tl, ins):
                ins.then_inc(out_done.sem, 1)
                dve.wait_ge(out_done.sem, tl.next(out_done))

            def links(order, **per_step):
                return sum(per_step.get(s[0], 0) for s in order)

            def left(tl, *step):
                dve.wait_ge(tr_done.sem, tl.after(tr_done, *step))

            def with_residual(tl, chain, t, dst, residual, behind):
                bank = filled(tl)
                dve.wait_ge(resid_ready.sem, tl.after(resid_ready, behind, t))
                signal_out(tl, nc.vector.tensor_tensor(dst, bank[:, 0:D], residual, ALU.add))
                moments(tl, chain, dst)

            def attention(tl, chain, nk):
                def scores(t):
                    dve.wait_ge(sc_full.sem, tl.next(sc_full))
                    v = SCR[:, :, 0:CHUNK_HEADS * nk].rearrange("p c (h k) -> p c h k", k=nk)
                    chain(nc.vector.tensor_reduce(mx, v, AX, ALU.max))
                    nc.vector.tensor_tensor(P[:, t % 2, :, 0:nk].rearrange("p (c h) k -> p c h k", c=NCH), v,
                                            mx.rearrange("p (c h) -> p c h", c=NCH).unsqueeze(3)
                                            .to_broadcast([128, NCH, CHUNK_HEADS, nk]), ALU.subtract)\
                        .then_inc(sc_done.sem, 1)

                def normalise(t):
                    bank = filled(tl).rearrange("p (h d) -> p h d", d=32)
                    chain(nc.vector.reciprocal(rsum, bank[:, :, DH]))
                    signal_out(tl, nc.vector.tensor_tensor(CA[:, :].rearrange("p (h d) -> p h d", d=DH),
                                                           bank[:, :, 0:DH],
                                                           rsum.unsqueeze(2).to_broadcast([128, H, DH]), ALU.mult))

                return {"S": scores, "OT": normalise}

            def pass_start(tl, small_values):
                dve.wait_ge(tr_done.sem, tl.value(tr_done))
                nc.vector.tensor_copy(VSW[0:KP, :, 0:VW], small_values).then_inc(vsw_ready.sem, 1)

            with dve.Fori(0, B) as b:
                tl = Tally("a", b)
                chain = Chain(b, links(order_a, LS=1, S=1, OT=1, PJ=1, PN=2, QK=2 * 2 * KD))

                def input_norm(t):
                    normalised(tl, chain, ("LS", t), X[:, b * TB + t, :], XN[:, t, :]).then_inc(tok_ready.sem, 1)

                def projected_norm(t):
                    dve.wait_ge(d_x1[t % 2], b * (TB // 2 * 16) + (t // 2 * 16 + DC))
                    if t >= 2:
                        left(tl, "LT", t - 2)
                    normalised(tl, chain, ("PJ", t), HB[:, t % 2, :], TOK[:, t % 2, :], affine="co")\
                        .then_inc(tok_ready.sem, 1)

                def pieces(k):
                    rest = HM[:, 2, :]
                    for e in range(2 * KD):
                        dve.wait_ge(tr_done.sem, tl.next(tr_done))
                        chain(nc.vector.tensor_tensor(rest, RR[:, e % 2, :], PC[:, e, 0, :], ALU.subtract))
                        chain(nc.vector.tensor_copy(PC[:, e, 1, :], rest))
                        nc.vector.tensor_tensor(PC[:, e, 2, :], rest, PC[:, e, 1, :], ALU.subtract)\
                            .then_inc(pc_ready.sem, 1)
                        dve.wait_ge(pc_ready.sem, tl.next(pc_ready))

                def self_values(t):
                    bank = filled(tl)
                    signal_out(tl, nc.vector.tensor_tensor(
                        VX[:, bass.ds(b * H, H), t, 0:DH], bank[:, 0:D].rearrange("p (h d) -> p h d", d=DH),
                        rows["sv_b"].rearrange("p (h d) -> p h d", d=DH), ALU.add))

                tl.walk(order_a, groups, attention(tl, chain, SC) | {
                    "VW": lambda: pass_start(tl, VS0[0:KP, b, :, :]), "LS": lambda t: moments(tl, chain, X[:, b * TB + t, :]), "LN0": input_norm,
                    "PJ": lambda t: with_residual(tl, chain, t, HB[:, t % 2, :], XN[:, t, :], "RA"),
                    "PN": projected_norm, "QK": pieces, "SV": self_values})
            chain.close(B)

            dve.wait_ge(sc_full.sem, sc_full.base["b0"])
            for j in range(UNROLL):
                ins = nc.vector.memset(KX[j][QROWS:QROWS + 3, :], 1.0)
            link(ins)

            def sq_filled(tl):
                bank = tl.slot(sq_full, 3)
                dve.wait_ge(sq_full.sem, tl.next(sq_full))
                return SQ[bank]

            def max_scores(tl, kt):
                for hf in range(2):
                    bank = sq_filled(tl)
                    nc.vector.tensor_reduce(nm2[:, 2 * kt + hf:2 * kt + hf + 1], bank, AX, ALU.max)\
                        .then_inc(sq_done.sem, 1)
                    tl.next(sq_done)

            def maxima(tl, r):
                dve.wait_ge(sq_done.sem, tl.value(sq_done))
                nc.vector.tensor_reduce(nm[:, r, :], nm2.rearrange("p (q h) -> p q h", h=2), AX, ALU.max,
                                        negate=True).then_inc(max_ready.sem, 1)
                dve.wait_ge(max_ready.sem, tl.next(max_ready))

            def maxima_rows(tl, stored):
                bank = sq_filled(tl)
                dve.wait_ge(d_m1, stored)
                nc.vector.tensor_copy(MT[:, :], bank.bitcast(BF16)[0:24, 0:128]).then_inc(sq_done.sem, 1)
                tl.next(sq_done)

            def head_out(tl, chain, n, r):
                bank = sq_filled(tl)[:, 0:256].rearrange("p (s g d) -> p g s d", s=2, g=4)
                rs = rsum[:, 0:8].rearrange("p (g s) -> p g s", s=2)
                chain(nc.vector.reciprocal(rs, bank[:, :, :, DH]))
                dve.wait_ge(d_oh[r], (n // 2) * 16 + DC)
                nc.vector.tensor_tensor(OH[:, r, :, :].rearrange("p (g s) d -> p g s d", s=2),
                                        bank[:, :, :, 0:DH],
                                        rs.unsqueeze(3).to_broadcast([128, 4, 2, DH]), ALU.mult)\
                    .then_inc(sq_done.sem, 1)
                dve.wait_ge(sq_done.sem, tl.next(sq_done))

            tl = Tally("b0")
            for j in range(2):
                for kt in range(QT_PER_HEAD):
                    max_scores(tl, kt)
                maxima(tl, j)
            maxima_rows(tl, 0)
            tl.close(sq_full)

            def head(tl, chain, i, j, last):
                n = i * UNROLL + j
                for kt in range(QT_PER_HEAD):
                    if not (last and j >= 2):
                        max_scores(tl, kt)
                    if kt == 1 and j >= 1:
                        head_out(tl, chain, n - 1, (j - 1) % 2)
                    if kt == 2 and not (last and j == UNROLL - 1):
                        maxima_rows(tl, (n + 1) * 16)
                if not (last and j >= 2):
                    maxima(tl, j % 2)
                if j == UNROLL - 1:
                    head_out(tl, chain, n, j % 2)

            with dve.Fori(0, NH // UNROLL - 1) as i:
                tl = Tally("b", i)
                chain = Chain(i, UNROLL)
                for j in range(UNROLL):
                    head(tl, chain, i, j, False)
                tl.close(sq_full, sq_done, max_ready)
            chain.close(NH // UNROLL - 1)
            tl = Tally("blast")
            chain = Chain(0, UNROLL)
            for j in range(UNROLL):
                head(tl, chain, NH // UNROLL - 1, j, True)
            tl.close(sq_full, sq_done, max_ready)
            chain.close(1)

            with dve.Fori(0, B) as b:
                tl = Tally("c", b)
                chain = Chain(b, links(order_c, SO=1, SN=2, FO=1, FN=5, RT=3 + 2 * 6 + 5, DL=1, S=1, OT=1, PJ=1))

                def self_norm(t):
                    xn = XN[:, t % BT, :]
                    normalised(tl, chain, ("SO", t), xn, xn, affine="so").then_inc(tok_ready.sem, 1)

                def gelu_norm(t):
                    xt, h = X[:, b * TB + t, :], HB[:, t % 2, :]
                    chain(normalised(tl, chain, ("FO", t), h, h, affine="fo"))
                    chain(nc.vector.tensor_tensor(xt, xt, h, ALU.add))
                    moments(tl, chain, xt)

                def experts_input(t):
                    if t >= 2:
                        left(tl, "L2", t - 2)
                    normalised(tl, chain, ("FN", t), X[:, b * TB + t, :], TOKF[:, t % 2, :]).then_inc(tok_ready.sem, 1)

                def router(k):
                    for hf in range(2):
                        bank = filled(tl)
                        signal_out(tl, nc.vector.tensor_copy(lg[:, hf * 2 * E:(hf + 1) * 2 * E], bank[:, 0:2 * E]))
                    dve.wait_ge(gate_exp.sem, tl.next(gate_exp))
                    chain(nc.vector.tensor_scalar(pr, pr, 1.0, None, ALU.add))
                    chain(nc.vector.reciprocal(pr, pr))
                    rk = rank.unsqueeze(1).to_broadcast([128, BT, E])
                    chain(nc.vector.tensor_copy(pw, pr))
                    for c in range(2):
                        v, key = top[:, 3 * c, :], top[:, 3 * c + 1, :]
                        vb = v.unsqueeze(2).to_broadcast([128, BT, E])
                        chain(nc.vector.tensor_reduce(v, pw, AX, ALU.max))
                        chain(nc.vector.tensor_tensor(eq, pw, vb, ALU.is_equal))
                        chain(nc.vector.tensor_tensor(eq, eq, rk, ALU.mult))
                        chain(nc.vector.tensor_reduce(key, eq, AX, ALU.max))
                        h = hot if c == 0 else eq
                        chain(nc.vector.tensor_tensor(h, eq, key.unsqueeze(2).to_broadcast([128, BT, E]), ALU.is_equal))
                        if c == 0:
                            chain(nc.vector.scalar_tensor_tensor(pw, h, -4.0, pw, ALU.mult, ALU.add))
                        else:
                            chain(nc.vector.tensor_tensor(hot, hot, h, ALU.add))
                    chain(nc.vector.tensor_tensor(top[:, 2, :], top[:, 0, :], top[:, 3, :], ALU.add))
                    chain(nc.vector.tensor_scalar(top[:, 2, :], top[:, 2, :], 1e-20, None, ALU.add))
                    chain(nc.vector.reciprocal(top[:, 5, :], top[:, 2, :]))
                    chain(nc.vector.tensor_tensor(hot, hot, pr, ALU.mult))
                    chain(nc.vector.tensor_tensor(cw[:, k * BT:(k + 1) * BT, :], hot,
                                                  top[:, 5, :].unsqueeze(2).to_broadcast([128, BT, E]), ALU.mult))

                def squares(places):
                    for dst in places:
                        dve.wait_ge(tr_done.sem, tl.next(tr_done))
                        r = RR[:, tl.slot(a_ready, 2), :]
                        nc.vector.tensor_tensor(dst, r, r, ALU.mult).then_inc(a_ready.sem, 1)
                        tl.next(a_ready)

                def expert_up(k, e):
                    squares([HM[:, (e % 2) * 2 + m, :] for m in range(2)])

                def expert_down(k, e, t):
                    bank = filled(tl)
                    xt = X[:, b * TB + t, :]
                    signal_out(tl, nc.vector.scalar_tensor_tensor(xt, bank[:, 0:D], cw[:, t, e:e + 1], xt,
                                                                  ALU.mult, ALU.add))

                def last_expert_down(k, e, t):
                    expert_down(k, e, t)
                    moments(tl, chain, X[:, b * TB + t, :])

                def experts_norm(t):
                    if t >= 2:
                        left(tl, "L3", t - 2)
                    normalised(tl, chain, ("DL", t // BT, E - 1, t), X[:, b * TB + t, :], TOKM[:, t % 2, :])\
                        .then_inc(tok_ready.sem, 1)

                def projected(t):
                    bank = filled(tl)
                    xt = X[:, b * TB + t, :]
                    dve.wait_ge(resid_ready.sem, tl.after(resid_ready, "RX", t))
                    signal_out(tl, nc.vector.tensor_tensor(xt, bank[:, 0:D], xt, ALU.add))
                    moments(tl, chain, xt)

                def projected_norm(t):
                    if t >= 2:
                        left(tl, "LT", t - 2)
                    normalised(tl, chain, ("PJ", t), X[:, b * TB + t, :], TOK[:, t % 2, :]).then_inc(tok_ready.sem, 1)

                def output(t):
                    bank = filled(tl)
                    dve.wait_ge(d_out[t % 2], b * (TB // 2 * 16) + (t // 2 * 16 + DC))
                    nc.vector.tensor_tensor(OB[:, t % 2, :], bank[:, 0:D], X[:, b * TB + t, :], ALU.add)\
                        .then_inc(out_done.sem, 1)

                tl.walk(order_c, groups, attention(tl, chain, SC1) | {
                    "VW": lambda: pass_start(tl, VS1[0:KP, b, :, :]), "SN": self_norm, "FN": gelu_norm,
                    "SO": lambda t: with_residual(tl, chain, t, XN[:, t % BT, :], RB[:, t % BT, :], "RS"),
                    "FO": lambda t: with_residual(tl, chain, t, HB[:, t % 2, :], XN[:, t % BT, :], "RF"),
                    "FM": experts_input, "RT": router, "UP": expert_up, "DN": expert_down,
                    "DL": last_expert_down, "DM": experts_norm, "PJ": projected, "PN": projected_norm,
                    "FC": lambda k: squares([hid[:, m, :] for m in range(MF)]), "FP": output})
            chain.close(B)

        @block.gpsimd
        def _(pool):
            steps = [0]

            def link(ins):
                steps[0] += 1
                ins.then_inc(s_pool, 1)
                pool.wait_ge(s_pool, steps[0])

            for s in (sc_full, sc_done, ln_stats, pc_ready, a_ready, st_full, st_done, pv_full, pv_done):
                pool.sem_inc(s.sem, s.credit)
            for s in (d_pieces, *d_x1, *d_out, *d_oh):
                pool.sem_inc(s, DC)
            nc.gpsimd.memset(identf[:, :], 0.0)
            nc.gpsimd.memset(identb[:, :], 0.0)
            nc.gpsimd.memset(blockmask[:, :], 1.0)
            nc.gpsimd.memset(minus_half, -0.5)
            nc.gpsimd.memset(onesb[:, :], 1.0)
            nc.gpsimd.memset(mask0[:, :, :], 0.0)
            nc.gpsimd.memset(mask1[:, :, :], 0.0)
            nc.gpsimd.memset(VS0[:, :, :, :], 0.0)
            link(nc.gpsimd.memset(VS1[:, :, :, :], 0.0))
            for m in (identf, identb):
                nc.gpsimd.affine_select(out=m[:, :], in_=m[:, :], compare_op=ALU.not_equal, fill=1.0, base=0,
                                        pattern=[[-1, 128]], channel_multiplier=1).then_inc(c_ready.sem, 1)
            for vs in (VS0, VS1):
                nc.gpsimd.memset(vs[:, :, :, DH:VW], 1.0).then_inc(c_ready.sem, 1)
            link(nc.gpsimd.affine_select(out=blockmask[:, :], in_=blockmask[:, :], compare_op=ALU.is_ge, fill=0.0,
                                         base=0, pattern=[[-DH, 128 // DH]], channel_multiplier=1))
            nc.gpsimd.affine_select(out=blockmask[:, :], in_=blockmask[:, :], compare_op=ALU.is_ge, fill=0.0,
                                    base=DH - 1, pattern=[[DH, 128 // DH]], channel_multiplier=-1)\
                .then_inc(c_ready.sem, 1)
            for e in range(E):
                ins = nc.gpsimd.memset(rank[:, e:e + 1], float(E - e))
            ins.then_inc(c_ready.sem, 1)

            class Chain:
                def __init__(self, i, per):
                    self.i, self.per, self.n, self.at = i, per, 0, steps[0]

                def __call__(self, ins):
                    self.n += 1
                    ins.then_inc(s_pool, 1)
                    pool.wait_ge(s_pool, self.i * self.per + (self.at + self.n))
                    carry_wait(pool)

                def close(self, trips):
                    assert self.n == self.per, self.n
                    steps[0] += self.per * trips

            def root(tl, chain):
                r = tl.slot(ln_stats, LR)
                pool.wait_ge(ln_stats.sem, tl.next(ln_stats))
                carry_wait(pool)
                chain(nc.gpsimd.tensor_scalar(ve[:, r:r + 1], mv[:, r, 1:2], EPS, None, ALU.add))
                nc.gpsimd.tensor_tensor(rstd[:, r:r + 1], ve[:, r:r + 1], minus_half, ALU.pow)\
                    .then_inc(ln_rstd.sem, 1)

            def roots(tl, chain):
                one = lambda *_: root(tl, chain)
                return {"LS": one, "PJ": one, "SO": one, "FO": one, "FN": one, "DL": one}

            def add_bias(tile, name):
                nc.gpsimd.tensor_tensor(tile, tile, rows[name], ALU.add).then_inc(resid_ready.sem, 1)

            pool.wait_ge(setup_done.sem, 1)
            with pool.Fori(0, B) as b:
                tl = Tally("a", b)
                chain = Chain(b, ln_stats.per["a"])

                def bias_a(t):
                    pool.wait_ge(tr_done.sem, tl.after(tr_done, "LN0", t))
                    add_bias(XN[:, t, :], "co_b")

                tl.walk(order_a, groups, roots(tl, chain) | {"RA": bias_a})
            chain.close(B)

            def head_values(n, j):
                carry_wait(pool)
                nc.gpsimd.tensor_copy(VH[:, j % 2, :, 0:VW], VX[:, n, :, :]).then_inc(vh_ready.sem, 1)

            def split(tl, chain, r):
                pool.wait_ge(max_ready.sem, tl.next(max_ready))
                carry_wait(pool)
                v = nm[:, r, :]
                chain(nc.gpsimd.tensor_copy(ms[:, r, 0:8], v))
                chain(nc.gpsimd.tensor_tensor(nres, v, ms[:, r, 0:8], ALU.subtract))
                chain(nc.gpsimd.tensor_copy(ms[:, r, 8:16], nres))
                nc.gpsimd.tensor_tensor(ms[:, r, 16:24], nres, ms[:, r, 8:16], ALU.subtract).then_inc(m_split.sem, 1)
                pool.wait_ge(m_split.sem, tl.next(m_split))

            pool.wait_ge(out_done.sem, out_done.base["b0"])
            tl = Tally("b0")
            chain = Chain(0, 6)
            for j in range(2):
                head_values(j, j)
            for j in range(2):
                split(tl, chain, j)
            chain.close(1)

            def head(tl, chain, i, j, last):
                n = i * UNROLL + j
                if not (last and j >= 2):
                    split(tl, chain, j % 2)
                    pool.wait_ge(pv_full.sem, tl.next(pv_full))
                    head_values(n + 2, j)

            with pool.Fori(0, NH // UNROLL - 1) as i:
                tl = Tally("b", i)
                chain = Chain(i, 3 * UNROLL)
                for j in range(UNROLL):
                    head(tl, chain, i, j, False)
            chain.close(NH // UNROLL - 1)
            tl = Tally("blast")
            chain = Chain(0, 3 * (UNROLL - 2))
            for j in range(UNROLL):
                head(tl, chain, NH // UNROLL - 1, j, True)
            chain.close(1)

            pool.wait_ge(sq_done.sem, sq_done.total)
            with pool.Fori(0, B) as b:
                tl = Tally("c", b)
                chain = Chain(b, ln_stats.per["c"])

                def bias_so(t):
                    pool.wait_ge(d_rb, b * (BLOCKS * 16) + (t // BT + 1) * 16)
                    add_bias(RB[:, t % BT, :], "so_b")

                def bias_fo(t):
                    pool.wait_ge(tr_done.sem, tl.after(tr_done, "LX", t))
                    add_bias(XN[:, t % BT, :], "fo_b")

                def bias_x(t):
                    pool.wait_ge(tok_ready.sem, tl.after(tok_ready, "DM", t))
                    add_bias(X[:, b * TB + t, :], "bo")

                tl.walk(order_c, groups, roots(tl, chain) | {"RS": bias_so, "RF": bias_fo, "RX": bias_x})
            chain.close(B)


def kernel(**inputs):
    import concourse.bacc as bacc
    from concourse.bass_utils import run_bass_kernel_spmd

    nc = bacc.Bacc("TRN2", target_bir_lowering=False, num_devices=1)
    arrays, aps = {}, {}
    for name, value in inputs.items():
        a = np.ascontiguousarray(value)
        if a.ndim == 0:
            a = a.reshape(1)
        arrays[f"in_{name}"] = a
        aps[name] = nc.dram_tensor(f"in_{name}", a.shape, mybir.dt.from_np(a.dtype), kind="ExternalInput").ap()
    out = nc.dram_tensor("out", (B, S, D), F32, kind="ExternalOutput").ap()
    build(nc, aps, out)
    result = run_bass_kernel_spmd(nc, [arrays], core_ids=[0])
    return result.results[0]["out"]
```

```python
from contextlib import ExitStack

import numpy as np
import concourse.bass as bass
from concourse import mybir

F32 = mybir.dt.float32
BF16 = mybir.dt.bfloat16
I32 = mybir.dt.int32
ALU = mybir.AluOpType
ACT = mybir.ActivationFunctionType
AX = mybir.AxisListType.X

B, S, D, H = 2, 1024, 256, 16
DH = D // H
KD = D // 128
SC = 77
NP = 10
SC1 = SC + NP
F = 1024
MF = F // 128
E, W = 8, 256
R = 16
T = B * S // 128
BT = 4
N = BT * 128
TB = S // 128
BLOCKS = TB // BT
QT_PER_HEAD = S // 128
KP = 96
NH = B * H
VW = DH + 1
EPS = 1e-5
DC = 16
CHUNK_HEADS = 4
NCH = H // CHUNK_HEADS
QROWS = 6 * DH
UNROLL = 4


STEP = {
    "VW": dict(vsw=1),
    "LS": dict(ln=1),
    "LN0": dict(tr=1, tok=1),
    "QP": dict(tr=KD),
    "S": dict(sc=1),
    "E": dict(exp=1),
    "T": dict(tr=4),
    "PV": dict(tr=1),
    "OT": dict(out=1),
    "CT": dict(tr=1),
    "PJ": dict(out=1, ln=1),
    "PN": dict(tok=1),
    "LT": dict(tr=1),
    "RA": dict(res=1),
    "QK": dict(tr=2 * KD, pc=2 * KD),
    "SV": dict(out=1),
    "LD": dict(),
    "NX": dict(),
    "ST": dict(tr=1),
    "RS": dict(res=1),
    "SO": dict(out=1, ln=1),
    "SN": dict(tok=1),
    "LX": dict(tr=1),
    "FI": dict(tr=MF),
    "RF": dict(res=1),
    "FO": dict(out=1, ln=1),
    "FN": dict(ln=1),
    "FM": dict(tok=1),
    "L2": dict(tr=1),
    "RT": dict(out=2, gate=1),
    "UP": dict(tr=2, act=2),
    "DN": dict(out=1),
    "DL": dict(out=1, ln=1),
    "DM": dict(tok=1),
    "L3": dict(tr=1),
    "RX": dict(res=1),
    "FC": dict(tr=MF, act=MF),
    "FP": dict(out=1),
}
ORDER_A = """
LS.1 VW LS.0 LS.2 LN0.0 LN0.1 LS.3 LN0.2 LS.4 RA.1 LS.7 LN0.3 QP.0 LN0.4 S.0 E.0 S.1 T.0 LS.5 E.1 RA.4 S.2 PV.0
T.1 RA.3 LN0.5 RA.0 LS.6 OT.0 PV.1 LN0.6 LN0.7 S.3 E.2 CT.0 T.2 OT.1 QP.1 RA.2 PJ.0 PN.0 PV.2 E.3 CT.1 S.4 T.3
RA.5 OT.2 PJ.1 PV.3 S.5 E.4 CT.2 OT.3 LT.0 T.4 PN.1 PJ.2 PV.4 S.6 E.5 RA.7 CT.3 OT.4 LT.1 T.5 PN.2 PJ.3 CT.4 E.6
PV.5 LT.2 PJ.4 PN.3 RA.6 T.6 PN.4 OT.5 S.7 CT.5 PV.6 LT.3 E.7 PJ.5 OT.6 PN.5 QK.0 SV.1 T.7 CT.6 PV.7 SV.3 OT.7
PJ.6 CT.7 SV.2 PJ.7 SV.0 LT.5 LT.4 PN.6 PN.7 SV.4 LT.6 SV.5 LT.7 QK.1 SV.7 SV.6
"""
ORDER_C = """
RS.0 ST.0 ST.1 RS.3 RS.1 SO.0 RS.2 SO.1 ST.3 ST.5 ST.2 SN.0 SO.3 SO.2 SN.1 LX.1 LD.1 ST.6 RS.5 SN.2 LX.0 RF.0
ST.7 RS.6 SN.3 LX.2 RF.2 LX.3 FI.0 RS.4 ST.4 RF.1 RF.3 FO.0 SO.4 FN.0 RS.7 FO.1 SN.4 FM.0 SO.5 FN.1 FO.2 FO.3
SO.7 SO.6 LX.4 SN.5 L2.0 SN.6 RF.4 LX.6 LX.5 SN.7 FM.1 LX.7 RF.6 FN.2 FN.3 FM.2 L2.1 RF.7 FM.3 RF.5 FI.1 L2.3
L2.2 RT.0 UP.0.0 FO.4 FO.5 UP.0.1 DN.0.0.3 DN.0.0.0 DN.0.1.3 DN.0.0.2 DN.0.0.1 FN.4 DN.0.1.0 FO.6 DN.0.1.2 FN.5
UP.0.2 FM.4 FN.6 FO.7 DN.0.1.1 UP.0.3 L2.4 DN.0.2.3 DN.0.2.2 DN.0.3.2 DN.0.2.1 DN.0.3.1 DN.0.2.0 FM.5 FN.7
DN.0.3.3 UP.0.4 DN.0.3.0 UP.0.5 DN.0.4.3 DN.0.4.1 L2.5 DN.0.4.0 DN.0.5.0 DN.0.4.2 DN.0.5.3 FM.6 DN.0.5.2 FM.7
DN.0.5.1 UP.0.6 UP.0.7 L2.6 DN.0.6.2 DN.0.6.0 DL.0.7.0 DL.0.7.2 L2.7 DN.0.6.1 DM.0 DN.0.6.3 RT.1 DL.0.7.1
DL.0.7.3 UP.1.0 UP.1.1 L3.0 DN.1.0.5 DN.1.0.4 DM.1 DN.1.1.5 DN.1.0.7 L3.1 DN.1.0.6 DM.2 DN.1.1.4 DN.1.1.6
DN.1.1.7 DM.3 UP.1.2 UP.1.3 L3.3 DN.1.2.7 DN.1.2.5 L3.2 DN.1.2.4 DN.1.3.5 DN.1.2.6 DN.1.3.7 RX.0 QP.0 DN.1.3.4
S.1 UP.1.4 S.0 VW DN.1.3.6 E.0 DN.1.4.5 UP.1.5 DN.1.4.6 T.0 E.1 DN.1.4.4 RX.3 PV.0 DN.1.5.4 DN.1.5.5 S.2
DN.1.4.7 DN.1.5.7 UP.1.6 E.2 DN.1.5.6 UP.1.7 OT.0 T.1 DN.1.6.4 DL.1.7.4 CT.0 DN.1.6.6 PV.1 DM.4 DN.1.6.7
DN.1.6.5 PJ.0 DL.1.7.5 RX.2 DM.5 PN.0 L3.4 T.2 DL.1.7.6 OT.1 RX.4 PV.2 L3.5 DM.6 DL.1.7.7 CT.1 L3.6 DM.7 S.3
L3.7 RX.6 RX.1 RX.7 LT.0 OT.2 QP.1 PJ.1 E.3 S.4 CT.2 T.3 RX.5 PJ.2 PN.1 PV.3 S.5 E.4 T.4 E.5 OT.3 LT.1 PN.2 PV.4
S.6 CT.3 T.5 OT.4 LT.2 PJ.3 E.6 PV.5 PN.3 S.7 CT.4 T.6 OT.5 LT.3 PV.6 E.7 FC.0 PJ.4 T.7 CT.5 PN.4 OT.6 PV.7 PJ.5
CT.6 PN.5 FP.0 OT.7 LT.4 LT.5 NX PJ.6 PN.6 CT.7 FP.1 PJ.7 LT.6 PN.7 FP.2 LT.7 FP.3 FC.1 FP.4 FP.5 FP.6 FP.7
"""


def attention_order(before):
    for t in range(TB - 1):
        for a, b in (("PV", "T"), ("OT", "PV"), ("CT", "OT"), ("PJ", "CT")):
            before((a, t), (b, t + 1))
        if t + 2 < TB:
            before(("T", t), ("S", t + 2))
            before(("LT", t), ("PN", t + 2))
    before(("S", BT - 1), ("QP", 1))
    before(("QP", 1), ("S", BT))


def parsed(text):
    order = [(w.split(".")[0], *map(int, w.split(".")[1:])) for w in text.split()]
    assert len(set(order)) == len(order)

    def before(a, b):
        assert order.index(a) < order.index(b), (a, b)

    return order, before


def schedule_a():
    order, before = parsed(ORDER_A)
    attention_order(before)
    for t in range(BT):
        before(("SV", t), ("LT", BT))
    for t in range(TB - 2):
        before(("PN", t), ("PJ", t + 2))
    return order


def schedule_c():
    order, before = parsed(ORDER_C)
    attention_order(before)
    for t in range(BT):
        before(("SO", t), ("ST", t + BT))
        before(("FO", t), ("SO", t + BT))
        before(("SO", t), ("LD", 1))
        before(("DN", 0, E - 2, t), ("UP", 1, 0))
        before(("DL", 0, E - 1, t), ("UP", 1, 1))
        before(("FO", t), ("FI", 1))
        before(("SO", t + BT), ("LT", 0))
        before(("FO", t + BT), ("FC", 0))
        before(("FP", t), ("FC", 1))
        before(("ST", t + BT), ("T", 0))
    for t in range(TB - 2):
        before(("FN", t), ("FO", t + 2))
        before(("L2", t), ("FM", t + 2))
        before(("L3", t), ("DM", t + 2))
    for k in range(BLOCKS):
        for e in range(2, E):
            for t in range(BT):
                before(("DN", k, e - 2, k * BT + t), ("UP", k, e))
    before(("PV", TB - 1), ("NX",))
    for t in range(BT, TB):
        before(("SO", t), ("NX",))
    before(("FI", 0), ("LX", BT))
    before(("RT", 0), ("RT", 1))
    before(("FI", 1), ("L3", 0))
    before(("QP", 0), ("L3", BT))
    before(("FC", 0), ("LT", BT))
    return order


class Signal:

    TRIPS = {"setup": 1, "a": B, "b0": 1, "b": NH // UNROLL - 1, "blast": 1, "w": 1, "c": B}

    def __init__(self, sem, credit=0, **per):
        self.sem, self.credit = sem, credit
        self.per = {part: per.get(part, 0) for part in self.TRIPS}
        self.base, total = {}, credit
        for part, n in self.per.items():
            self.base[part] = total
            total += n * self.TRIPS[part]
        self.total = total


class Tally:

    def __init__(self, part, i=0):
        self.part, self.i, self.n = part, i, {}

    def at(self, s, n):
        return self.i * s.per[self.part] + max(s.base[self.part] + n, s.credit)

    def value(self, s):
        return self.at(s, self.n.get(s, 0))

    def next(self, s, m=1):
        self.n[s] = self.n.get(s, 0) + m
        return self.value(s)

    def back(self, s, lag):
        return self.at(s, self.n.get(s, 0) - lag)

    def slot(self, s, ring):
        before = s.base[self.part] - s.credit
        assert isinstance(self.i, int) or s.per[self.part] % ring == 0
        return (before + self.n.get(s, 0)) % ring

    def slot_of(self, s, ring, *step):
        n = self.counts[step][s]
        assert self.n.get(s, 0) <= n - 1 + ring, step
        return (s.base[self.part] - s.credit + n - 1) % ring

    def close(self, *signals):
        for s in signals:
            assert self.n.get(s, 0) == s.per[self.part], (self.part, s.sem, self.n.get(s, 0), s.per[self.part])

    def walk(self, order, groups, handlers):
        self.counts, n = {}, {s: 0 for g in groups.values() for s in g}
        for step in order:
            for g, m in STEP[step[0]].items():
                for s in groups[g]:
                    n[s] += m
            self.counts[step] = dict(n)
        n = {s: 0 for s in n}
        for self.now, step in enumerate(order):
            self.n = dict(n)
            if step[0] in handlers:
                handlers[step[0]](*step[1:])
            n = self.counts[step]

    def after(self, s, *step):
        assert list(self.counts).index(step) <= self.now, step
        return self.at(s, self.counts[step][s])

    def after_block(self, s, name, k):
        last = max(range(k * BT, (k + 1) * BT), key=lambda t: self.counts[name, t][s])
        return self.after(s, name, last)


def build(nc, A, out):
    ctx = ExitStack()
    with ctx:
        def sb(name, shape, dt=F32):
            return ctx.enter_context(nc.sbuf_tensor(name, shape, dt))

        def ps(name, shape, dt=F32):
            return ctx.enter_context(nc.psum_tensor(name, shape, dt))

        def sem(name):
            return ctx.enter_context(nc.semaphore(name))

        X = sb("X", [128, T, D])
        shared = sb("shared", [128, 3 * 4096])
        VX = shared[:, 0:NH * 8 * VW].rearrange("p (n k d) -> p n k d", n=NH, k=8)
        o = NH * 8 * VW
        PC = shared[:, o:o + 3072].bitcast(BF16).rearrange("p (e c n) -> p e c n", e=4, c=3)
        PTB = shared[:, o:o + 2048].rearrange("p (r n) -> p r n", r=2)
        o += 3072
        KB0 = shared[:, o:o + B * H * SC].rearrange("p (b n) -> p b n", b=B)
        QX = [shared[:, o + 512 * j:o + 512 * (j + 1)].bitcast(BF16) for j in range(UNROLL)]
        KX = [shared[:, o + 2048 + 512 * j:o + 2048 + 512 * (j + 1)].bitcast(BF16) for j in range(UNROLL)]
        assert o + 4096 <= 3 * 4096
        w1 = shared[:, 0:4096].rearrange("p (k n) -> p k n", k=KD)
        w2 = shared[:, 4096:8192].rearrange("p (m n) -> p m n", m=2 * E)
        hid = shared[:, 8192:12288].rearrange("p (m n) -> p m n", m=MF)
        fifo = sb("fifo", [128, 2 * 2048])
        cq, co, sq, sk, sv = (fifo[:, 512 * j:512 * (j + 1)].rearrange("p (k n) -> p k n", k=KD) for j in range(5))
        fi = fifo[:, 0:2048].rearrange("p (k n) -> p k n", k=KD)
        fo = fifo[:, 2048:4096].rearrange("p (m n) -> p m n", m=MF)

        fcT = sb("fcT", [128, KD, F])
        projT = sb("projT", [128, MF, D])
        so, wq, wo = (sb(n, [128, KD, D]) for n in ("so", "wq", "wo"))
        routerT = sb("routerT", [128, KD, E])
        KB1 = sb("KB1", [128, B, H * SC1])
        VS0 = sb("VS0", [128, B, H, VW])
        VS1 = sb("VS1", [128, B, H, VW])
        VSW = sb("VSW", [128, H, 32])
        mask0 = sb("mask0", [128, B, SC], BF16)
        mask1 = sb("mask1", [128, QT_PER_HEAD, SC1], BF16)
        rows_a = sb("rows_a", [128, 4, D])
        names_a = ("co_b", "co_g", "co_be", "sv_b")
        rows = {n: rows_a[:, j, :] for j, n in enumerate(names_a)}
        rows |= {n: sb(n, [128, D])[:, :] for n in ("so_b", "so_g", "so_be", "fo_b", "fo_g", "fo_be", "bo")}
        TOKF, OB = rows_a[:, 0:2, :], rows_a[:, 2:4, :]
        cols = {n: sb(n, [128, m]) for n, m in (("cq_b", KD), ("sq_b", KD), ("sk_b", KD), ("bq", KD),
                                                ("ck_b", KD), ("bk", KD), ("fi_b", MF))}
        identf = sb("identf", [128, 128])
        identb = sb("identb", [128, 128], BF16)
        onesb = sb("onesb", [128, 128], BF16)
        blockmask = sb("blockmask", [128, 128 // DH])

        XN = sb("XN", [128, TB, D])
        RB = XN[:, BT:, :]
        TOK = sb("TOK", [128, 2, D])
        TOKM = sb("TOKM", [128, 2, D])
        HB = sb("HB", [128, 2, D])
        xT2 = sb("xT2", [128, 2, KD, N])
        xT3 = sb("xT3", [128, 2, KD, N])
        xTb, xTs = xT3[:, 0], xT3[:, 1]
        wfc = xT3[:, :, :, :].rearrange("p b k n -> p (b k n)").rearrange("p (m d) -> p m d", m=MF)
        wproj = xT2[:, :, :, :].rearrange("p b k n -> p (b k n)").rearrange("p (m d) -> p m d", m=KD)
        QT = sb("QT", [128, KD, N])
        P = sb("P", [128, 2, H, KP])
        ck, cv, wk, wv = (P[:, j // 2].rearrange("p h k -> p (h k)")[:, 512 * (j % 2):512 * (j % 2) + 512]
                          .rearrange("p (k n) -> p k n", k=KD) for j in range(4))
        PTS = sb("PTS", [128, H, 128])
        OSB = sb("OSB", [128, 512])
        CA = sb("CA", [128, D])
        CAT = sb("CAT", [128, KD, 128])
        TOKS = PTS[:, :, :].rearrange("p h n -> p (h n)").rearrange("p (t d) -> p t d", d=D)
        RR = sb("RR", [128, 2, N])
        HM = sb("HM", [128, 4, N])
        VH = HM[:, 0, :].rearrange("p (r k d) -> p r k d", r=2, d=32)
        OH = HM[:, 1, 0:256].rearrange("p (r q d) -> p r q d", r=2, d=DH)
        small = sb("small", [128, 512])
        LR = 8
        mv = small[:, 448:464].rearrange("p (r s) -> p r s", r=LR)
        rstd = small[:, 464:472]
        ve = small[:, 472:480]
        minus_half = small[:, 16:17]
        stats = small[:, 20:26]
        rsum = small[:, 32:48]
        mx = small[:, 48:64]
        lg = small[:, 64:96]
        pr = small[:, 96:128].rearrange("p (t e) -> p t e", e=E)
        pw = small[:, 128:160].rearrange("p (t e) -> p t e", e=E)
        eq = small[:, 160:192].rearrange("p (t e) -> p t e", e=E)
        hot = small[:, 192:224].rearrange("p (t e) -> p t e", e=E)
        cw = small[:, 384:448].rearrange("p (t e) -> p t e", e=E)
        rank = small[:, 256:264]
        top = small[:, 264:288].rearrange("p (j t) -> p j t", t=BT)
        nm = small[:, 304:320].rearrange("p (r q) -> p r q", r=2)
        nres = small[:, 320:328]
        wscale = small[:, 480:510].rearrange("p (j m) -> p j m", j=3)
        gate = small[0:R, 352:353]
        ms = small[:, 360:384].bitcast(BF16).rearrange("p (r n) -> p r n", r=2)
        MT = sb("MT", [24, 128], BF16)
        ctxs = XN[0:SC, 0:B, :]
        ctxT = xT2[:, 0, :, 0:B * SC]
        kT = xTb[:, :, 0:B * SC]
        kT1 = xTb[:, :, B * SC:2 * B * SC]
        pkT = QT[:, :, 0:NP]
        masks = QT[0:3, 0, 256:256 + 2 * SC]
        mtmp = QT[0:3, 1, 256:256 + 2 * SC]
        mpiece = OSB[0:3, 0:B * SC].bitcast(BF16)[:, 0:2 * SC]
        maski = HM[:, 2:4, :].rearrange("p a n -> p (a n)")[:, 0:QT_PER_HEAD * SC].bitcast(I32)\
            .rearrange("p (q k) -> p q k", k=SC)
        vb0, vb1 = TOK[:, 0, :], TOK[:, 1, :]
        u_sb = HB[:, 0, 0:MF * R].rearrange("p (m r) -> p m r", r=R)
        fbT = HB[0:R, 1, 0:R]
        v_sb = CA[0:R, :]
        G_sb = CAT[0:R, :, :].rearrange("p k n -> p (k n)")
        uT = RB[0:R, :, :].rearrange("p t n -> p (t n)")
        TN = OSB[:, 256:512]

        SCR = ps("SCR", [128, 4, 512])
        TR = ps("TR", [128, 2, 512])
        OUT = ps("OUT", [128, 2, 512])
        SQ = [TR, SCR[:, 2:4, :]]
        AUX = OUT[:, 0, :]
        PV = OUT[:, 1, :]

        scratch = nc.dram_tensor("pieces", [2, 3, NH * DH, S], BF16)
        o_dram = nc.dram_tensor("self_out", [128, TB, NH * DH], F32)
        x1_dram = nc.dram_tensor("x1", [128, T, D], F32)
        mscratch = nc.dram_tensor("maxima", [2, 24, 128], BF16)

        d_ctx, d_kv, d_low, d_tern, d_const, d_x, d_aw, d_cw, d_mask, d_prefix, d_fifo, d_moe, d_m1, d_m2, \
            d_pieces, d_rb, d_late = (sem(n) for n in (
                "ctx_loaded", "small_kv_weights_loaded", "low_rank_loaded", "ternary_sources_loaded",
                "biases_loaded", "x_loaded", "part_a_weights_loaded", "part_c_weights_loaded", "masks_loaded",
                "prefix_loaded", "gelu_weights_loaded", "expert_weights_loaded",
                "maxima_to_dram", "maxima_to_rows", "pieces_stored", "residuals_loaded", "part_c_biases_loaded"))
        order_a, order_c = schedule_a(), schedule_c()

        def count(group):
            return {part: sum(STEP[s[0]].get(group, 0) for s in order) for part, order in (("a", order_a), ("c", order_c))}

        tr_full = Signal(sem("tr_full"), setup=1 + 4 + 2 + 1 + 4, w=4, **count("tr"))
        tr_done = Signal(sem("tr_done"), **tr_full.per)
        out_full = Signal(sem("out_full"), setup=4, w=4, **count("out"))
        out_done = Signal(sem("out_done"), **out_full.per)
        sc_full = Signal(sem("scores_full"), 1, **count("sc"))
        sc_done = Signal(sem("scores_done"), 1, **count("sc"))
        p_ready = Signal(sem("probs_ready"), **count("exp"))
        ln_stats = Signal(sem("ln_stats"), 1, **count("ln"))
        ln_rstd = Signal(sem("ln_rstd"), **count("ln"))
        tok_ready = Signal(sem("token_tile_ready"), **count("tok"))
        resid_ready = Signal(sem("residual_ready"), **count("res"))
        vsw_ready = Signal(sem("small_values_ready"), **count("vsw"))
        pc_ready = Signal(sem("pieces_ready"), 1, **count("pc"))
        gate_exp = Signal(sem("gate_exp"), **count("gate"))
        a_ready = Signal(sem("squared_ready"), 1, **count("act"))
        groups = {"tr": (tr_full, tr_done), "out": (out_full, out_done), "sc": (sc_full, sc_done), "exp": (p_ready,),
                  "ln": (ln_stats, ln_rstd), "tok": (tok_ready,), "res": (resid_ready,), "vsw": (vsw_ready,),
                  "pc": (pc_ready,), "gate": (gate_exp,), "act": (a_ready,)}
        d_o = [sem(f"self_out_loaded_{k}") for k in range(BLOCKS)]
        d_x1, d_out, d_oh = ([sem(f"{n}_{r}") for r in range(2)] for n in ("x1_stored", "out_stored", "head_out_stored"))
        sq_full = Signal(sem("max_scores_full"), b0=2 * QT_PER_HEAD, b=UNROLL * QT_PER_HEAD,
                         blast=(UNROLL - 2) * QT_PER_HEAD)
        sq_done = Signal(sem("maxima_ready"), **sq_full.per)
        aux_full = Signal(sem("transposes_full"), 1, b0=1, b=2 * UNROLL, blast=2 * UNROLL - 1)
        aux_done = Signal(sem("transposes_taken"), 1, **aux_full.per)
        st_full = Signal(sem("t_scores_full"), 1, b=UNROLL * 16, blast=UNROLL * 16)
        st_done = Signal(sem("t_probs_ready"), 1, **st_full.per)
        pv_full = Signal(sem("head_out_full"), 1, b=UNROLL, blast=UNROLL)
        pv_done = Signal(sem("head_out_done"), 1, **pv_full.per)
        vh_ready = Signal(sem("head_values_ready"), b0=2, b=UNROLL, blast=UNROLL - 2)
        m_split = Signal(sem("maxima_split"), b0=2, b=UNROLL, blast=UNROLL - 2)
        c_ready = Signal(sem("constants_ready"), setup=6)
        carrier = sem("wait_carrier")
        s_dve, s_pool = sem("vector_step"), sem("gpsimd_step")
        kb1_ready = sem("layer_1_keys_ready")
        sums_ready = sem("weight_sums_ready")
        wscale_ready = sem("weight_scales_ready")
        signs_ready = Signal(sem("weight_signs_ready"), b=1 + KD, blast=1 + KD)
        tern_ready = Signal(sem("ternary_ready"), b=1 + KD, blast=1 + KD)
        mask1_ready = Signal(sem("mask1_ready"), setup=1)
        setup_done = Signal(sem("setup_done"), setup=1)
        d_head = [sem(f"head_loaded_{j}") for j in range(UNROLL)]

        def r4(ap):
            return ap.rearrange("(k p) n -> p k n", p=128)

        def col(ap):
            return ap.rearrange("(k p) -> p k", p=128)

        def row(ap, parts=128):
            return ap.rearrange("(o n) -> o n", o=1).to_broadcast([parts, ap.shape[0]])

        def carry_wait(eng):
            eng.sem_inc(carrier, 1)

        def aux_value(tl, j, last, output):
            n = 0
            for jj in range(j + 1):
                n += not (last and jj == UNROLL - 1)
                if jj < j or output:
                    n += jj >= 1
            return Tally(tl.part, tl.i).next(aux_done, n)

        block = ctx.enter_context(nc.Block())

        @block.sync
        def _(sp):
            with nc.allow_non_contiguous_dma(reason="biases and small transposed loads"):
                sp.dma_start(ctxs, A["ctx_1024"].rearrange("b s d -> s b d")).then_inc(d_ctx, 16)
                for dst, n in ((ck, "L0_xattn_ck_w"), (cv, "L0_xattn_cv_w"), (wk, "L1_xattn_Wk"), (wv, "L1_xattn_Wv")):
                    sp.dma_start(dst, r4(A[n])).then_inc(d_kv, 16)
                for dst, n in ((cols["ck_b"], "L0_xattn_ck_b"), (cols["bk"], "L1_xattn_bk")):
                    sp.dma_start(dst[:, :], col(A[n])).then_inc(d_kv, 16)
                for dst, n in ((vb0, "L0_xattn_cv_b"), (vb1, "L1_xattn_bv")):
                    sp.dma_start(dst, row(A[n])).then_inc(d_kv, 16)
                for h in range(H):
                    sp.dma_start(pkT[h % 8 * DH:(h % 8 + 1) * DH, h // 8, :],
                                 A["L1_xattn_prefix_k"][h].rearrange("p d -> d p")).then_inc(d_prefix, 16)
                sp.dma_start(u_sb, A["L1_ffn_u"].rearrange("(m p) r -> p m r", p=128)).then_inc(d_low, 16)
                sp.dma_start(fbT, A["L1_ffn_fast_b"].rearrange("a b -> b a")).then_inc(d_low, 16)
                sp.dma_start(v_sb, A["L1_ffn_v"]).then_inc(d_low, 16)
                sp.dma_start(gate, row(A["L1_ffn_gate"], R)).then_inc(d_low, 16)
                m0 = A["mask_Bx1x1xS2_ff0"].rearrange("b x y k -> (x y) (b k)")
                sp.dma_start(masks, m0.to_broadcast([3, B * SC])).then_inc(d_mask, 16)
                sp.dma_start(maski, A["mask_1x1xSxS2_ik0"].rearrange("x y (q p) k -> p (x y q) k", p=128))\
                    .then_inc(d_mask, 16)
                sp.wait_ge(c_ready.sem, c_ready.total)
                for b in range(B):
                    sp.dma_start(VS1[SC:SC1, b, :, 0:DH], A["L1_xattn_prefix_v"].rearrange("h p d -> p h d"))\
                        .then_inc(d_prefix, 16)
                sp.dma_start(X[:, :, :], A["x"].rearrange("b (t p) d -> p (b t) d", p=128)).then_inc(d_x, 16)
                for dst, n in ((cq, "cq_w"), (co, "co_w"), (sq, "sq_w"), (sk, "sk_w"), (sv, "sv_w")):
                    sp.dma_start(dst, r4(A["L0_xattn_" + n])).then_inc(d_aw, 16)

                def load_biases(row_names, col_names, done):
                    for n in row_names:
                        sp.dma_start(rows[n], row(A["L1_xattn_bo" if n == "bo" else "L0_xattn_" + n])).then_inc(done, 16)
                    for n in col_names:
                        sp.dma_start(cols[n][:, :], col(A["L1_xattn_bq" if n == "bq" else "L0_xattn_" + n])).then_inc(done, 16)

                load_biases(names_a, ("cq_b", "sq_b", "sk_b"), d_const)
                load_biases([n for n in rows if n not in names_a], ("bq", "fi_b"), d_late)
                for dst, n in ((so, "L0_xattn_so_w"), (wq, "L1_xattn_Wq"), (wo, "L1_xattn_Wo")):
                    sp.dma_start(dst[:, :, :], r4(A[n])).then_inc(d_cw, 16)
                for k in range(KD):
                    sp.dma_start(routerT[:, k, :], A["L0_ffn_router_w"][:, k * 128:(k + 1) * 128]
                                 .rearrange("e p -> p e")).then_inc(d_cw, 16)

                with sp.Fori(0, B) as b:
                    tl = Tally("a", b)

                    def store_x1(t):
                        sp.wait_ge(tok_ready.sem, tl.after(tok_ready, "PN", t))
                        sp.dma_start(x1_dram[:, b * TB + t, :], TOK[:, t % 2, :]).then_inc(d_x1[t % 2], 16)

                    def store_pieces(k):
                        for e in range(2 * KD):
                            sp.wait_ge(pc_ready.sem, tl.next(pc_ready))
                            dst = scratch[e // 2, :, :, :].rearrange("c r s -> r c s")[
                                bass.ds(b * D + (e % 2) * 128, 128), :, k * N:(k + 1) * N]
                            sp.dma_start(dst, PC[:, e]).then_inc(d_pieces, 16)

                    tl.walk(order_a, groups, {"PN": store_x1, "QK": store_pieces})
                sp.wait_ge(d_pieces, DC + 16 * 4 * B * BLOCKS)
                for r in range(2):
                    sp.wait_ge(d_x1[r], DC + 16 * T // 2)
                def load_head(n, j):
                    src = scratch[:, :, bass.ds(n * DH, DH), :]
                    for c, r, m in ((0, 0, 3), (1, 3, 2), (2, 5, 1)):
                        rows = slice(r * DH, (r + m) * DH)
                        sp.dma_start(QX[j][rows, :], src[0, c].unsqueeze(0).to_broadcast([m, DH, S]))\
                            .then_inc(d_head[j], 16)
                        sp.dma_start(KX[j][rows, :], src[1, 0:m]).then_inc(d_head[j], 16)

                def store_output(n, r, taken):
                    sp.wait_ge(aux_done.sem, taken)
                    carry_wait(sp)
                    sp.dma_start(o_dram[:, :, bass.ds(n * DH, DH)], OH[:, r, :, :]).then_inc(d_oh[r], 16)

                def store_maxima(taken, j):
                    sp.wait_ge(aux_done.sem, taken)
                    sp.dma_start(mscratch[j % 2], MT[:, :]).then_inc(d_m1, 16)
                    return mscratch[j % 2].rearrange("(c q) t -> c (q t)", c=3)

                for j in range(3):
                    load_head(j, j)
                sp.wait_ge(out_done.sem, out_done.base["b0"])
                sp.wait_ge(tr_done.sem, tr_done.base["b0"])
                sp.dma_start(wfc, A["L1_ffn_w_fc"].rearrange("(m p) d -> p m d", p=128)).then_inc(d_tern, 16)
                sp.dma_start(wproj, A["L1_ffn_w_proj"].rearrange("(m p) d -> p m d", p=128)).then_inc(d_tern, 16)
                sp.dma_start(fi, r4(A["L0_xattn_fi_w"])).then_inc(d_fifo, 16)
                sp.dma_start(fo, A["L0_xattn_fo_w"].rearrange("(m p) n -> p m n", p=128)).then_inc(d_fifo, 16)
                src = store_maxima(aux_done.base["b"], 0)
                sp.wait_ge(d_m1, 16)
                sp.dma_start(QX[0][QROWS:QROWS + 3, :], src).then_inc(d_m2, 16)

                def head(tl, i, j, last):
                    n = i * UNROLL + j
                    if not (last and j >= 1):
                        sp.wait_ge(pv_full.sem, tl.value(pv_full))
                        load_head(n + 3, (j + 3) % UNROLL)
                    tl.next(pv_full)
                    if not (last and j == UNROLL - 1):
                        src = store_maxima(aux_value(tl, j, last, False), (j + 1) % UNROLL)
                        sp.wait_ge(d_m1, 16 + 16 * (n + 1))
                        sp.dma_start(QX[(j + 1) % UNROLL][QROWS:QROWS + 3, :], src).then_inc(d_m2, 16)
                    if j >= 1:
                        store_output(n - 1, (j - 1) % 2, aux_value(tl, j, last, True))
                    if j == UNROLL - 1:
                        store_output(n, j % 2, Tally(tl.part, tl.i).next(aux_done, aux_done.per[tl.part]))

                with sp.Fori(0, NH // UNROLL - 1) as i:
                    tl = Tally("b", i)
                    for j in range(UNROLL):
                        head(tl, i, j, False)
                tl = Tally("blast")
                for j in range(UNROLL):
                    head(tl, NH // UNROLL - 1, j, True)

                for r in range(2):
                    sp.wait_ge(d_oh[r], DC + 16 * NH // 2)

                def first_loads(b):
                    for k in range(BLOCKS):
                        sp.dma_start(TOKS[:, k * BT:(k + 1) * BT, :],
                                     o_dram[:, k * BT:(k + 1) * BT, bass.ds(b * D, D)]).then_inc(d_o[k], 16)
                        if k == 0:
                            sp.dma_start(RB, x1_dram[:, bass.ds(b * TB, BT), :]).then_inc(d_rb, 16)

                first_loads(0)

                sp.wait_ge(pv_full.sem, pv_full.total)
                for k in range(KD):
                    sp.dma_start(w1[:, k, :], A["L0_ffn_w1"][k * 128:(k + 1) * 128, :]).then_inc(d_moe, 16)
                for m in range(2):
                    sp.dma_start(w2[:, m * E:(m + 1) * E, :],
                                 A["L0_ffn_w2"][m * 1024:(m + 1) * 1024, :].rearrange("(m p) n -> p m n", p=128))\
                        .then_inc(d_moe, 16)
                with sp.Fori(0, B) as b:
                    tl = Tally("c", b)

                    def load_residuals(k):
                        sp.wait_ge(out_done.sem, tl.after_block(out_done, "SO", k - 1))
                        carry_wait(sp)
                        sp.dma_start(RB, x1_dram[:, bass.ds(b * TB + k * BT, BT), :]).then_inc(d_rb, 16)

                    def next_loads():
                        sp.wait_ge(tr_done.sem, tl.after(tr_done, "PV", TB - 1))
                        carry_wait(sp)
                        first_loads((b + 1) % B)

                    def store_out(t):
                        sp.wait_ge(out_done.sem, tl.after(out_done, "FP", t))
                        sp.dma_start(out[b, t * 128:(t + 1) * 128, :], OB[:, t % 2, :]).then_inc(d_out[t % 2], 16)

                    tl.walk(order_c, groups, {"LD": load_residuals, "NX": next_loads, "FP": store_out})
                for r in range(2):
                    sp.wait_ge(d_out[r], DC + 16 * T // 2)

        @block.tensor
        def _(pe):
            def tr_bank(tl):
                bank = tl.slot(tr_full, 2)
                tl.next(tr_full)
                v = tl.back(tr_full, 2)
                pe.wait_ge(tr_done.sem, v)
                return TR[:, bank, :]

            def out_bank(tl):
                bank = tl.slot(out_full, 2)
                tl.next(out_full)
                v = tl.back(out_full, 2)
                pe.wait_ge(out_done.sem, v)
                return OUT[:, bank, :]

            def evacuated(tl):
                pe.wait_ge(tr_done.sem, tl.value(tr_full))

            def product(dst, pairs):
                for n, (l, r) in enumerate(pairs):
                    ins = nc.tensor.matmul(dst, l, r, start=(n == 0), stop=(n == len(pairs) - 1))
                return ins

            def transposes(dst, srcs, ident=identf, width=128):
                for n, s in enumerate(srcs):
                    m, p = s.shape[1], s.shape[0]
                    ins = nc.tensor.transpose(dst[0:m, n * width:n * width + p], s, ident[0:p, 0:p])
                return ins

            tl = Tally("setup")
            pe.wait_ge(c_ready.sem, c_ready.total)
            pe.wait_ge(d_ctx, 16)
            bank = tr_bank(tl)
            transposes(bank, [ctxs[:, b, k * 128:(k + 1) * 128] for b in range(B) for k in range(KD)], width=SC)\
                .then_inc(tr_full.sem, 1)
            evacuated(tl)
            pe.wait_ge(d_kv, 16 * 8)
            for w in (ck, wk):
                for m in range(KD):
                    bank = tr_bank(tl)
                    product(bank[:, 0:B * SC], [(w[:, k, m * 128:(m + 1) * 128], ctxT[:, k, :]) for k in range(KD)])\
                        .then_inc(tr_full.sem, 1)
            pe.wait_ge(d_low, 16 * 4)
            for hf in range(2):
                bank = tr_bank(tl)
                transposes(bank, [u_sb[:, 4 * hf + m, :] for m in range(4)]).then_inc(tr_full.sem, 1)
            bank = tr_bank(tl)
            product(bank[0:R, 0:D], [(fbT, v_sb)]).then_inc(tr_full.sem, 1)
            evacuated(tl)
            for k in range(KD):
                for hf in range(2):
                    bank = tr_bank(tl)
                    product(bank, [(G_sb[:, k * 128:(k + 1) * 128], uT[:, hf * 512:(hf + 1) * 512])])\
                        .then_inc(tr_full.sem, 1)
            for w in (cv, wv):
                for b in range(B):
                    bank = out_bank(tl)
                    product(bank[0:SC, 0:D], [(ctxT[:, k, b * SC:(b + 1) * SC], w[:, k, :]) for k in range(KD)])\
                        .then_inc(out_full.sem, 1)
            tl.close(tr_full, out_full)

            class Steps:

                def __init__(self, tl, b):
                    self.tl, self.b = tl, b

                def copied(self, *step):
                    pe.wait_ge(tr_done.sem, self.tl.after(tr_done, *step))

                def block_copied(self, name, k):
                    pe.wait_ge(tr_done.sem, self.tl.after_block(tr_done, name, k))

                def transposed(self, src, behind):
                    pe.wait_ge(tok_ready.sem, self.tl.after(tok_ready, *behind))
                    bank = tr_bank(self.tl)
                    transposes(bank, [src[:, k * 128:(k + 1) * 128] for k in range(KD)]).then_inc(tr_full.sem, 1)

                def feature_major(self, w, src, m):
                    bank = tr_bank(self.tl)
                    product(bank, [(w[:, k, m * 128:(m + 1) * 128], src[:, k, :]) for k in range(KD)])\
                        .then_inc(tr_full.sem, 1)

                def token_major(self, src, w, t, ks):
                    bank = out_bank(self.tl)
                    c = t % BT * 128
                    product(bank[:, 0:D], [(src[:, k, c:c + 128], w[:, k, :]) for k in ks]).then_inc(out_full.sem, 1)

                def attention(self, keys, nk, project):
                    tl, b = self.tl, self.b

                    def scores(t):
                        self.copied("QP", t // BT)
                        pe.wait_ge(sc_done.sem, tl.value(sc_done))
                        w = CHUNK_HEADS * nk
                        c0 = t % BT * 128
                        for c in range(NCH):
                            k = c * CHUNK_HEADS // 8
                            nc.tensor.matmul(SCR[:, c, 0:w], QT[:, k, c0:c0 + 128],
                                             keys[:, b, c * w:(c + 1) * w], start=True, stop=False)
                            if nk == SC:
                                l, m = onesb[:, :], mask0[:, b, :]
                            else:
                                l, m = identb[:, :], mask1[:, t, :]
                            ins = nc.tensor.matmul(SCR[:, c, 0:w].rearrange("p (h k) -> p h k", k=nk), l,
                                                   m.unsqueeze(1).to_broadcast([128, CHUNK_HEADS, nk]),
                                                   start=False, stop=True)
                        ins.then_inc(sc_full.sem, 1)

                    def prob_transposes(t):
                        pe.wait_ge(p_ready.sem, tl.after(p_ready, "E", t))
                        for g in range(4):
                            bank = tr_bank(tl)
                            transposes(bank, [P[:, t % 2, 4 * g + hh, :] for hh in range(4)]).then_inc(tr_full.sem, 1)

                    def values(t):
                        self.copied("T", t)
                        if t == 0:
                            pe.wait_ge(vsw_ready.sem, tl.after(vsw_ready, "VW"))
                        bank = tr_bank(tl)
                        for h in range(H):
                            g, c = h % 4, h // 4
                            ins = nc.tensor.matmul(bank[32 * g:32 * g + 32, c * 128:(c + 1) * 128], VSW[0:KP, h, :],
                                                   PTS[0:KP, h, :], start=True, stop=True)
                        ins.then_inc(tr_full.sem, 1)

                    def out_transposes(t):
                        self.copied("PV", t)
                        bank = out_bank(tl)
                        transposes(bank, [OSB[:, c * 128:(c + 1) * 128] for c in range(4)]).then_inc(out_full.sem, 1)

                    def ca_transposes(t):
                        pe.wait_ge(out_done.sem, tl.after(out_done, "OT", t))
                        bank = tr_bank(tl)
                        transposes(bank, [CA[:, k * 128:(k + 1) * 128] for k in range(KD)]).then_inc(tr_full.sem, 1)

                    def projected(t):
                        self.copied("CT", t)
                        bank = out_bank(tl)
                        product(bank[:, 0:D], [(CAT[:, k, :], project[:, k, :]) for k in range(KD)])\
                            .then_inc(out_full.sem, 1)

                    return {"S": scores, "T": prob_transposes, "PV": values, "OT": out_transposes,
                            "CT": ca_transposes, "PJ": projected,
                            "LT": lambda t: self.transposed(TOK[:, t % 2, :], ("PN", t))}

            pe.wait_ge(setup_done.sem, 1)
            pe.wait_ge(kb1_ready, 1)
            pe.wait_ge(d_aw, 16 * 5)
            with pe.Fori(0, B) as b:
                tl = Tally("a", b)
                at = Steps(tl, b)

                def queries(k):
                    at.block_copied("LN0", k)
                    for m in range(KD):
                        at.feature_major(cq, xT2[:, k], m)

                def self_qk(k):
                    at.block_copied("LT", k)
                    for w in (sq, sk):
                        for m in range(KD):
                            at.feature_major(w, xTb, m)

                def self_values(t):
                    at.copied("LT", t)
                    at.token_major(xTb, sv, t, range(KD))

                tl.walk(order_a, groups, at.attention(KB0, SC, co) | {
                    "LN0": lambda t: at.transposed(XN[:, t, :], ("LN0", t)),
                    "QP": queries, "QK": self_qk, "SV": self_values})

            def max_scores(tl, j, kt):
                pair = SQ[tl.slot(sq_full, 2)]
                tl.next(sq_full)
                pe.wait_ge(sq_done.sem, tl.back(sq_full, 2))
                for hf in range(2):
                    ins = nc.tensor.matmul(pair[:, hf, :], QX[j][0:QROWS, kt * 128:(kt + 1) * 128],
                                           KX[j][0:QROWS, hf * 512:(hf + 1) * 512], start=True, stop=True)
                ins.then_inc(sq_full.sem, 1)

            def aux_bank(tl):
                pe.wait_ge(aux_done.sem, tl.value(aux_full))
                tl.next(aux_full)
                return AUX

            def maxima_transpose(tl, r, heads):
                pe.wait_ge(m_split.sem, heads)
                bank = aux_bank(tl)
                nc.tensor.transpose(bank.bitcast(BF16)[0:24, 0:128], ms[:, r, :], identb[:, :])\
                    .then_inc(aux_full.sem, 1)

            def head_out_transposes(tl):
                pe.wait_ge(pv_done.sem, tl.value(pv_full))
                bank = aux_bank(tl)
                transposes(bank, [OSB[:, s * 128:(s + 1) * 128] for s in range(2)]).then_inc(aux_full.sem, 1)

            tl = Tally("b0")
            pe.wait_ge(tr_done.sem, tr_done.base["b0"])
            pe.wait_ge(out_done.sem, out_done.base["b0"])
            pe.wait_ge(sc_done.sem, sc_done.base["b0"])
            for j in range(2):
                pe.wait_ge(d_head[j], 16 * 6)
                for kt in range(QT_PER_HEAD):
                    max_scores(tl, j, kt)
            maxima_transpose(tl, 0, 1)
            tl.close(sq_full, aux_full)

            def head(tl, i, j, last, rest):
                n = i * UNROLL + j

                def t_scores(kt):
                    for hf in range(2):
                        bank = tl.slot(st_full, 2)
                        tl.next(st_full)
                        pe.wait_ge(st_done.sem, tl.back(st_full, 2))
                        nc.tensor.matmul(SCR[:, bank, :], KX[j][0:QROWS + 3, kt * 128:(kt + 1) * 128],
                                         QX[j][0:QROWS + 3, hf * 512:(hf + 1) * 512], start=True, stop=True)\
                            .then_inc(st_full.sem, 1)

                def values(kt, ahead):
                    pe.wait_ge(st_done.sem, tl.back(st_full, ahead))
                    if kt == 0:
                        pe.wait_ge(pv_done.sem, tl.value(pv_full))
                        pe.wait_ge(vh_ready.sem, (n + 1))
                    for g in range(4):
                        ins = nc.tensor.matmul(PV[32 * g:32 * g + 32, 0:256], VH[:, j % 2, kt, :],
                                               PTB[:, kt % 2, g * 256:(g + 1) * 256], start=(kt == 0),
                                               stop=(kt == QT_PER_HEAD - 1))
                    if kt == QT_PER_HEAD - 1:
                        ins.then_inc(pv_full.sem, 1)
                        tl.next(pv_full)

                for kt in range(QT_PER_HEAD):
                    if kt == 0:
                        pe.wait_ge(d_m2, (n + 1) * 16)
                    t_scores(kt)
                    if kt > 0:
                        values(kt - 1, 2)
                    elif rest:
                        rest(2)
                    if kt == 2 and not (last and j == UNROLL - 1):
                        maxima_transpose(tl, (j + 1) % 2, n + 2)
                    if kt == 4 and j >= 1:
                        head_out_transposes(tl)
                    if not (last and j >= 2):
                        if kt == 0:
                            pe.wait_ge(d_head[(j + 2) % UNROLL], (i + (1 + (j + 2) // UNROLL)) * (16 * 6))
                            max_scores(tl, (j + 2) % UNROLL, 0)
                        if rest or kt > 1:
                            if kt > 0:
                                max_scores(tl, (j + 2) % UNROLL, kt)
                        elif kt == 0:
                            max_scores(tl, (j + 2) % UNROLL, 1)
                if j < UNROLL - 1:
                    return lambda ahead: values(QT_PER_HEAD - 1, ahead)
                values(QT_PER_HEAD - 1, 0)
                head_out_transposes(tl)

            with pe.Fori(0, NH // UNROLL - 1) as i:
                tl = Tally("b", i)
                rest = None
                for j in range(UNROLL):
                    rest = head(tl, i, j, False, rest)
                tl.close(sq_full, st_full, pv_full, aux_full)
            tl = Tally("blast")
            rest = None
            for j in range(UNROLL):
                rest = head(tl, NH // UNROLL - 1, j, True, rest)
            tl.close(sq_full, st_full, pv_full, aux_full)

            tl = Tally("w")
            pe.wait_ge(sq_done.sem, sq_done.total)
            pe.wait_ge(aux_done.sem, aux_done.total)
            pe.wait_ge(st_done.sem, st_done.total)
            pe.wait_ge(pv_done.sem, pv_done.total)
            pe.wait_ge(tern_ready.sem, tern_ready.total)
            for k in range(KD):
                for hf in range(2):
                    transposes(out_bank(tl), [wfc[:, 4 * hf + c, k * 128:(k + 1) * 128] for c in range(4)])\
                        .then_inc(out_full.sem, 1)
            for m in range(KD):
                for hf in range(2):
                    transposes(tr_bank(tl), [wproj[:, m, (4 * hf + c) * 128:(4 * hf + c + 1) * 128] for c in range(4)])\
                        .then_inc(tr_full.sem, 1)
            tl.close(tr_full, out_full)

            pe.wait_ge(d_cw, 16 * 5)
            pe.wait_ge(d_fifo, 16 * 2)
            with pe.Fori(0, B) as b:
                tl = Tally("c", b)
                at = Steps(tl, b)

                def self_output_transposes(t):
                    pe.wait_ge(d_o[t // BT], b * 16 + 16)
                    bank = tr_bank(tl)
                    transposes(bank, [TOKS[:, t, k * 128:(k + 1) * 128] for k in range(KD)]).then_inc(tr_full.sem, 1)

                def self_projection(t):
                    at.copied("ST", t)
                    at.token_major(xTs, so, t, range(KD))

                def gelu_up(k):
                    at.block_copied("LX", k)
                    for m in range(MF):
                        at.feature_major(fi, xTb, m)

                def gelu_down(t):
                    at.copied("FI", t // BT)
                    at.token_major(hid, fo, t, range(MF))

                def router(k):
                    at.block_copied("L2", k)
                    for hf in range(2):
                        bank = out_bank(tl)
                        for c in range(2):
                            t = 2 * hf + c
                            ins = product(bank[:, c * E:(c + 1) * E],
                                          [(xT2[:, k, f, t * 128:(t + 1) * 128], routerT[:, f, :]) for f in range(KD)])
                        ins.then_inc(out_full.sem, 1)

                def expert_up(k, e):
                    if e == 0:
                        pe.wait_ge(d_moe, 16 * 4)
                        at.block_copied("L2", k)
                    for m in range(2):
                        at.feature_major(w1, xT2[:, k], 2 * e + m)

                def expert_down(k, e, t):
                    pe.wait_ge(a_ready.sem, tl.after(a_ready, "UP", k, e))
                    c = t % BT * 128
                    bank = out_bank(tl)
                    product(bank[:, 0:D], [(HM[:, (e % 2) * 2 + m, c:c + 128], w2[:, 2 * e + m, :]) for m in range(2)])\
                        .then_inc(out_full.sem, 1)

                def queries(k):
                    at.block_copied("L3", k)
                    for m in range(KD):
                        at.feature_major(wq, xTb, m)

                def ternary_up(k):
                    at.block_copied("LT", k)
                    for m in range(MF):
                        at.feature_major(fcT, xTs, m)

                def ternary_down(t):
                    pe.wait_ge(a_ready.sem, tl.after(a_ready, "FC", t // BT))
                    at.token_major(hid, projT, t, range(MF))

                tl.walk(order_c, groups, at.attention(KB1, SC1, wo) | {
                    "ST": self_output_transposes, "SO": self_projection,
                    "LX": lambda t: at.transposed(XN[:, t % BT, :], ("SN", t)),
                    "FI": gelu_up, "FO": gelu_down,
                    "L2": lambda t: at.transposed(TOKF[:, t % 2, :], ("FM", t)),
                    "RT": router, "UP": expert_up, "DN": expert_down, "DL": expert_down,
                    "L3": lambda t: at.transposed(TOKM[:, t % 2, :], ("DM", t)),
                    "QP": queries, "FC": ternary_up, "FP": ternary_down})

        @block.scalar
        def _(act):
            def emptied(tl):
                bank = tl.slot(tr_full, 2)
                act.wait_ge(tr_full.sem, tl.next(tr_full))
                return TR[:, bank, :]

            tl = Tally("setup")
            bank = emptied(tl)
            nc.scalar.activation(ctxT.rearrange("p k (b n) -> p b k n", b=B),
                                 bank[:, 0:B * KD * SC].rearrange("p (b k n) -> p b k n", b=B, k=KD), ACT.Copy)\
                .then_inc(tr_done.sem, 1)
            for dst, bias in ((kT, cols["ck_b"]), (kT1, cols["bk"])):
                for m in range(KD):
                    bank = emptied(tl)
                    if m == 0:
                        act.wait_ge(d_kv, 16 * 8)
                    nc.scalar.activation(dst[:, m, :], bank[:, 0:B * SC], ACT.Identity, bias=bias[:, m:m + 1])\
                        .then_inc(tr_done.sem, 1)
            for hf in range(2):
                bank = emptied(tl)
                nc.scalar.activation(uT[:, hf * 512:(hf + 1) * 512], bank[0:R, :], ACT.Copy).then_inc(tr_done.sem, 1)
            bank = emptied(tl)
            act.wait_ge(d_low, 16 * 4)
            nc.scalar.activation(G_sb, bank[0:R, 0:D], ACT.Identity, scale=gate).then_inc(tr_done.sem, 1)
            for k in range(KD):
                for hf in range(2):
                    bank = emptied(tl)
                    nc.scalar.activation(fcT[:, k, hf * 512:(hf + 1) * 512], bank, ACT.Copy).then_inc(tr_done.sem, 1)

            def copy_transposed(tl, dst, t):
                bank = emptied(tl)
                c = t % BT * 128
                nc.scalar.activation(dst[:, :, c:c + 128],
                                     bank[:, 0:256].rearrange("p (k n) -> p k n", k=KD), ACT.Copy)\
                    .then_inc(tr_done.sem, 1)

            def attention(tl, nk, bias, dst):
                def queries(k):
                    for m in range(KD):
                        bank = emptied(tl)
                        nc.scalar.activation(QT[:, m, :], bank, ACT.Identity, bias=bias[:, m:m + 1])\
                            .then_inc(tr_done.sem, 1)

                def exps(t):
                    act.wait_ge(sc_done.sem, tl.after(sc_done, "S", t))
                    v = P[:, t % 2, :, 0:nk]
                    nc.scalar.activation(v, v, ACT.Exp, scale=DH ** -0.5).then_inc(p_ready.sem, 1)

                def prob_transposes(t):
                    for g in range(4):
                        bank = emptied(tl)
                        nc.scalar.activation(PTS[0:KP, 4 * g:4 * g + 4, :],
                                             bank[0:KP].rearrange("p (h n) -> p h n", h=4), ACT.Copy)\
                            .then_inc(tr_done.sem, 1)

                def values(t):
                    bank = emptied(tl)
                    nc.scalar.activation(OSB[:, :], bank, ACT.Copy).then_inc(tr_done.sem, 1)

                return {"QP": queries, "E": exps, "T": prob_transposes, "PV": values,
                        "CT": lambda t: copy_transposed(tl, CAT, 0), "LT": lambda t: copy_transposed(tl, dst, t)}

            act.wait_ge(d_const, 16 * 7)
            act.wait_ge(kb1_ready, 1)
            with act.Fori(0, B) as b:
                tl = Tally("a", b)

                def self_qk(k):
                    act.wait_ge(d_pieces, b * (BLOCKS * 4 * 16) + (k * 4 * 16 + DC))
                    for e in range(2 * KD):
                        bank = emptied(tl)
                        bias = cols["sq_b" if e < KD else "sk_b"][:, e % KD:e % KD + 1]
                        act.wait_ge(pc_ready.sem, tl.back(pc_ready, 1))
                        tl.next(pc_ready)
                        nc.scalar.activation(PC[:, e, 0, :], bank, ACT.Identity, bias=bias)
                        nc.scalar.activation(RR[:, e % 2, :], bank, ACT.Identity, bias=bias).then_inc(tr_done.sem, 1)

                tl.walk(order_a, groups, attention(tl, SC, cols["cq_b"], xTb) | {
                    "LN0": lambda t: copy_transposed(tl, xT2[:, t // BT], t), "QK": self_qk})

            def head_output(tl):
                act.wait_ge(pv_full.sem, tl.next(pv_full))
                nc.scalar.activation(OSB[:, 0:256], PV[:, 0:256], ACT.Copy).then_inc(pv_done.sem, 1)

            def head(tl, j):
                for kt in range(QT_PER_HEAD):
                    for hf in range(2):
                        bank = tl.slot(st_full, 2)
                        act.wait_ge(st_full.sem, tl.next(st_full))
                        nc.scalar.activation(PTB[:, kt % 2, hf * 512:(hf + 1) * 512], SCR[:, bank, :], ACT.Exp,
                                             scale=DH ** -0.5).then_inc(st_done.sem, 1)
                    if kt == 0 and j > 0:
                        head_output(tl)
                if j == UNROLL - 1:
                    head_output(tl)

            act.wait_ge(d_pieces, DC + 16 * 4 * B * BLOCKS)
            act.wait_ge(d_tern, 32)
            for m in range(MF):
                nc.scalar.activation(XN[:, m, :], wfc[:, m, :], ACT.Abs, accum_out=wscale[:, 0, m:m + 1])
            for m in range(KD):
                ins = nc.scalar.activation(TOKS[:, m * BT:(m + 1) * BT, :],
                                           wproj[:, m, :].rearrange("p (t d) -> p t d", d=D), ACT.Abs,
                                           accum_out=wscale[:, 0, MF + m:MF + m + 1])
            ins.then_inc(sums_ready, 1)
            with act.Fori(0, NH // UNROLL - 1) as i:
                tl = Tally("b", i)
                for j in range(UNROLL):
                    head(tl, j)
            tl = Tally("blast")
            for j in range(UNROLL):
                head(tl, j)

            act.wait_ge(d_late, 16 * 9)
            tl = Tally("w")
            for m in range(KD):
                for hf in range(2):
                    bank = emptied(tl)
                    nc.scalar.activation(projT[:, 4 * hf:4 * hf + 4, m * 128:(m + 1) * 128],
                                         bank.rearrange("p (c n) -> p c n", c=4), ACT.Copy).then_inc(tr_done.sem, 1)

            with act.Fori(0, B) as b:
                tl = Tally("c", b)

                def gelu_up(k):
                    for m in range(MF):
                        bank = emptied(tl)
                        nc.scalar.activation(hid[:, m, :], bank, ACT.Gelu, bias=cols["fi_b"][:, m:m + 1])\
                            .then_inc(tr_done.sem, 1)

                def router(k):
                    act.wait_ge(out_done.sem, tl.after(out_done, "RT", k))
                    nc.scalar.activation(pr.rearrange("p t e -> p (t e)"), lg, ACT.Exp, scale=-1.0)\
                        .then_inc(gate_exp.sem, 1)

                def relus(count):
                    for _ in range(count):
                        bank = emptied(tl)
                        act.wait_ge(a_ready.sem, tl.back(a_ready, 1))
                        nc.scalar.activation(RR[:, tl.slot(a_ready, 2), :], bank, ACT.Relu).then_inc(tr_done.sem, 1)
                        tl.next(a_ready)

                tl.walk(order_c, groups, attention(tl, SC1, cols["bq"], xTs) | {
                    "ST": lambda t: copy_transposed(tl, xTs, t), "LX": lambda t: copy_transposed(tl, xTb, t),
                    "FI": gelu_up, "L2": lambda t: copy_transposed(tl, xT2[:, t // BT], t), "RT": router,
                    "UP": lambda k, e: relus(2), "L3": lambda t: copy_transposed(tl, xTb, t),
                    "FC": lambda k: relus(MF)})

        @block.vector
        def _(dve):
            steps = [0]

            def link(ins):
                steps[0] += 1
                ins.then_inc(s_dve, 1)
                dve.wait_ge(s_dve, steps[0])

            class Chain:
                def __init__(self, i, per):
                    self.i, self.per, self.n, self.at = i, per, 0, steps[0]

                def __call__(self, ins):
                    self.n += 1
                    ins.then_inc(s_dve, 1)
                    dve.wait_ge(s_dve, self.i * self.per + (self.at + self.n))
                    carry_wait(dve)

                def close(self, trips):
                    assert self.n == self.per, self.n
                    steps[0] += self.per * trips

            tl = Tally("setup")
            dve.wait_ge(c_ready.sem, c_ready.total)
            dve.wait_ge(d_mask, 32)
            m0 = mask0[0:3].rearrange("p b k -> p (b k)")
            link(nc.vector.tensor_scalar(masks, masks, 4.0, -3.0e38, ALU.mult, ALU.max))
            for c in range(3):
                link(nc.vector.tensor_copy(mpiece, masks))
                if c == 0:
                    link(nc.vector.tensor_scalar(m0, mpiece, identf[0:3, 0:1], None, ALU.mult))
                else:
                    link(nc.vector.scalar_tensor_tensor(m0, mpiece, identf[0:3, c:c + 1], m0, ALU.mult, ALU.add))
                link(nc.vector.tensor_tensor(masks, masks, mpiece, ALU.subtract))
            nc.vector.tensor_scalar(mask1[:, :, 0:SC], maski, 0, 4.0 * -1.0e9, ALU.is_equal, ALU.mult)\
                .then_inc(mask1_ready.sem, 1)
            dve.wait_ge(tr_done.sem, tl.next(tr_done, 5))
            kb0 = KB0.rearrange("p b (k h n) -> p b k h n", k=KD, n=SC)
            for hh in range(8):
                bm = blockmask[:, hh:hh + 1]
                for b in range(B):
                    ins = nc.vector.tensor_scalar(kb0[:, b, :, hh, :], kT[:, :, b * SC:(b + 1) * SC], bm, None,
                                                  ALU.mult)
            link(ins)
            for vs, bias in ((VS0, vb0), (VS1, vb1)):
                for b in range(B):
                    bank = tl.slot(out_full, 2)
                    dve.wait_ge(out_full.sem, tl.next(out_full))
                    if b == 0:
                        dve.wait_ge(d_kv, 16 * 8)
                    nc.vector.tensor_tensor(vs[0:SC, b, :, 0:DH],
                                            OUT[0:SC, bank, 0:D].rearrange("p (h d) -> p h d", d=DH),
                                            bias[0:SC].rearrange("p (h d) -> p h d", d=DH), ALU.add)\
                        .then_inc(out_done.sem, 1)
            tl.close(out_full)
            dve.wait_ge(tr_done.sem, tr_done.base["a"])
            nc.vector.memset(P[:, :, :, SC:KP], 0.0)
            nc.vector.memset(VX[:, :, :, DH:VW], 1.0)
            nc.vector.memset(VSW[:, :, VW:32], 0.0)
            dve.wait_ge(d_x, 16)
            dve.wait_ge(d_const, 16 * 7)
            nc.vector.memset(VH[:, :, :, VW:32], 0.0).then_inc(setup_done.sem, 1)
            dve.wait_ge(setup_done.sem, 1)

            def moments(tl, chain, src):
                r = tl.slot(ln_stats, LR)
                dve.wait_ge(ln_stats.sem, tl.value(ln_stats))
                tl.next(ln_stats)
                carry_wait(dve)
                chain(nc.vector.bn_stats(stats, src))
                nc.vector.bn_aggr(mv[:, r, :], stats).then_inc(ln_stats.sem, 1)

            def normalised(tl, chain, behind, src, dst, affine=None):
                r = tl.slot_of(ln_stats, LR, *behind)
                dve.wait_ge(ln_rstd.sem, tl.after(ln_rstd, *behind))
                ins = nc.vector.tensor_scalar(dst, src, mv[:, r, 0:1], rstd[:, r:r + 1], ALU.subtract, ALU.mult)
                if affine:
                    chain(ins)
                    chain(nc.vector.tensor_tensor(dst, dst, rows[affine + "_g"], ALU.mult))
                    ins = nc.vector.tensor_tensor(dst, dst, rows[affine + "_be"], ALU.add)
                return ins

            def filled(tl):
                bank = tl.slot(out_full, 2)
                dve.wait_ge(out_full.sem, tl.next(out_full))
                return OUT[:, bank, :]

            def signal_out(tl, ins):
                ins.then_inc(out_done.sem, 1)
                dve.wait_ge(out_done.sem, tl.next(out_done))

            def links(order, **per_step):
                return sum(per_step.get(s[0], 0) for s in order)

            def left(tl, *step):
                dve.wait_ge(tr_done.sem, tl.after(tr_done, *step))

            def with_residual(tl, chain, t, dst, residual, behind):
                bank = filled(tl)
                dve.wait_ge(resid_ready.sem, tl.after(resid_ready, behind, t))
                signal_out(tl, nc.vector.tensor_tensor(dst, bank[:, 0:D], residual, ALU.add))
                moments(tl, chain, dst)

            def attention(tl, chain, nk):
                def scores(t):
                    dve.wait_ge(sc_full.sem, tl.next(sc_full))
                    v = SCR[:, :, 0:CHUNK_HEADS * nk].rearrange("p c (h k) -> p c h k", k=nk)
                    chain(nc.vector.tensor_reduce(mx, v, AX, ALU.max))
                    nc.vector.tensor_tensor(P[:, t % 2, :, 0:nk].rearrange("p (c h) k -> p c h k", c=NCH), v,
                                            mx.rearrange("p (c h) -> p c h", c=NCH).unsqueeze(3)
                                            .to_broadcast([128, NCH, CHUNK_HEADS, nk]), ALU.subtract)\
                        .then_inc(sc_done.sem, 1)

                def normalise(t):
                    bank = filled(tl).rearrange("p (h d) -> p h d", d=32)
                    chain(nc.vector.reciprocal(rsum, bank[:, :, DH]))
                    signal_out(tl, nc.vector.tensor_tensor(CA[:, :].rearrange("p (h d) -> p h d", d=DH),
                                                           bank[:, :, 0:DH],
                                                           rsum.unsqueeze(2).to_broadcast([128, H, DH]), ALU.mult))

                return {"S": scores, "OT": normalise}

            def pass_start(tl, small_values):
                dve.wait_ge(tr_done.sem, tl.value(tr_done))
                nc.vector.tensor_copy(VSW[0:KP, :, 0:VW], small_values).then_inc(vsw_ready.sem, 1)

            with dve.Fori(0, B) as b:
                tl = Tally("a", b)
                chain = Chain(b, links(order_a, LS=1, S=1, OT=1, PJ=1, PN=2, QK=2 * 2 * KD))

                def input_norm(t):
                    normalised(tl, chain, ("LS", t), X[:, b * TB + t, :], XN[:, t, :]).then_inc(tok_ready.sem, 1)

                def projected_norm(t):
                    dve.wait_ge(d_x1[t % 2], b * (TB // 2 * 16) + (t // 2 * 16 + DC))
                    if t >= 2:
                        left(tl, "LT", t - 2)
                    normalised(tl, chain, ("PJ", t), HB[:, t % 2, :], TOK[:, t % 2, :], affine="co")\
                        .then_inc(tok_ready.sem, 1)

                def pieces(k):
                    rest = HM[:, 2, :]
                    for e in range(2 * KD):
                        dve.wait_ge(tr_done.sem, tl.next(tr_done))
                        chain(nc.vector.tensor_tensor(rest, RR[:, e % 2, :], PC[:, e, 0, :], ALU.subtract))
                        chain(nc.vector.tensor_copy(PC[:, e, 1, :], rest))
                        nc.vector.tensor_tensor(PC[:, e, 2, :], rest, PC[:, e, 1, :], ALU.subtract)\
                            .then_inc(pc_ready.sem, 1)
                        dve.wait_ge(pc_ready.sem, tl.next(pc_ready))

                def self_values(t):
                    bank = filled(tl)
                    signal_out(tl, nc.vector.tensor_tensor(
                        VX[:, bass.ds(b * H, H), t, 0:DH], bank[:, 0:D].rearrange("p (h d) -> p h d", d=DH),
                        rows["sv_b"].rearrange("p (h d) -> p h d", d=DH), ALU.add))

                tl.walk(order_a, groups, attention(tl, chain, SC) | {
                    "VW": lambda: pass_start(tl, VS0[0:KP, b, :, :]), "LS": lambda t: moments(tl, chain, X[:, b * TB + t, :]), "LN0": input_norm,
                    "PJ": lambda t: with_residual(tl, chain, t, HB[:, t % 2, :], XN[:, t, :], "RA"),
                    "PN": projected_norm, "QK": pieces, "SV": self_values})
            chain.close(B)

            dve.wait_ge(sc_full.sem, sc_full.base["b0"])
            for j in range(UNROLL):
                ins = nc.vector.memset(KX[j][QROWS:QROWS + 3, :], 1.0)
            link(ins)

            def max_scores(tl, r, kt):
                pair = SQ[tl.slot(sq_full, 2)]
                dve.wait_ge(sq_full.sem, tl.next(sq_full))
                nc.vector.tensor_reduce(nm[:, r, kt:kt + 1], pair.rearrange("p h n -> p (h n)"), AX, ALU.max, negate=True)\
                    .then_inc(sq_done.sem, 1)
                tl.next(sq_done)

            def aux_filled(tl):
                dve.wait_ge(aux_full.sem, tl.next(aux_full))
                return AUX

            def maxima_rows(tl, stored):
                bank = aux_filled(tl)
                dve.wait_ge(d_m1, stored)
                nc.vector.tensor_copy(MT[:, :], bank.bitcast(BF16)[0:24, 0:128]).then_inc(aux_done.sem, 1)

            def head_out(tl, chain, n, r):
                bank = aux_filled(tl)[:, 0:256].rearrange("p (s g d) -> p g s d", s=2, g=4)
                rs = rsum[:, 0:8].rearrange("p (g s) -> p g s", s=2)
                chain(nc.vector.reciprocal(rs, bank[:, :, :, DH]))
                dve.wait_ge(d_oh[r], (n // 2) * 16 + DC)
                nc.vector.tensor_tensor(OH[:, r, :, :].rearrange("p (g s) d -> p g s d", s=2),
                                        bank[:, :, :, 0:DH],
                                        rs.unsqueeze(3).to_broadcast([128, 4, 2, DH]), ALU.mult)\
                    .then_inc(aux_done.sem, 1)
                dve.wait_ge(aux_done.sem, tl.value(aux_full))

            tl = Tally("b0")
            for j in range(2):
                for kt in range(QT_PER_HEAD):
                    max_scores(tl, j, kt)
            maxima_rows(tl, 0)
            tl.close(sq_full, aux_full)
            dve.wait_ge(sums_ready, 1)
            sc = wscale[:, 0, :]
            link(nc.vector.tensor_scalar(sc[:, 0:MF], sc[:, 0:MF], 1.0 / D, 1e-5, ALU.mult, ALU.max))
            link(nc.vector.tensor_scalar(sc[:, MF:], sc[:, MF:], 1.0 / F, 1e-5, ALU.mult, ALU.max))
            nc.vector.tensor_scalar(wscale[:, 1, :], sc, 0.5, None, ALU.mult)
            nc.vector.tensor_scalar(wscale[:, 2, :], sc, -0.5, None, ALU.mult).then_inc(wscale_ready, 1)
            dve.wait_ge(wscale_ready, 1)

            def signs(tl, chain, i):
                def below(w, m):
                    chain(nc.vector.tensor_scalar(TN[:, 0:w.shape[-1]], w, wscale[:, 2, m], None, ALU.is_lt))

                def sign(w, m):
                    nc.vector.scalar_tensor_tensor(w, w, wscale[:, 1, m], TN[:, 0:w.shape[-1]], ALU.is_gt, ALU.subtract)\
                        .then_inc(signs_ready.sem, 1)
                    dve.wait_ge(signs_ready.sem, tl.next(signs_ready))

                parts = [(wfc[:, i, :], bass.ds(i, 1))]
                parts += [(wproj[:, m, bass.ds(i * 128, 128)], slice(MF + m, MF + m + 1)) for m in range(KD)]
                return {at: [lambda f=f, p=p: f(*p)] for at, f, p in zip(
                    ((0, 1), (0, 7), (2, 1), (2, 7), (3, 1), (3, 7)), (below, sign) * 3, [p for p in parts for _ in range(2)])}

            def head(tl, chain, i, j, last, share):
                n = i * UNROLL + j
                if not (last and j >= 2):
                    dve.wait_ge(m_split.sem, (n + 1))
                for kt in range(QT_PER_HEAD):
                    if kt == 3 and not (last and j == UNROLL - 1):
                        maxima_rows(tl, (n + 1) * 16)
                    if kt == 5 and j >= 1:
                        head_out(tl, chain, n - 1, (j - 1) % 2)
                    if not (last and j >= 2):
                        max_scores(tl, j % 2, kt)
                    for op in share.get((j, kt), ()):
                        op()
                if j == UNROLL - 1:
                    head_out(tl, chain, n, j % 2)

            with dve.Fori(0, NH // UNROLL - 1) as i:
                tl = Tally("b", i)
                chain = Chain(i, UNROLL + 3)
                share = signs(tl, chain, i)
                for j in range(UNROLL):
                    head(tl, chain, i, j, False, share)
                tl.close(sq_full, sq_done, aux_full)
            chain.close(NH // UNROLL - 1)
            tl = Tally("blast")
            chain = Chain(0, UNROLL + 3)
            share = signs(tl, chain, NH // UNROLL - 1)
            for j in range(UNROLL):
                head(tl, chain, NH // UNROLL - 1, j, True, share)
            tl.close(sq_full, sq_done, aux_full)
            chain.close(1)

            dve.wait_ge(d_late, 16 * 9)
            tl = Tally("w")
            for k in range(KD):
                for hf in range(2):
                    bank = filled(tl)
                    dst = fcT[:, k, hf * 512:(hf + 1) * 512]
                    nc.vector.tensor_tensor(dst, dst, bank, ALU.add).then_inc(out_done.sem, 1)

            with dve.Fori(0, B) as b:
                tl = Tally("c", b)
                chain = Chain(b, links(order_c, SO=1, SN=2, FO=1, FN=5, RT=3 + 2 * 6 + 5, DL=1, S=1, OT=1, PJ=1))

                def self_norm(t):
                    xn = XN[:, t % BT, :]
                    normalised(tl, chain, ("SO", t), xn, xn, affine="so").then_inc(tok_ready.sem, 1)

                def gelu_norm(t):
                    xt, h = X[:, b * TB + t, :], HB[:, t % 2, :]
                    chain(normalised(tl, chain, ("FO", t), h, h, affine="fo"))
                    chain(nc.vector.tensor_tensor(xt, xt, h, ALU.add))
                    moments(tl, chain, xt)

                def experts_input(t):
                    if t >= 2:
                        left(tl, "L2", t - 2)
                    normalised(tl, chain, ("FN", t), X[:, b * TB + t, :], TOKF[:, t % 2, :]).then_inc(tok_ready.sem, 1)

                def router(k):
                    for hf in range(2):
                        bank = filled(tl)
                        signal_out(tl, nc.vector.tensor_copy(lg[:, hf * 2 * E:(hf + 1) * 2 * E], bank[:, 0:2 * E]))
                    dve.wait_ge(gate_exp.sem, tl.next(gate_exp))
                    chain(nc.vector.tensor_scalar(pr, pr, 1.0, None, ALU.add))
                    chain(nc.vector.reciprocal(pr, pr))
                    rk = rank.unsqueeze(1).to_broadcast([128, BT, E])
                    chain(nc.vector.tensor_copy(pw, pr))
                    for c in range(2):
                        v, key = top[:, 3 * c, :], top[:, 3 * c + 1, :]
                        vb = v.unsqueeze(2).to_broadcast([128, BT, E])
                        chain(nc.vector.tensor_reduce(v, pw, AX, ALU.max))
                        chain(nc.vector.tensor_tensor(eq, pw, vb, ALU.is_equal))
                        chain(nc.vector.tensor_tensor(eq, eq, rk, ALU.mult))
                        chain(nc.vector.tensor_reduce(key, eq, AX, ALU.max))
                        h = hot if c == 0 else eq
                        chain(nc.vector.tensor_tensor(h, eq, key.unsqueeze(2).to_broadcast([128, BT, E]), ALU.is_equal))
                        if c == 0:
                            chain(nc.vector.scalar_tensor_tensor(pw, h, -4.0, pw, ALU.mult, ALU.add))
                        else:
                            chain(nc.vector.tensor_tensor(hot, hot, h, ALU.add))
                    chain(nc.vector.tensor_tensor(top[:, 2, :], top[:, 0, :], top[:, 3, :], ALU.add))
                    chain(nc.vector.tensor_scalar(top[:, 2, :], top[:, 2, :], 1e-20, None, ALU.add))
                    chain(nc.vector.reciprocal(top[:, 5, :], top[:, 2, :]))
                    chain(nc.vector.tensor_tensor(hot, hot, pr, ALU.mult))
                    chain(nc.vector.tensor_tensor(cw[:, k * BT:(k + 1) * BT, :], hot,
                                                  top[:, 5, :].unsqueeze(2).to_broadcast([128, BT, E]), ALU.mult))

                def squares(places):
                    for dst in places:
                        dve.wait_ge(tr_done.sem, tl.next(tr_done))
                        r = RR[:, tl.slot(a_ready, 2), :]
                        nc.vector.tensor_tensor(dst, r, r, ALU.mult).then_inc(a_ready.sem, 1)
                        tl.next(a_ready)

                def expert_up(k, e):
                    squares([HM[:, (e % 2) * 2 + m, :] for m in range(2)])

                def expert_down(k, e, t):
                    bank = filled(tl)
                    xt = X[:, b * TB + t, :]
                    signal_out(tl, nc.vector.scalar_tensor_tensor(xt, bank[:, 0:D], cw[:, t, e:e + 1], xt,
                                                                  ALU.mult, ALU.add))

                def last_expert_down(k, e, t):
                    expert_down(k, e, t)
                    moments(tl, chain, X[:, b * TB + t, :])

                def experts_norm(t):
                    if t >= 2:
                        left(tl, "L3", t - 2)
                    normalised(tl, chain, ("DL", t // BT, E - 1, t), X[:, b * TB + t, :], TOKM[:, t % 2, :])\
                        .then_inc(tok_ready.sem, 1)

                def projected(t):
                    bank = filled(tl)
                    xt = X[:, b * TB + t, :]
                    dve.wait_ge(resid_ready.sem, tl.after(resid_ready, "RX", t))
                    signal_out(tl, nc.vector.tensor_tensor(xt, bank[:, 0:D], xt, ALU.add))
                    moments(tl, chain, xt)

                def projected_norm(t):
                    if t >= 2:
                        left(tl, "LT", t - 2)
                    normalised(tl, chain, ("PJ", t), X[:, b * TB + t, :], TOK[:, t % 2, :]).then_inc(tok_ready.sem, 1)

                def output(t):
                    bank = filled(tl)
                    dve.wait_ge(d_out[t % 2], b * (TB // 2 * 16) + (t // 2 * 16 + DC))
                    nc.vector.tensor_tensor(OB[:, t % 2, :], bank[:, 0:D], X[:, b * TB + t, :], ALU.add)\
                        .then_inc(out_done.sem, 1)

                tl.walk(order_c, groups, attention(tl, chain, SC1) | {
                    "VW": lambda: pass_start(tl, VS1[0:KP, b, :, :]), "SN": self_norm, "FN": gelu_norm,
                    "SO": lambda t: with_residual(tl, chain, t, XN[:, t % BT, :], RB[:, t % BT, :], "RS"),
                    "FO": lambda t: with_residual(tl, chain, t, HB[:, t % 2, :], XN[:, t % BT, :], "RF"),
                    "FM": experts_input, "RT": router, "UP": expert_up, "DN": expert_down,
                    "DL": last_expert_down, "DM": experts_norm, "PJ": projected, "PN": projected_norm,
                    "FC": lambda k: squares([hid[:, m, :] for m in range(MF)]), "FP": output})
            chain.close(B)

        @block.gpsimd
        def _(pool):
            steps = [0]

            def link(ins):
                steps[0] += 1
                ins.then_inc(s_pool, 1)
                pool.wait_ge(s_pool, steps[0])

            for s in (sc_full, sc_done, ln_stats, aux_full, aux_done, pc_ready, a_ready, st_full, st_done, pv_full, pv_done):
                pool.sem_inc(s.sem, s.credit)
            for s in (d_pieces, *d_x1, *d_out, *d_oh):
                pool.sem_inc(s, DC)
            nc.gpsimd.memset(identf[:, :], 0.0)
            nc.gpsimd.memset(identb[:, :], 0.0)
            nc.gpsimd.memset(blockmask[:, :], 1.0)
            nc.gpsimd.memset(minus_half, -0.5)
            nc.gpsimd.memset(onesb[:, :], 1.0)
            nc.gpsimd.memset(mask0[:, :, :], 0.0)
            nc.gpsimd.memset(mask1[:, :, :], 0.0)
            nc.gpsimd.memset(VS0[:, :, :, :], 0.0)
            link(nc.gpsimd.memset(VS1[:, :, :, :], 0.0))
            for m in (identf, identb):
                nc.gpsimd.affine_select(out=m[:, :], in_=m[:, :], compare_op=ALU.not_equal, fill=1.0, base=0,
                                        pattern=[[-1, 128]], channel_multiplier=1).then_inc(c_ready.sem, 1)
            for vs in (VS0, VS1):
                nc.gpsimd.memset(vs[:, :, :, DH:VW], 1.0).then_inc(c_ready.sem, 1)
            link(nc.gpsimd.affine_select(out=blockmask[:, :], in_=blockmask[:, :], compare_op=ALU.is_ge, fill=0.0,
                                         base=0, pattern=[[-DH, 128 // DH]], channel_multiplier=1))
            nc.gpsimd.affine_select(out=blockmask[:, :], in_=blockmask[:, :], compare_op=ALU.is_ge, fill=0.0,
                                    base=DH - 1, pattern=[[DH, 128 // DH]], channel_multiplier=-1)\
                .then_inc(c_ready.sem, 1)
            for e in range(E):
                ins = nc.gpsimd.memset(rank[:, e:e + 1], float(E - e))
            ins.then_inc(c_ready.sem, 1)

            class Chain:
                def __init__(self, i, per):
                    self.i, self.per, self.n, self.at = i, per, 0, steps[0]

                def __call__(self, ins):
                    self.n += 1
                    ins.then_inc(s_pool, 1)
                    pool.wait_ge(s_pool, self.i * self.per + (self.at + self.n))
                    carry_wait(pool)

                def close(self, trips):
                    assert self.n == self.per, self.n
                    steps[0] += self.per * trips

            def root(tl, chain):
                r = tl.slot(ln_stats, LR)
                pool.wait_ge(ln_stats.sem, tl.next(ln_stats))
                carry_wait(pool)
                chain(nc.gpsimd.tensor_scalar(ve[:, r:r + 1], mv[:, r, 1:2], EPS, None, ALU.add))
                nc.gpsimd.tensor_tensor(rstd[:, r:r + 1], ve[:, r:r + 1], minus_half, ALU.pow)\
                    .then_inc(ln_rstd.sem, 1)

            def roots(tl, chain):
                one = lambda *_: root(tl, chain)
                return {"LS": one, "PJ": one, "SO": one, "FO": one, "FN": one, "DL": one}

            def add_bias(tile, name):
                nc.gpsimd.tensor_tensor(tile, tile, rows[name], ALU.add).then_inc(resid_ready.sem, 1)

            pool.wait_ge(tr_done.sem, 5)
            pool.wait_ge(d_prefix, 16 * (H + B))
            kb1 = KB1[:, :, :].rearrange("p b (k h n) -> p b k h n", k=KD, n=SC1)
            for hh in range(8):
                bm = blockmask[:, hh:hh + 1]
                for b in range(B):
                    nc.gpsimd.tensor_scalar(kb1[:, b, :, hh, 0:SC], kT1[:, :, b * SC:(b + 1) * SC], bm, None, ALU.mult)
                    ins = nc.gpsimd.tensor_scalar(kb1[:, b, :, hh, SC:SC1], pkT, bm, None, ALU.mult)
            ins.then_inc(kb1_ready, 1)

            pool.wait_ge(setup_done.sem, 1)
            with pool.Fori(0, B) as b:
                tl = Tally("a", b)
                chain = Chain(b, ln_stats.per["a"])

                def bias_a(t):
                    pool.wait_ge(tr_done.sem, tl.after(tr_done, "LN0", t))
                    add_bias(XN[:, t, :], "co_b")

                tl.walk(order_a, groups, roots(tl, chain) | {"RA": bias_a})
            chain.close(B)

            def head_values(n, j):
                carry_wait(pool)
                nc.gpsimd.tensor_copy(VH[:, j % 2, :, 0:VW], VX[:, n, :, :]).then_inc(vh_ready.sem, 1)

            def split(tl, chain, r):
                pool.wait_ge(sq_done.sem, tl.next(sq_done, QT_PER_HEAD))
                carry_wait(pool)
                v = nm[:, r, :]
                chain(nc.gpsimd.tensor_copy(ms[:, r, 0:8], v))
                chain(nc.gpsimd.tensor_tensor(nres, v, ms[:, r, 0:8], ALU.subtract))
                chain(nc.gpsimd.tensor_copy(ms[:, r, 8:16], nres))
                nc.gpsimd.tensor_tensor(ms[:, r, 16:24], nres, ms[:, r, 8:16], ALU.subtract).then_inc(m_split.sem, 1)
                pool.wait_ge(m_split.sem, tl.next(m_split))

            pool.wait_ge(out_done.sem, out_done.base["b0"])
            tl = Tally("b0")
            chain = Chain(0, 6)
            for j in range(2):
                head_values(j, j)
            for j in range(2):
                split(tl, chain, j)
            chain.close(1)

            def ternary(tl, i, part):
                pool.wait_ge(signs_ready.sem, tl.next(signs_ready))
                if part == 0:
                    w, scale = wfc[:, i, :], wscale[:, 0, bass.ds(i, 1)].to_broadcast([128, D])
                else:
                    m = part - 1
                    w, scale = wproj[:, m, bass.ds(i * 128, 128)], wscale[:, 0, MF + m:MF + m + 1].to_broadcast([128, 128])
                nc.gpsimd.tensor_tensor(w, w, scale, ALU.mult).then_inc(tern_ready.sem, 1)

            def head(tl, chain, i, j, last):
                n = i * UNROLL + j
                if not (last and j >= 2):
                    split(tl, chain, j % 2)
                    pool.wait_ge(pv_full.sem, tl.next(pv_full))
                    head_values(n + 2, j)
                if j != 1:
                    ternary(tl, i, (0, None, 1, 2)[j])

            pool.wait_ge(wscale_ready, 1)
            with pool.Fori(0, NH // UNROLL - 1) as i:
                tl = Tally("b", i)
                chain = Chain(i, 3 * UNROLL)
                for j in range(UNROLL):
                    head(tl, chain, i, j, False)
            chain.close(NH // UNROLL - 1)
            tl = Tally("blast")
            chain = Chain(0, 3 * (UNROLL - 2))
            for j in range(UNROLL):
                head(tl, chain, NH // UNROLL - 1, j, True)
            chain.close(1)

            pool.wait_ge(sq_done.sem, sq_done.total)
            pool.wait_ge(d_late, 16 * 9)
            with pool.Fori(0, B) as b:
                tl = Tally("c", b)
                chain = Chain(b, ln_stats.per["c"])

                def bias_so(t):
                    pool.wait_ge(d_rb, b * (BLOCKS * 16) + (t // BT + 1) * 16)
                    add_bias(RB[:, t % BT, :], "so_b")

                def bias_fo(t):
                    pool.wait_ge(tr_done.sem, tl.after(tr_done, "LX", t))
                    add_bias(XN[:, t % BT, :], "fo_b")

                def bias_x(t):
                    pool.wait_ge(tok_ready.sem, tl.after(tok_ready, "DM", t))
                    add_bias(X[:, b * TB + t, :], "bo")

                tl.walk(order_c, groups, roots(tl, chain) | {"RS": bias_so, "RF": bias_fo, "RX": bias_x})
            chain.close(B)


def kernel(**inputs):
    import concourse.bacc as bacc
    from concourse.bass_utils import run_bass_kernel_spmd

    nc = bacc.Bacc("TRN2", target_bir_lowering=False, num_devices=1)
    arrays, aps = {}, {}
    for name, value in inputs.items():
        a = np.ascontiguousarray(value)
        if a.ndim == 0:
            a = a.reshape(1)
        arrays[f"in_{name}"] = a
        aps[name] = nc.dram_tensor(f"in_{name}", a.shape, mybir.dt.from_np(a.dtype), kind="ExternalInput").ap()
    out = nc.dram_tensor("out", (B, S, D), F32, kind="ExternalOutput").ap()
    build(nc, aps, out)
    result = run_bass_kernel_spmd(nc, [arrays], core_ids=[0])
    return result.results[0]["out"]
```
